# Optimizing a Trainium2 kernel written in Bass

```python
import numpy as np
import jax
import jax.numpy as jnp

def _softmax(x, axis=-1):
    return jax.nn.softmax(x, axis=axis)

def _gelu(x):
    return jax.nn.gelu(x, approximate=True)

def _silu(x):
    return jax.nn.silu(x)

def _sigmoid(x):
    return jax.nn.sigmoid(x)

def _layernorm(x, axis=-1, eps=1e-05):
    m = jnp.mean(x, axis=axis, keepdims=True)
    v = jnp.var(x, axis=axis, keepdims=True)
    return (x - m) / jnp.sqrt(v + eps)

def _scatter_add(tgt, idx, src, axis=0):
    return tgt.at[idx].add(src)

def _segment_sum(src, seg, n):
    return jax.ops.segment_sum(src, seg, n)
kernel_name = 'mk_perceiver_d4_seqx_r4_9ec9ea'

def setup_inputs(seed: int=0):
    np.random.seed(seed)
    _w = jnp.asarray

    def _rec_inputs():
        import jax
        import jax.numpy as jnp
        _rk = jax.random.key(seed)
        x = -0.0002928 + 1 * jax.random.normal(jax.random.fold_in(_rk, 1), (16, 64, 256), jnp.float32)
        _lenS = 64 - jax.random.randint(jax.random.fold_in(_rk, 7), (16,), 0, max(1, 64 // 4) + 1, jnp.int32)
        _lenS2 = 1601 - jax.random.randint(jax.random.fold_in(_rk, 8), (16,), 0, max(1, 1601 // 4) + 1, jnp.int32)
        _ctx_1024P = jax.random.normal(jax.random.fold_in(_rk, 11), (16, 16, 256), jnp.float32)
        _ctx_1024c = jax.random.dirichlet(jax.random.fold_in(_rk, 511), 0.3 * jnp.ones((16,), jnp.float32), (16, 1601))
        _ctx_1024t = jnp.einsum('bsk,bkd->bsd', _ctx_1024c, _ctx_1024P)
        _ctx_1024t = _ctx_1024t * jax.lax.rsqrt(jnp.mean(jnp.square(_ctx_1024t)) + 1e-12) * 0.953939
        ctx_1024 = -1.39393e-06 + 0.999914 * (_ctx_1024t + 0.3 * jax.random.normal(jax.random.fold_in(_rk, 611), (16, 1601, 256), jnp.float32))
        _validS = jnp.arange(64)[None, :] < _lenS[:, None]
        _validS2 = jnp.arange(1601)[None, :] < _lenS2[:, None]
        _causal = jnp.tril(jnp.ones((64, 64), dtype=bool))
        mask_Bx1xSxS2_ff0 = jnp.where(jnp.ones((16, 1, 64, 1601), dtype=bool), 0.0, -1000000000.0).astype(jnp.float32)
        mask_Bx1x1xS2_if1 = jnp.where(jnp.ones((16, 1, 1, 1601), dtype=bool), 1, 0).astype(jnp.int32)
        return (x, ctx_1024, mask_Bx1xSxS2_ff0, mask_Bx1x1xS2_if1)
    x, ctx_1024, mask_Bx1xSxS2_ff0, mask_Bx1x1xS2_if1 = _rec_inputs()

    def _L0_xattn_setup():
        import jax, jax.numpy as jnp
        import numpy as np
        B, S, D, H = (2, 512, 256, 16)
        HD = D // H

        def _split_heads(x):
            b, s, _ = x.shape
            return x.reshape(b, s, H, HD).transpose(0, 2, 1, 3)
        key = jax.random.key(seed)
        ks = jax.random.split(key, 12)
        init = lambda k, shape: jax.random.normal(k, shape, dtype=jnp.float32) * (1.0 / np.sqrt(shape[0]))
        return {'q': jax.random.normal(ks[0], (B, S, D), dtype=jnp.float32), 'k': jax.random.normal(ks[1], (B, S, D), dtype=jnp.float32), 'v': jax.random.normal(ks[2], (B, S, D), dtype=jnp.float32), 'mask': jnp.zeros((B, 1, S, S), dtype=jnp.float32), 'Wq': init(ks[3], (D, D)), 'bq': jnp.zeros((D,), jnp.float32), 'Wk': init(ks[4], (D, D)), 'bk': jnp.zeros((D,), jnp.float32), 'Wv': init(ks[5], (D, D)), 'bv': jnp.zeros((D,), jnp.float32), 'Wo': init(ks[6], (D, D)), 'bo': jnp.zeros((D,), jnp.float32)}
    _L0_xattn_all = _L0_xattn_setup()
    _L0_xattn_in = {k: v for k, v in _L0_xattn_all.items() if k in ('Wq', 'bq', 'Wk', 'bk', 'Wv', 'bv', 'Wo', 'bo')}
    del _L0_xattn_all

    def _L0_attn_setup():
        import jax, jax.numpy as jnp
        import numpy as np
        NUM_HEADS = 16
        N_EMBD = 256

        def alibi_bias(num_heads: int, seq_len: int) -> jnp.ndarray:
            pos = jnp.arange(seq_len, dtype=jnp.float32)
            dgrid = pos[None, :] - pos[:, None]
            slopes = 2.0 ** (-8.0 / num_heads * (jnp.arange(num_heads, dtype=jnp.float32) + 1.0))
            bias = slopes[:, None, None] * dgrid[None, :, :]
            return jnp.where(dgrid[None, :, :] > 0, -jnp.inf, bias)
        key = jax.random.key(seed)
        k1, k2, k3 = jax.random.split(key, 3)
        B, L, E = (2, 512, N_EMBD)
        x = jax.random.normal(k1, (B, L, E), dtype=jnp.float32)
        w_in = jax.random.normal(k2, (3 * E, E), dtype=jnp.float32) * 0.02
        w_out = jax.random.normal(k3, (E, E), dtype=jnp.float32) * 0.02
        return {'x': x, 'w_in': w_in, 'w_out': w_out}
    _L0_attn_all = _L0_attn_setup()
    _L0_attn_in = {k: v for k, v in _L0_attn_all.items() if k in ('w_in', 'w_out')}
    del _L0_attn_all

    def _L0_ffn_setup():
        import jax, jax.numpy as jnp
        import numpy as np
        BLOCK = 32
        W_BITS = 4
        ACT_BITS = 16

        def act_qdq(x):
            qmax = 2.0 ** (ACT_BITS - 1) - 1.0
            scale = jnp.maximum(jnp.max(jnp.abs(x)) / qmax, 1e-12)
            return jnp.clip(jnp.round(x / scale), -qmax - 1.0, qmax) * scale

        def fixed_qdq_u16(x):
            scale = 1.0 / 65536.0
            return jnp.clip(jnp.round(x / scale), 0.0, 65535.0) * scale

        def lpbq_dequant(w):
            O, I = w.shape
            qmax = 2.0 ** (W_BITS - 1) - 1.0
            wb = w.reshape(O, I // BLOCK, BLOCK)
            s = jnp.maximum(jnp.max(jnp.abs(wb), axis=-1, keepdims=True) / qmax, 1e-12)
            wq = jnp.clip(jnp.round(wb / s), -qmax - 1.0, qmax) * s
            return wq.reshape(O, I)
        key = jax.random.key(seed)
        k1, k2, k3, k4 = jax.random.split(key, 4)
        B, S, H, I = (2, 1024, 256, 768)
        x = jax.random.normal(k1, (B, S, H), jnp.float32)
        w_gate = jax.random.normal(k2, (I, H), jnp.float32) * 0.02
        w_up = jax.random.normal(k3, (I, H), jnp.float32) * 0.02
        w_down = jax.random.normal(k4, (H, I), jnp.float32) * 0.02
        return {'x': x, 'w_gate': w_gate, 'w_up': w_up, 'w_down': w_down}
    _L0_ffn_all = _L0_ffn_setup()
    _L0_ffn_in = {k: v for k, v in _L0_ffn_all.items() if k in ('w_gate', 'w_up', 'w_down')}
    del _L0_ffn_all

    def _L1_xattn_setup():
        import jax, jax.numpy as jnp
        import numpy as np
        D_MODEL = 256
        N_HEAD = 16
        D_K = D_MODEL // N_HEAD

        def _split_heads(x):
            B, S, _ = x.shape
            return x.reshape(B, S, N_HEAD, D_K).transpose(0, 2, 1, 3)
        key = jax.random.key(seed)
        ks = jax.random.split(key, 11)
        B, S = (2, 512)
        scale = 1.0 / np.sqrt(D_MODEL)
        inp = {'q': jax.random.normal(ks[0], (B, S, D_MODEL), jnp.float32), 'k': jax.random.normal(ks[1], (B, S, D_MODEL), jnp.float32), 'v': jax.random.normal(ks[2], (B, S, D_MODEL), jnp.float32), 'Wq': jax.random.normal(ks[3], (D_MODEL, D_MODEL), jnp.float32) * scale, 'bq': jnp.zeros((D_MODEL,), jnp.float32), 'Wk': jax.random.normal(ks[4], (D_MODEL, D_MODEL), jnp.float32) * scale, 'bk': jnp.zeros((D_MODEL,), jnp.float32), 'Wv': jax.random.normal(ks[5], (D_MODEL, D_MODEL), jnp.float32) * scale, 'bv': jnp.zeros((D_MODEL,), jnp.float32), 'Wo': jax.random.normal(ks[6], (D_MODEL, D_MODEL), jnp.float32) * scale, 'bo': jnp.zeros((D_MODEL,), jnp.float32)}
        return inp
    _L1_xattn_all = _L1_xattn_setup()
    _L1_xattn_in = {k: v for k, v in _L1_xattn_all.items() if k in ('Wq', 'bq', 'Wk', 'bk', 'Wv', 'bv', 'Wo', 'bo')}
    del _L1_xattn_all

    def _L1_attn_setup():
        import jax, jax.numpy as jnp
        import numpy as np
        D_MODEL = 256
        N_HEADS = 16
        N_GROUPS = 4
        D_HEAD = D_MODEL // N_HEADS
        HPG = N_HEADS // N_GROUPS
        B, T = (2, 512)

        def _rope(x):
            t, d = (x.shape[2], x.shape[3])
            pos = jnp.arange(t, dtype=jnp.float32)[:, None]
            freq = jnp.exp(-(jnp.arange(0, d, 2, dtype=jnp.float32) / d) * jnp.log(jnp.float32(10000.0)))
            angle = pos * freq
            cos, sin = (jnp.cos(angle), jnp.sin(angle))
            xe, xo = (x[..., ::2], x[..., 1::2])
            re = xe * cos - xo * sin
            ro = xe * sin + xo * cos
            return jnp.stack([re, ro], axis=-1).reshape(x.shape)
        key = jax.random.key(seed)
        ks = jax.random.split(key, 10)
        s = 0.02
        return {'x': jax.random.normal(ks[0], (B, T, D_MODEL), dtype=jnp.float32), 'Wq': jax.random.normal(ks[1], (D_MODEL, D_MODEL), dtype=jnp.float32) * s, 'bq': jax.random.normal(ks[2], (D_MODEL,), dtype=jnp.float32) * s, 'Wk': jax.random.normal(ks[3], (D_MODEL, N_GROUPS * D_HEAD), dtype=jnp.float32) * s, 'bk': jax.random.normal(ks[4], (N_GROUPS * D_HEAD,), dtype=jnp.float32) * s, 'Wv': jax.random.normal(ks[5], (D_MODEL, N_GROUPS * D_HEAD), dtype=jnp.float32) * s, 'bv': jax.random.normal(ks[6], (N_GROUPS * D_HEAD,), dtype=jnp.float32) * s, 'Wo': jax.random.normal(ks[7], (D_MODEL, D_MODEL), dtype=jnp.float32) * s, 'bo': jax.random.normal(ks[8], (D_MODEL,), dtype=jnp.float32) * s}
    _L1_attn_all = _L1_attn_setup()
    _L1_attn_in = {k: v for k, v in _L1_attn_all.items() if k in ('Wq', 'bq', 'Wk', 'bk', 'Wv', 'bv', 'Wo', 'bo')}
    del _L1_attn_all

    def _L1_ffn_setup():
        import jax, jax.numpy as jnp
        import numpy as np
        from jax import lax
        T, B, I, M, O = (64, 64, 256, 256, 256)

        def _xavier(key, shape):
            fan_out, fan_in = shape
            limit = float(np.sqrt(6.0 / (fan_in + fan_out)))
            return jax.random.uniform(key, shape, jnp.float32, -limit, limit)
        key = jax.random.key(seed)
        ks = jax.random.split(key, 9)
        x = jax.random.normal(ks[0], (T, B, I), jnp.float32)
        return {'x': x, 'wf': _xavier(ks[1], (M, I)), 'uf': _xavier(ks[2], (M, M)), 'bf': jnp.zeros((M,), jnp.float32), 'wi': _xavier(ks[3], (M, I)), 'ui': _xavier(ks[4], (M, M)), 'bi': jnp.zeros((M,), jnp.float32), 'wc': _xavier(ks[5], (M, I)), 'uc': _xavier(ks[6], (M, M)), 'bc': jnp.zeros((M,), jnp.float32), 'wo': _xavier(ks[7], (O, I)), 'uo': _xavier(ks[8], (O, M)), 'bo': jnp.zeros((O,), jnp.float32), 'in_c': jnp.zeros((M,), jnp.float32)}
    _L1_ffn_all = _L1_ffn_setup()
    _L1_ffn_in = {k: v for k, v in _L1_ffn_all.items() if k in ('wf', 'uf', 'bf', 'wi', 'ui', 'bi', 'wc', 'uc', 'bc', 'wo', 'uo', 'bo', 'in_c')}
    del _L1_ffn_all

    def _L2_xattn_setup():
        import jax, jax.numpy as jnp
        import numpy as np
        HIDDEN = 256
        NUM_HEAD = 16
        HEAD_DIM = HIDDEN // NUM_HEAD

        def _split_heads(x):
            bs, seq, _ = x.shape
            return x.reshape(bs, seq, NUM_HEAD, HEAD_DIM).transpose(0, 2, 1, 3)
        key = jax.random.key(seed)
        ks = jax.random.split(key, 12)
        bs, seq = (4, 512)
        inp = {'srcQ': jax.random.normal(ks[0], (bs, seq, HIDDEN), jnp.float32), 'srcK': jax.random.normal(ks[1], (bs, seq, HIDDEN), jnp.float32), 'srcV': jax.random.normal(ks[2], (bs, seq, HIDDEN), jnp.float32), 'mask': jnp.ones((bs, 1, 1, seq), jnp.int32), 'Wq': jax.random.normal(ks[3], (HIDDEN, HIDDEN), jnp.float32) * 0.02, 'bq': jnp.zeros((HIDDEN,), jnp.float32), 'Wk': jax.random.normal(ks[4], (HIDDEN, HIDDEN), jnp.float32) * 0.02, 'bk': jnp.zeros((HIDDEN,), jnp.float32), 'Wv': jax.random.normal(ks[5], (HIDDEN, HIDDEN), jnp.float32) * 0.02, 'bv': jnp.zeros((HIDDEN,), jnp.float32), 'Wo': jax.random.normal(ks[6], (HIDDEN, HIDDEN), jnp.float32) * 0.02, 'bo': jnp.zeros((HIDDEN,), jnp.float32)}
        return inp
    _L2_xattn_all = _L2_xattn_setup()
    _L2_xattn_in = {k: v for k, v in _L2_xattn_all.items() if k in ('Wq', 'bq', 'Wk', 'bk', 'Wv', 'bv', 'Wo', 'bo')}
    del _L2_xattn_all

    def _L2_attn_setup():
        import jax, jax.numpy as jnp
        import numpy as np
        N_HEADS = 16
        EPS = 1e-06
        key = jax.random.key(seed)
        ks = jax.random.split(key, 5)
        B, N, D, H = (4, 512, 256, N_HEADS)
        x = jax.random.normal(ks[0], (B, N, D), dtype=jnp.float32)
        Wq = jax.random.normal(ks[1], (D, D), dtype=jnp.float32) * D ** (-0.5)
        Wk = jax.random.normal(ks[2], (D, D), dtype=jnp.float32) * D ** (-0.5)
        Wv = jax.random.normal(ks[3], (D, D), dtype=jnp.float32) * D ** (-0.5)
        Wo = jax.random.normal(ks[4], (D, D), dtype=jnp.float32) * D ** (-0.5)
        q_scale = jnp.ones((H,), dtype=jnp.float32)
        k_scale = jnp.ones((H,), dtype=jnp.float32)
        return {'x': x, 'Wq': Wq, 'Wk': Wk, 'Wv': Wv, 'Wo': Wo, 'q_scale': q_scale, 'k_scale': k_scale}
    _L2_attn_all = _L2_attn_setup()
    _L2_attn_in = {k: v for k, v in _L2_attn_all.items() if k in ('Wq', 'Wk', 'Wv', 'Wo', 'q_scale', 'k_scale')}
    del _L2_attn_all

    def _L2_ffn_setup():
        import jax, jax.numpy as jnp
        import numpy as np
        E = 8
        K = 2
        D = 256
        H = 684
        B, S = (2, 512)

        def _moe_forward(x, centroid, Wg, bg, W1, b1, W2, b2):
            T = x.shape[0] * x.shape[1]
            xs = x.reshape(T, D)
            d2 = jnp.sum(xs * xs, axis=-1, keepdims=True) + jnp.sum(centroid * centroid, axis=-1)[None, :] - 2.0 * (xs @ centroid.T)
            dist = jnp.sqrt(jnp.maximum(d2, 1e-12))
            w, sel = jax.lax.top_k(dist, K)
            w = jax.nn.softmax(w.astype(jnp.float32), axis=1).astype(x.dtype)
            we = jnp.zeros((T, E), dtype=x.dtype).at[jnp.arange(T)[:, None], sel].add(w)
            out = jnp.zeros_like(xs)
            for e in range(E):
                h = jax.nn.silu(xs @ Wg[e] + bg[e]) * (xs @ W1[e] + b1[e])
                out = out + we[:, e:e + 1] * (h @ W2[e] + b2[e])
            return out.reshape(x.shape)
        key = jax.random.key(seed)
        ks = jax.random.split(key, 9)
        scale = 0.02
        return {'x': jax.random.normal(ks[0], (B, S, D), dtype=jnp.float32), 'centroid': jax.random.normal(ks[1], (E, D), dtype=jnp.float32), 'Wg': jax.random.normal(ks[2], (E, D, H), dtype=jnp.float32) * scale, 'bg': jnp.zeros((E, H), dtype=jnp.float32), 'W1': jax.random.normal(ks[3], (E, D, H), dtype=jnp.float32) * scale, 'b1': jnp.zeros((E, H), dtype=jnp.float32), 'W2': jax.random.normal(ks[4], (E, H, D), dtype=jnp.float32) * scale, 'b2': jnp.zeros((E, D), dtype=jnp.float32)}
    _L2_ffn_all = _L2_ffn_setup()
    _L2_ffn_in = {k: v for k, v in _L2_ffn_all.items() if k in ('centroid', 'Wg', 'bg', 'W1', 'b1', 'W2', 'b2')}
    del _L2_ffn_all

    def _L3_xattn_setup():
        import jax, jax.numpy as jnp
        import numpy as np
        E = 256
        H = 16
        D = E // H
        B, L, S = (2, 512, 512)
        key = jax.random.key(seed)
        ks = jax.random.split(key, 10)
        scale = 1.0 / np.sqrt(E)
        return {'x': jax.random.normal(ks[0], (B, L, E), jnp.float32), 'context': jax.random.normal(ks[1], (B, S, E), jnp.float32), 'Wq': jax.random.normal(ks[2], (E, E), jnp.float32) * scale, 'bq': jnp.zeros((E,), jnp.float32), 'Wk': jax.random.normal(ks[3], (E, E), jnp.float32) * scale, 'bk': jnp.zeros((E,), jnp.float32), 'Wv': jax.random.normal(ks[4], (E, E), jnp.float32) * scale, 'bv': jnp.zeros((E,), jnp.float32), 'Wp': jax.random.normal(ks[5], (E, E), jnp.float32) * scale, 'bp': jnp.zeros((E,), jnp.float32)}
    _L3_xattn_all = _L3_xattn_setup()
    _L3_xattn_in = {k: v for k, v in _L3_xattn_all.items() if k in ('Wq', 'bq', 'Wk', 'bk', 'Wv', 'bv', 'Wp', 'bp')}
    del _L3_xattn_all

    def _L3_attn_setup():
        import jax, jax.numpy as jnp
        import numpy as np
        from math import sqrt
        N_HEAD = 16
        W_SCALE = 0.02

        def _reference_tuple_inner(x, W_dq, W_uq, W_dkv, W_uk, W_uv, W_o):
            B, T, C = x.shape
            nh = N_HEAD
            hs = C // nh
            n_kvl = W_dkv.shape[0]
            k_eff = (W_dq.T @ W_uq.T @ W_uk).reshape(nh, hs, n_kvl)
            v_eff = jnp.transpose((W_uv.T @ W_o.T).reshape(n_kvl, nh, hs), (1, 0, 2))
            c_kv = x @ W_dkv.T
            q = x @ W_dq.T @ W_uq.T
            q = q.reshape(B, T, nh, hs)
            q_lat = jnp.einsum('bqhd,hdl->bhql', q, k_eff)
            attn = jnp.einsum('bhql,bkl->bhqk', q_lat, c_kv) / sqrt(hs)
            causal = jnp.tril(jnp.ones((T, T), dtype=bool))
            attn = jnp.where(causal[None, None], attn, -jnp.inf)
            attn = jax.nn.softmax(attn, axis=-1)
            y_lat = jnp.einsum('bhqk,bkl->bhql', attn, c_kv)
            y = jnp.einsum('bhql,hld->bqhd', y_lat, v_eff).reshape(B, T, C)
            return (y, c_kv)
        key = jax.random.key(seed)
        ks = jax.random.split(key, 7)
        B, T, C = (2, 512, 256)
        QL, KVL = (128, 128)
        return {'x': jax.random.normal(ks[0], (B, T, C), dtype=jnp.float32), 'W_dq': jax.random.normal(ks[1], (QL, C), dtype=jnp.float32) * W_SCALE, 'W_uq': jax.random.normal(ks[2], (C, QL), dtype=jnp.float32) * W_SCALE, 'W_dkv': jax.random.normal(ks[3], (KVL, C), dtype=jnp.float32) * W_SCALE, 'W_uk': jax.random.normal(ks[4], (C, KVL), dtype=jnp.float32) * W_SCALE, 'W_uv': jax.random.normal(ks[5], (C, KVL), dtype=jnp.float32) * W_SCALE, 'W_o': jax.random.normal(ks[6], (C, C), dtype=jnp.float32) * W_SCALE}
    _L3_attn_all = _L3_attn_setup()
    _L3_attn_in = {k: v for k, v in _L3_attn_all.items() if k in ('W_dq', 'W_uq', 'W_dkv', 'W_uk', 'W_uv', 'W_o')}
    del _L3_attn_all

    def _L3_ffn_setup():
        import jax, jax.numpy as jnp
        import numpy as np
        S, B, H, F, E, K = (512, 2, 256, 512, 8, 2)

        def _moe_forward(hidden_states, router_w, w1, b1, w2, b2):
            s, b, h = hidden_states.shape
            T = s * b
            x = hidden_states.reshape(T, h)
            logits = jnp.einsum('th,eh->te', x, router_w)
            topk_logits, topk_idx = jax.lax.top_k(logits, K)
            probs = jax.nn.softmax(topk_logits, axis=-1)
            combine = jnp.zeros((T, E), dtype=x.dtype)
            combine = combine.at[jnp.arange(T)[:, None], topk_idx].add(probs.astype(x.dtype))
            hmid = jnp.einsum('th,efh->etf', x, w1) + b1[:, None, :]
            hmid = jax.nn.gelu(hmid, approximate=False)
            y = jnp.einsum('etf,ehf->eth', hmid, w2) + b2[:, None, :]
            out = jnp.einsum('eth,te->th', y, combine)
            return out.reshape(s, b, h)
        key = jax.random.key(seed)
        ks = jax.random.split(key, 6)
        std = 0.02
        return {'hidden_states': jax.random.normal(ks[0], (S, B, H), dtype=jnp.float32), 'router_w': jax.random.normal(ks[1], (E, H), dtype=jnp.float32) * std, 'w1': jax.random.normal(ks[2], (E, F, H), dtype=jnp.float32) * (1.0 / np.sqrt(H)), 'b1': jnp.zeros((E, F), dtype=jnp.float32), 'w2': jax.random.normal(ks[3], (E, H, F), dtype=jnp.float32) * (1.0 / np.sqrt(F)), 'b2': jnp.zeros((E, H), dtype=jnp.float32)}
    _L3_ffn_all = _L3_ffn_setup()
    _L3_ffn_in = {k: v for k, v in _L3_ffn_all.items() if k in ('router_w', 'w1', 'b1', 'w2', 'b2')}
    del _L3_ffn_all
    return {'x': x, 'ctx_1024': ctx_1024, 'mask_Bx1xSxS2_ff0': mask_Bx1xSxS2_ff0, 'mask_Bx1x1xS2_if1': mask_Bx1x1xS2_if1, 'L0_xattn_Wq': _L0_xattn_in['Wq'], 'L0_xattn_bq': _L0_xattn_in['bq'], 'L0_xattn_Wk': _L0_xattn_in['Wk'], 'L0_xattn_bk': _L0_xattn_in['bk'], 'L0_xattn_Wv': _L0_xattn_in['Wv'], 'L0_xattn_bv': _L0_xattn_in['bv'], 'L0_xattn_Wo': _L0_xattn_in['Wo'], 'L0_xattn_bo': _L0_xattn_in['bo'], 'L0_attn_w_in': _L0_attn_in['w_in'], 'L0_attn_w_out': _L0_attn_in['w_out'], 'L0_ffn_w_gate': _L0_ffn_in['w_gate'], 'L0_ffn_w_up': _L0_ffn_in['w_up'], 'L0_ffn_w_down': _L0_ffn_in['w_down'], 'L1_xattn_Wq': _L1_xattn_in['Wq'], 'L1_xattn_bq': _L1_xattn_in['bq'], 'L1_xattn_Wk': _L1_xattn_in['Wk'], 'L1_xattn_bk': _L1_xattn_in['bk'], 'L1_xattn_Wv': _L1_xattn_in['Wv'], 'L1_xattn_bv': _L1_xattn_in['bv'], 'L1_xattn_Wo': _L1_xattn_in['Wo'], 'L1_xattn_bo': _L1_xattn_in['bo'], 'L1_attn_Wq': _L1_attn_in['Wq'], 'L1_attn_bq': _L1_attn_in['bq'], 'L1_attn_Wk': _L1_attn_in['Wk'], 'L1_attn_bk': _L1_attn_in['bk'], 'L1_attn_Wv': _L1_attn_in['Wv'], 'L1_attn_bv': _L1_attn_in['bv'], 'L1_attn_Wo': _L1_attn_in['Wo'], 'L1_attn_bo': _L1_attn_in['bo'], 'L1_ffn_wf': _L1_ffn_in['wf'], 'L1_ffn_uf': _L1_ffn_in['uf'], 'L1_ffn_bf': _L1_ffn_in['bf'], 'L1_ffn_wi': _L1_ffn_in['wi'], 'L1_ffn_ui': _L1_ffn_in['ui'], 'L1_ffn_bi': _L1_ffn_in['bi'], 'L1_ffn_wc': _L1_ffn_in['wc'], 'L1_ffn_uc': _L1_ffn_in['uc'], 'L1_ffn_bc': _L1_ffn_in['bc'], 'L1_ffn_wo': _L1_ffn_in['wo'], 'L1_ffn_uo': _L1_ffn_in['uo'], 'L1_ffn_bo': _L1_ffn_in['bo'], 'L1_ffn_in_c': _L1_ffn_in['in_c'], 'L2_xattn_Wq': _L2_xattn_in['Wq'], 'L2_xattn_bq': _L2_xattn_in['bq'], 'L2_xattn_Wk': _L2_xattn_in['Wk'], 'L2_xattn_bk': _L2_xattn_in['bk'], 'L2_xattn_Wv': _L2_xattn_in['Wv'], 'L2_xattn_bv': _L2_xattn_in['bv'], 'L2_xattn_Wo': _L2_xattn_in['Wo'], 'L2_xattn_bo': _L2_xattn_in['bo'], 'L2_attn_Wq': _L2_attn_in['Wq'], 'L2_attn_Wk': _L2_attn_in['Wk'], 'L2_attn_Wv': _L2_attn_in['Wv'], 'L2_attn_Wo': _L2_attn_in['Wo'], 'L2_attn_q_scale': _L2_attn_in['q_scale'], 'L2_attn_k_scale': _L2_attn_in['k_scale'], 'L2_ffn_centroid': _L2_ffn_in['centroid'], 'L2_ffn_Wg': _L2_ffn_in['Wg'], 'L2_ffn_bg': _L2_ffn_in['bg'], 'L2_ffn_W1': _L2_ffn_in['W1'], 'L2_ffn_b1': _L2_ffn_in['b1'], 'L2_ffn_W2': _L2_ffn_in['W2'], 'L2_ffn_b2': _L2_ffn_in['b2'], 'L3_xattn_Wq': _L3_xattn_in['Wq'], 'L3_xattn_bq': _L3_xattn_in['bq'], 'L3_xattn_Wk': _L3_xattn_in['Wk'], 'L3_xattn_bk': _L3_xattn_in['bk'], 'L3_xattn_Wv': _L3_xattn_in['Wv'], 'L3_xattn_bv': _L3_xattn_in['bv'], 'L3_xattn_Wp': _L3_xattn_in['Wp'], 'L3_xattn_bp': _L3_xattn_in['bp'], 'L3_attn_W_dq': _L3_attn_in['W_dq'], 'L3_attn_W_uq': _L3_attn_in['W_uq'], 'L3_attn_W_dkv': _L3_attn_in['W_dkv'], 'L3_attn_W_uk': _L3_attn_in['W_uk'], 'L3_attn_W_uv': _L3_attn_in['W_uv'], 'L3_attn_W_o': _L3_attn_in['W_o'], 'L3_ffn_router_w': _L3_ffn_in['router_w'], 'L3_ffn_w1': _L3_ffn_in['w1'], 'L3_ffn_b1': _L3_ffn_in['b1'], 'L3_ffn_w2': _L3_ffn_in['w2'], 'L3_ffn_b2': _L3_ffn_in['b2']}

def reference(x, ctx_1024, mask_Bx1xSxS2_ff0, mask_Bx1x1xS2_if1, L0_xattn_Wq, L0_xattn_bq, L0_xattn_Wk, L0_xattn_bk, L0_xattn_Wv, L0_xattn_bv, L0_xattn_Wo, L0_xattn_bo, L0_attn_w_in, L0_attn_w_out, L0_ffn_w_gate, L0_ffn_w_up, L0_ffn_w_down, L1_xattn_Wq, L1_xattn_bq, L1_xattn_Wk, L1_xattn_bk, L1_xattn_Wv, L1_xattn_bv, L1_xattn_Wo, L1_xattn_bo, L1_attn_Wq, L1_attn_bq, L1_attn_Wk, L1_attn_bk, L1_attn_Wv, L1_attn_bv, L1_attn_Wo, L1_attn_bo, L1_ffn_wf, L1_ffn_uf, L1_ffn_bf, L1_ffn_wi, L1_ffn_ui, L1_ffn_bi, L1_ffn_wc, L1_ffn_uc, L1_ffn_bc, L1_ffn_wo, L1_ffn_uo, L1_ffn_bo, L1_ffn_in_c, L2_xattn_Wq, L2_xattn_bq, L2_xattn_Wk, L2_xattn_bk, L2_xattn_Wv, L2_xattn_bv, L2_xattn_Wo, L2_xattn_bo, L2_attn_Wq, L2_attn_Wk, L2_attn_Wv, L2_attn_Wo, L2_attn_q_scale, L2_attn_k_scale, L2_ffn_centroid, L2_ffn_Wg, L2_ffn_bg, L2_ffn_W1, L2_ffn_b1, L2_ffn_W2, L2_ffn_b2, L3_xattn_Wq, L3_xattn_bq, L3_xattn_Wk, L3_xattn_bk, L3_xattn_Wv, L3_xattn_bv, L3_xattn_Wp, L3_xattn_bp, L3_attn_W_dq, L3_attn_W_uq, L3_attn_W_dkv, L3_attn_W_uk, L3_attn_W_uv, L3_attn_W_o, L3_ffn_router_w, L3_ffn_w1, L3_ffn_b1, L3_ffn_w2, L3_ffn_b2):
    import jax
    import jax.numpy as jnp

    def _L0_xattn_ref(q, k, v, mask, Wq, bq, Wk, bk, Wv, bv, Wo, bo):
        import jax, jax.numpy as jnp
        import numpy as np
        B, S, D, H = (2, 512, 256, 16)
        HD = D // H

        def _split_heads(x):
            b, s, _ = x.shape
            return x.reshape(b, s, H, HD).transpose(0, 2, 1, 3)
        qh = _split_heads(q @ Wq + bq)
        kh = _split_heads(k @ Wk + bk)
        vh = _split_heads(v @ Wv + bv)
        scores = jnp.einsum('bhqd,bhkd->bhqk', qh, kh) / jnp.sqrt(jnp.float32(D))
        scores = scores + mask * -1000000000.0
        attn = jax.nn.softmax(scores, axis=-1)
        out = jnp.einsum('bhqk,bhkd->bhqd', attn, vh)
        out = out.transpose(0, 2, 1, 3).reshape(q.shape[0], -1, D)
        return out @ Wo + bo

    def _L0_attn_ref(x, w_in, w_out):
        import jax, jax.numpy as jnp
        import numpy as np
        NUM_HEADS = 16
        N_EMBD = 256

        def alibi_bias(num_heads: int, seq_len: int) -> jnp.ndarray:
            pos = jnp.arange(seq_len, dtype=jnp.float32)
            dgrid = pos[None, :] - pos[:, None]
            slopes = 2.0 ** (-8.0 / num_heads * (jnp.arange(num_heads, dtype=jnp.float32) + 1.0))
            bias = slopes[:, None, None] * dgrid[None, :, :]
            return jnp.where(dgrid[None, :, :] > 0, -jnp.inf, bias)
        B, L, E = x.shape
        H = NUM_HEADS
        D = E // H
        qkv = jnp.einsum('ble,fe->blf', x, w_in)
        q, k, v = jnp.split(qkv, 3, axis=-1)

        def to_heads(t):
            return t.reshape(B, L, H, D).transpose(0, 2, 1, 3)
        q, k, v = (to_heads(q), to_heads(k), to_heads(v))
        scale = 1.0 / jnp.sqrt(jnp.asarray(D, dtype=x.dtype))
        scores = jnp.einsum('bhqd,bhkd->bhqk', q, k) * scale
        scores = scores + alibi_bias(H, L)[None]
        attn = jax.nn.softmax(scores, axis=-1)
        ctx = jnp.einsum('bhqk,bhkd->bhqd', attn, v)
        ctx = ctx.transpose(0, 2, 1, 3).reshape(B, L, E)
        return jnp.einsum('ble,fe->blf', ctx, w_out)

    def _L0_ffn_ref(x, w_gate, w_up, w_down):
        import jax, jax.numpy as jnp
        import numpy as np
        BLOCK = 32
        W_BITS = 4
        ACT_BITS = 16

        def act_qdq(x):
            qmax = 2.0 ** (ACT_BITS - 1) - 1.0
            scale = jnp.maximum(jnp.max(jnp.abs(x)) / qmax, 1e-12)
            return jnp.clip(jnp.round(x / scale), -qmax - 1.0, qmax) * scale

        def fixed_qdq_u16(x):
            scale = 1.0 / 65536.0
            return jnp.clip(jnp.round(x / scale), 0.0, 65535.0) * scale

        def lpbq_dequant(w):
            O, I = w.shape
            qmax = 2.0 ** (W_BITS - 1) - 1.0
            wb = w.reshape(O, I // BLOCK, BLOCK)
            s = jnp.maximum(jnp.max(jnp.abs(wb), axis=-1, keepdims=True) / qmax, 1e-12)
            wq = jnp.clip(jnp.round(wb / s), -qmax - 1.0, qmax) * s
            return wq.reshape(O, I)
        x = act_qdq(x)
        up = act_qdq(x @ lpbq_dequant(w_up).T)
        gate = act_qdq(x @ lpbq_dequant(w_gate).T)
        sig = fixed_qdq_u16(jax.nn.sigmoid(gate))
        gate = act_qdq(gate * sig)
        o = act_qdq(gate * up)
        return o @ lpbq_dequant(w_down).T

    def _L1_xattn_ref(q, k, v, Wq, bq, Wk, bk, Wv, bv, Wo, bo):
        import jax, jax.numpy as jnp
        import numpy as np
        D_MODEL = 256
        N_HEAD = 16
        D_K = D_MODEL // N_HEAD

        def _split_heads(x):
            B, S, _ = x.shape
            return x.reshape(B, S, N_HEAD, D_K).transpose(0, 2, 1, 3)
        qh = _split_heads(q @ Wq.T + bq)
        kh = _split_heads(k @ Wk.T + bk)
        vh = _split_heads(v @ Wv.T + bv)
        score = jnp.einsum('bhqd,bhkd->bhqk', qh, kh) / jnp.sqrt(jnp.float32(D_K))
        attn = jax.nn.softmax(score, axis=-1)
        out = jnp.einsum('bhqk,bhkd->bhqd', attn, vh)
        B, H, S, Dk = out.shape
        out = out.transpose(0, 2, 1, 3).reshape(B, S, H * Dk)
        return out @ Wo.T + bo

    def _L1_attn_ref(x, Wq, bq, Wk, bk, Wv, bv, Wo, bo):
        import jax, jax.numpy as jnp
        import numpy as np
        D_MODEL = 256
        N_HEADS = 16
        N_GROUPS = 4
        D_HEAD = D_MODEL // N_HEADS
        HPG = N_HEADS // N_GROUPS
        B, T = (2, 512)

        def _rope(x):
            t, d = (x.shape[2], x.shape[3])
            pos = jnp.arange(t, dtype=jnp.float32)[:, None]
            freq = jnp.exp(-(jnp.arange(0, d, 2, dtype=jnp.float32) / d) * jnp.log(jnp.float32(10000.0)))
            angle = pos * freq
            cos, sin = (jnp.cos(angle), jnp.sin(angle))
            xe, xo = (x[..., ::2], x[..., 1::2])
            re = xe * cos - xo * sin
            ro = xe * sin + xo * cos
            return jnp.stack([re, ro], axis=-1).reshape(x.shape)
        b, t, _ = x.shape
        q = (x @ Wq + bq).reshape(b, t, N_HEADS, D_HEAD).transpose(0, 2, 1, 3)
        k = (x @ Wk + bk).reshape(b, t, N_GROUPS, D_HEAD).transpose(0, 2, 1, 3)
        v = (x @ Wv + bv).reshape(b, t, N_GROUPS, D_HEAD).transpose(0, 2, 1, 3)
        k = jnp.repeat(k, HPG, axis=1)
        v = jnp.repeat(v, HPG, axis=1)
        q = _rope(q)
        k = _rope(k)
        scale = jnp.float32(np.sqrt(D_HEAD))
        scores = jnp.einsum('bhtd,bhsd->bhts', q, k) / scale
        causal = jnp.tril(jnp.ones((t, t), dtype=bool))
        scores = jnp.where(causal, scores, -jnp.inf)
        probs = jax.nn.softmax(scores, axis=-1)
        attn = jnp.einsum('bhts,bhsd->bhtd', probs, v)
        out = attn.transpose(0, 2, 1, 3).reshape(b, t, N_HEADS * D_HEAD)
        return out @ Wo + bo

    def _L1_ffn_ref(x, wf, uf, bf, wi, ui, bi, wc, uc, bc, wo, uo, bo, in_c):
        import jax, jax.numpy as jnp
        import numpy as np
        from jax import lax
        T, B, I, M, O = (64, 64, 256, 256, 256)

        def _xavier(key, shape):
            fan_out, fan_in = shape
            limit = float(np.sqrt(6.0 / (fan_in + fan_out)))
            return jax.random.uniform(key, shape, jnp.float32, -limit, limit)
        batch = x.shape[1]
        c0 = jnp.broadcast_to(in_c, (batch, in_c.shape[0]))

        def step(c, xt):
            ft = jax.nn.sigmoid(xt @ wf.T + c @ uf.T + bf)
            it = jax.nn.sigmoid(xt @ wi.T + c @ ui.T + bi)
            gt = jnp.tanh(xt @ wc.T + c @ uc.T + bc)
            c = ft * c + it * gt
            return (c, None)
        c_final, _ = lax.scan(step, c0, x)
        h = jnp.tanh(jnp.einsum('tbi,oi->tbo', x, wo) + c_final @ uo.T + bo)
        return h

    def _L2_xattn_ref(srcQ, srcK, srcV, mask, Wq, bq, Wk, bk, Wv, bv, Wo, bo):
        import jax, jax.numpy as jnp
        import numpy as np
        HIDDEN = 256
        NUM_HEAD = 16
        HEAD_DIM = HIDDEN // NUM_HEAD

        def _split_heads(x):
            bs, seq, _ = x.shape
            return x.reshape(bs, seq, NUM_HEAD, HEAD_DIM).transpose(0, 2, 1, 3)
        Q = _split_heads(srcQ @ Wq + bq)
        K = _split_heads(srcK @ Wk + bk)
        V = _split_heads(srcV @ Wv + bv)
        scores = jnp.einsum('bhqd,bhkd->bhqk', Q, K)
        scores = jnp.where(mask == 0, jnp.float32(-10000.0), scores)
        attn = jax.nn.softmax(scores, axis=-1)
        out = jnp.einsum('bhqk,bhkd->bhqd', attn, V)
        bs, _, seq, _ = out.shape
        out = out.transpose(0, 2, 1, 3).reshape(bs, seq, HIDDEN)
        return out @ Wo + bo

    def _L2_attn_ref(x, Wq, Wk, Wv, Wo, q_scale, k_scale):
        import jax, jax.numpy as jnp
        import numpy as np
        N_HEADS = 16
        EPS = 1e-06
        B, N, D = x.shape
        H = N_HEADS
        hd = D // H
        q = jax.nn.silu(x @ Wq.T)
        k = jax.nn.silu(x @ Wk.T)
        v = jax.nn.silu(x @ Wv.T)
        q = q.reshape(B, N, H, hd).transpose(0, 2, 1, 3)
        k = k.reshape(B, N, H, hd).transpose(0, 2, 1, 3)
        v = v.reshape(B, N, H, hd).transpose(0, 2, 1, 3)
        r_q = jnp.linalg.norm(q, axis=-1, keepdims=True)
        r_k = jnp.linalg.norm(k, axis=-1, keepdims=True)
        q_dir = q / (r_q + EPS)
        k_dir = k / (r_k + EPS)
        scores = jnp.einsum('bhnd,bhmd->bhnm', q_dir, k_dir)
        sq = q_scale[None, :, None, None]
        sk = k_scale[None, :, None, None]
        scores = scores * (r_q * sq) * (jnp.swapaxes(r_k, -2, -1) * sk)
        mask = jnp.tril(jnp.ones((N, N), dtype=bool))
        scores = jnp.where(mask, scores, -jnp.inf)
        probs = jax.nn.softmax(scores, axis=-1)
        out = jnp.einsum('bhnm,bhmd->bhnd', probs, v)
        out = out.transpose(0, 2, 1, 3).reshape(B, N, D)
        return out @ Wo.T

    def _L2_ffn_ref(x, centroid, Wg, bg, W1, b1, W2, b2):
        import jax, jax.numpy as jnp
        import numpy as np
        E = 8
        K = 2
        D = 256
        H = 684
        B, S = (2, 512)

        def _moe_forward(x, centroid, Wg, bg, W1, b1, W2, b2):
            T = x.shape[0] * x.shape[1]
            xs = x.reshape(T, D)
            d2 = jnp.sum(xs * xs, axis=-1, keepdims=True) + jnp.sum(centroid * centroid, axis=-1)[None, :] - 2.0 * (xs @ centroid.T)
            dist = jnp.sqrt(jnp.maximum(d2, 1e-12))
            w, sel = jax.lax.top_k(dist, K)
            w = jax.nn.softmax(w.astype(jnp.float32), axis=1).astype(x.dtype)
            we = jnp.zeros((T, E), dtype=x.dtype).at[jnp.arange(T)[:, None], sel].add(w)
            out = jnp.zeros_like(xs)
            for e in range(E):
                h = jax.nn.silu(xs @ Wg[e] + bg[e]) * (xs @ W1[e] + b1[e])
                out = out + we[:, e:e + 1] * (h @ W2[e] + b2[e])
            return out.reshape(x.shape)
        return _moe_forward(x, centroid, Wg, bg, W1, b1, W2, b2)

    def _L3_xattn_ref(x, context, Wq, bq, Wk, bk, Wv, bv, Wp, bp):
        import jax, jax.numpy as jnp
        import numpy as np
        E = 256
        H = 16
        D = E // H
        B, L, S = (2, 512, 512)
        b, l, _ = x.shape
        s = context.shape[1]
        q = (x @ Wq + bq).reshape(b, l, H, D).transpose(0, 2, 1, 3)
        k = (context @ Wk + bk).reshape(b, s, H, D).transpose(0, 2, 1, 3)
        v = (context @ Wv + bv).reshape(b, s, H, D).transpose(0, 2, 1, 3)
        attn = jnp.einsum('bhld,bhsd->bhls', q, k) / jnp.sqrt(jnp.float32(D))
        attn = jax.nn.softmax(attn, axis=-1)
        out = jnp.einsum('bhls,bhsd->bhld', attn, v)
        out = out.transpose(0, 2, 1, 3).reshape(b, l, E)
        return out @ Wp + bp

    def _L3_attn_ref(x, W_dq, W_uq, W_dkv, W_uk, W_uv, W_o):
        import jax, jax.numpy as jnp
        import numpy as np
        from math import sqrt
        N_HEAD = 16
        W_SCALE = 0.02

        def _reference_tuple_inner(x, W_dq, W_uq, W_dkv, W_uk, W_uv, W_o):
            B, T, C = x.shape
            nh = N_HEAD
            hs = C // nh
            n_kvl = W_dkv.shape[0]
            k_eff = (W_dq.T @ W_uq.T @ W_uk).reshape(nh, hs, n_kvl)
            v_eff = jnp.transpose((W_uv.T @ W_o.T).reshape(n_kvl, nh, hs), (1, 0, 2))
            c_kv = x @ W_dkv.T
            q = x @ W_dq.T @ W_uq.T
            q = q.reshape(B, T, nh, hs)
            q_lat = jnp.einsum('bqhd,hdl->bhql', q, k_eff)
            attn = jnp.einsum('bhql,bkl->bhqk', q_lat, c_kv) / sqrt(hs)
            causal = jnp.tril(jnp.ones((T, T), dtype=bool))
            attn = jnp.where(causal[None, None], attn, -jnp.inf)
            attn = jax.nn.softmax(attn, axis=-1)
            y_lat = jnp.einsum('bhqk,bkl->bhql', attn, c_kv)
            y = jnp.einsum('bhql,hld->bqhd', y_lat, v_eff).reshape(B, T, C)
            return (y, c_kv)
        return _reference_tuple_inner(x, W_dq, W_uq, W_dkv, W_uk, W_uv, W_o)[0]

    def _L3_ffn_ref(hidden_states, router_w, w1, b1, w2, b2):
        import jax, jax.numpy as jnp
        import numpy as np
        S, B, H, F, E, K = (512, 2, 256, 512, 8, 2)

        def _moe_forward(hidden_states, router_w, w1, b1, w2, b2):
            s, b, h = hidden_states.shape
            T = s * b
            x = hidden_states.reshape(T, h)
            logits = jnp.einsum('th,eh->te', x, router_w)
            topk_logits, topk_idx = jax.lax.top_k(logits, K)
            probs = jax.nn.softmax(topk_logits, axis=-1)
            combine = jnp.zeros((T, E), dtype=x.dtype)
            combine = combine.at[jnp.arange(T)[:, None], topk_idx].add(probs.astype(x.dtype))
            hmid = jnp.einsum('th,efh->etf', x, w1) + b1[:, None, :]
            hmid = jax.nn.gelu(hmid, approximate=False)
            y = jnp.einsum('etf,ehf->eth', hmid, w2) + b2[:, None, :]
            out = jnp.einsum('eth,te->th', y, combine)
            return out.reshape(s, b, h)
        return _moe_forward(hidden_states, router_w, w1, b1, w2, b2)
    x = x + _L0_xattn_ref(_layernorm(x, axis=-1), ctx_1024, ctx_1024, mask_Bx1xSxS2_ff0, L0_xattn_Wq, L0_xattn_bq, L0_xattn_Wk, L0_xattn_bk, L0_xattn_Wv, L0_xattn_bv, L0_xattn_Wo, L0_xattn_bo)
    x = x + _L0_attn_ref(_layernorm(x, axis=-1), L0_attn_w_in, L0_attn_w_out)
    x = x + _L0_ffn_ref(_layernorm(x, axis=-1), L0_ffn_w_gate, L0_ffn_w_up, L0_ffn_w_down)
    x = x + _L1_xattn_ref(_layernorm(x, axis=-1), ctx_1024, ctx_1024, L1_xattn_Wq, L1_xattn_bq, L1_xattn_Wk, L1_xattn_bk, L1_xattn_Wv, L1_xattn_bv, L1_xattn_Wo, L1_xattn_bo)
    x = x + _L1_attn_ref(_layernorm(x, axis=-1), L1_attn_Wq, L1_attn_bq, L1_attn_Wk, L1_attn_bk, L1_attn_Wv, L1_attn_bv, L1_attn_Wo, L1_attn_bo)
    x = x + _L1_ffn_ref(_layernorm(x, axis=-1), L1_ffn_wf, L1_ffn_uf, L1_ffn_bf, L1_ffn_wi, L1_ffn_ui, L1_ffn_bi, L1_ffn_wc, L1_ffn_uc, L1_ffn_bc, L1_ffn_wo, L1_ffn_uo, L1_ffn_bo, L1_ffn_in_c)
    x = x + _L2_xattn_ref(_layernorm(x, axis=-1), ctx_1024, ctx_1024, mask_Bx1x1xS2_if1, L2_xattn_Wq, L2_xattn_bq, L2_xattn_Wk, L2_xattn_bk, L2_xattn_Wv, L2_xattn_bv, L2_xattn_Wo, L2_xattn_bo)
    x = x + _L2_attn_ref(_layernorm(x, axis=-1), L2_attn_Wq, L2_attn_Wk, L2_attn_Wv, L2_attn_Wo, L2_attn_q_scale, L2_attn_k_scale)
    x = x + _L2_ffn_ref(_layernorm(x, axis=-1), L2_ffn_centroid, L2_ffn_Wg, L2_ffn_bg, L2_ffn_W1, L2_ffn_b1, L2_ffn_W2, L2_ffn_b2)
    x = x + _L3_xattn_ref(_layernorm(x, axis=-1), ctx_1024, L3_xattn_Wq, L3_xattn_bq, L3_xattn_Wk, L3_xattn_bk, L3_xattn_Wv, L3_xattn_bv, L3_xattn_Wp, L3_xattn_bp)
    x = x + _L3_attn_ref(_layernorm(x, axis=-1), L3_attn_W_dq, L3_attn_W_uq, L3_attn_W_dkv, L3_attn_W_uk, L3_attn_W_uv, L3_attn_W_o)
    x = x + _L3_ffn_ref(_layernorm(x, axis=-1), L3_ffn_router_w, L3_ffn_w1, L3_ffn_b1, L3_ffn_w2, L3_ffn_b2)
    return x

_drawn_inputs = setup_inputs


def setup_inputs(seed=0):
    import zlib

    import numpy as np

    out = dict(_drawn_inputs(seed))
    spreads = {'L0_xattn_bq': (0.0, 0.1),
     'L0_xattn_bk': (0.0, 0.1),
     'L0_xattn_bv': (0.0, 0.1),
     'L0_xattn_bo': (0.0, 0.1),
     'L1_xattn_bq': (0.0, 0.1),
     'L1_xattn_bk': (0.0, 2.0),
     'L1_xattn_bv': (0.0, 0.1),
     'L1_xattn_bo': (0.0, 0.1),
     'L1_ffn_bf': (0.0, 0.347),
     'L1_ffn_bi': (0.0, 0.297),
     'L1_ffn_bc': (0.0, 0.1),
     'L1_ffn_bo': (0.0, 0.1),
     'L1_ffn_in_c': (0.0, 0.8),
     'L2_xattn_bq': (0.0, 0.8),
     'L2_xattn_bk': (0.0, 2.0),
     'L2_xattn_bv': (0.0, 0.1),
     'L2_xattn_bo': (0.0, 0.1),
     'L2_attn_q_scale': (1.0, 0.2),
     'L2_attn_k_scale': (1.0, 0.2),
     'L2_ffn_bg': (0.0, 0.387),
     'L2_ffn_b1': (0.0, 0.389),
     'L2_ffn_b2': (0.0, 0.1),
     'L3_xattn_bq': (0.0, 0.1),
     'L3_xattn_bk': (0.0, 2.0),
     'L3_xattn_bv': (0.0, 0.1),
     'L3_xattn_bp': (0.0, 0.1),
     'L3_ffn_b1': (0.0, 0.305),
     'L3_ffn_b2': (0.0, 0.1)}
    factors = {'L1_attn_Wq': 7.197,
     'L1_attn_bq': 23.028,
     'L1_attn_Wk': 8.0,
     'L1_attn_bk': 46.925,
     'L1_attn_bv': 3.402,
     'L2_xattn_Wq': 4.31,
     'L2_xattn_Wk': 3.642,
     'L3_attn_W_dq': 8.0,
     'L3_attn_W_uq': 8.0,
     'L3_attn_W_dkv': 2.925,
     'L3_attn_W_uk': 8.0,
     'L3_attn_W_uv': 3.013}
    for name, (base, spread) in spreads.items():
        noise = np.random.default_rng([zlib.crc32(name.encode()), seed]).standard_normal(out[name].shape)
        drawn = base * np.exp(spread * noise) if base else spread * noise
        out[name] = jnp.asarray(drawn.astype(out[name].dtype))
    for name, factor in factors.items():
        out[name] = (out[name] * factor).astype(out[name].dtype)
    return out
```

```python
from contextlib import ExitStack

import numpy as np

import concourse.bass as bass
from concourse import mybir
from concourse.alu_op_type import AluOpType as ALU

F32 = mybir.dt.float32
BF16 = mybir.dt.bfloat16
I32 = mybir.dt.int32
ACT = mybir.ActivationFunctionType
AX = mybir.AxisListType.X
RMAX = bass.bass_isa.ReduceOp.max

P = 128
B, S, D, H = 16, 64, 256, 16
HD = D // H
C = D // P
T = B * S // P
NT = B * S
KEYS = 1601
PAIRS = H // 2
ROWS = 4
KT = -(-KEYS // P)
KCH = [(401 * 0, 401), (401, 400), (801, 400), (1201, 400)]
BIG = 12582912.0
EPS = 1e-5
E_MOE, TOPK = 8, 2
NEG = -3.0e38

BIAS_COLS = ['L0_xattn_bq', 'L0_xattn_bk', 'L0_xattn_bv', 'L1_xattn_bq', 'L1_xattn_bk', 'L1_xattn_bv',
             'L1_attn_bq', 'L1_attn_bqs', 'L1_attn_bk', 'L1_attn_bks', 'L1_attn_bv',
             'L1_ffn_bf', 'L1_ffn_bi', 'L1_ffn_bc', 'L1_ffn_bo', 'L1_ffn_in_c',
             'L2_xattn_bq', 'L2_xattn_bk', 'L2_xattn_bv', 'L2_attn_q_scale', 'L2_attn_k_scale',
             'L3_xattn_bq', 'L3_xattn_bk', 'L3_xattn_bv']
BIAS_ROWS = ['L0_xattn_bo', 'L1_xattn_bo', 'L1_attn_bo', 'L2_xattn_bo', 'L3_xattn_bp']
CONSTS = [('ident', 128), ('pairblk', 32), ('pairmask', 128), ('headmask', 8), ('vmask', 256),
          ('headblk', 128), ('cosine', 64), ('sine', 64), ('before', 64)]


class Queue:

    def __init__(self, engine, sems, in_order):
        self.engine, self.sems, self.in_order = engine, sems, in_order
        self.begin(0)

    def begin(self, which):
        self.sem, self.n, self.seen = self.sems[which], 0, {}

    def wait(self, *tokens):
        for token in tokens:
            if token is None:
                continue
            sem, count = token
            if self.seen.get(sem.name, 0) < count:
                self.engine.wait_ge(sem, count)
                self.seen[sem.name] = count

    def do(self, build, *args, after=(), signal=True, **kw):
        self.wait(*after)
        if self.in_order and self.n:
            self.wait((self.sem, self.n))
        instruction = build(*args, **kw)
        if not signal:
            return None
        instruction.then_inc(self.sem, 1)
        self.n += 1
        return self.sem, self.n

    def dma(self, dst, src, after=()):
        self.wait(*after)
        self.engine.dma_start(dst, src).then_inc(self.sem, 16)
        self.n += 16
        return self.sem, self.n


class Program:
    def __init__(self, nc, dram, stages):
        self.nc, self.dram, self.stages = nc, dram, stages
        names = [('pe', nc.tensor, False), ('dve', nc.vector, True), ('act', nc.scalar, True),
                 ('pool', nc.gpsimd, True), ('sp', nc.sync, False)]
        self.sets = [{n: nc.alloc_semaphore(f"s_{n}_{'ab'[i]}") for n, _, _ in names} for i in range(2)]
        queues = {n: Queue(e, [self.sets[0][n], self.sets[1][n]], o) for n, e, o in names}
        self.pe, self.dve, self.act = queues['pe'], queues['dve'], queues['act']
        self.pool, self.sp = queues['pool'], queues['sp']
        self.queues, self.which = queues, 0
        self.ps = nc.alloc_psum_tensor("ps", [P, 8, 512], F32)
        self.X = nc.alloc_sbuf_tensor("X", [P, T, D], F32)
        self.XNT = nc.alloc_sbuf_tensor("XNT", [P, C, NT], F32)
        self.OT = nc.alloc_sbuf_tensor("OT", [P, C, NT], F32)
        self.cols = nc.alloc_sbuf_tensor("cols", [P, 2 * len(BIAS_COLS)], F32)
        self.cst = {n: nc.alloc_sbuf_tensor(f"c_{n}", [P, w], F32) for n, w in CONSTS}
        self.row = nc.alloc_sbuf_tensor("row", [P, D], F32)
        self.nm = 0

    def phase(self):
        if self.sp.n:
            self.sp.wait((self.sp.sem, self.sp.n))
        self.nc.all_engine_barrier()
        last, self.which = self.which, 1 - self.which
        for name, q in self.queues.items():
            q.engine.sem_clear(self.sets[last][name])
            q.begin(self.which)

    def tile(self, stack, name, shape, dt=F32):
        self.nm += 1
        return stack.enter_context(self.nc.sbuf_tensor(f"{name}_{self.nm}", shape, dt))

    def col(self, name):
        k = 2 * BIAS_COLS.index(name)
        return self.cols[:, k:k + 2]

    def weight(self, stack, name, rows=D, n=D):
        w = self.tile(stack, name, [P, rows // P, n])
        self.sp.dma(w[:], self.dram[name].rearrange("(c p) n -> p c n", p=P))
        return w

    def load_state(self):
        for name, w in CONSTS:
            self.sp.dma(self.cst[name][:], self.dram[f"c_{name}"])
        self.sp.dma(self.cols[:], self.dram["bias_cols"])
        self.sp.dma(self.X[:], self.dram["x"].rearrange("(t p) d -> p t d", p=P))
        self.phase()

    def store_state(self):
        self.phase()
        self.sp.dma(self.dram["out"].rearrange("(t p) d -> p t d", p=P), self.X[:])
        self.sp.wait((self.sp.sem, self.sp.n))

    def layernorm(self, keep=None):
        nc, ps, X = self.nc, self.ps, self.X
        with ExitStack() as st:
            xn = keep if keep is not None else self.tile(st, "xn", [P, T, D])
            stats = self.tile(st, "stats", [P, T, 6])
            mv = self.tile(st, "mv", [P, T, 2])
            rstd = self.tile(st, "rstd", [P, T])
            V = nc.vector
            for t in range(T):
                self.dve.do(V.bn_stats, stats[:, t, :], X[:, t, :])
            for t in range(T):
                self.dve.do(V.bn_aggr, mv[:, t, :], stats[:, t, :])
            t_var = self.dve.do(V.tensor_scalar, rstd[:], mv[:, :, 1], EPS, None, ALU.add)
            t_std = self.act.do(nc.scalar.activation, rstd[:], rstd[:], ACT.Sqrt, after=[t_var])
            self.dve.do(V.reciprocal, rstd[:], rstd[:], after=[t_std])
            free = [None] * 2
            for tp in range(T // 2):
                bank = tp % 2
                for u in range(2):
                    t = 2 * tp + u
                    t_xn = self.dve.do(V.tensor_scalar, xn[:, t, :], X[:, t, :], mv[:, t, 0:1],
                                       rstd[:, t:t + 1], ALU.subtract, ALU.mult)
                    for c in range(C):
                        t_tr = self.pe.do(nc.tensor.transpose,
                                          ps[:, bank, c * 256 + u * P:c * 256 + (u + 1) * P],
                                          xn[:, t, c * P:(c + 1) * P], self.cst['ident'][:],
                                          after=[t_xn, free[bank]])
                free[bank] = self.act.do(nc.scalar.copy, self.XNT[:, :, tp * 256:(tp + 1) * 256],
                                         ps[:, bank, :].rearrange("p (c t) -> p c t", c=C), after=[t_tr])
            self.phase()

    def project(self, dst, w, bias=None, scale=None, src=None, banks=(0, 1), free=None, after=()):
        nc, ps = self.nc, self.ps
        src = self.XNT if src is None else src
        free = free if free is not None else {}
        nin, nout, out = w.shape[1], w.shape[2] // P, None
        k = 0
        for m in range(nout):
            for n in range(NT // 512):
                bank = banks[k % len(banks)]
                k += 1
                for c in range(nin):
                    t_mm = self.pe.do(nc.tensor.matmul, ps[:, bank, :], w[:, c, m * P:(m + 1) * P],
                                      src[:, c, n * 512:(n + 1) * 512], start=(c == 0), stop=(c == nin - 1),
                                      after=[free.get(bank), *after], signal=(c == nin - 1))
                o = dst[:, m, n * 512:(n + 1) * 512]
                if scale is not None:
                    b = bias[:, m:m + 1] if bias is not None else 0.0
                    out = free[bank] = self.dve.do(nc.vector.tensor_scalar, o, ps[:, bank, :], b, scale,
                                                   ALU.add, ALU.mult, after=[t_mm])
                elif bias is not None:
                    out = free[bank] = self.act.do(nc.scalar.activation, o, ps[:, bank, :], ACT.Identity,
                                                   bias=bias[:, m:m + 1], after=[t_mm])
                else:
                    out = free[bank] = self.act.do(nc.scalar.copy, o, ps[:, bank, :], after=[t_mm])
        return out

    def out_project(self, w, bias_row=None):
        nc, ps, X = self.nc, self.ps, self.X
        if bias_row is not None:
            t_row = self.sp.dma(self.row[:], self.dram['bias_rows'][BIAS_ROWS.index(bias_row)]
                                .partition_broadcast(P))
            t_row = self.pool.do(nc.gpsimd.tensor_tensor, X[:], X[:],
                                 self.row[:].unsqueeze(1).broadcast_to([P, T, D]), ALU.add, after=[t_row])
        else:
            t_row = None
        free = [None] * 4
        for t in range(T):
            bank = t % 4
            for c in range(C):
                t_mm = self.pe.do(nc.tensor.matmul, ps[:, bank, 0:D], self.OT[:, c, t * P:(t + 1) * P],
                                  w[:, c, :], start=(c == 0), stop=(c == C - 1), after=[free[bank]],
                                  signal=(c == C - 1))
            free[bank] = self.dve.do(nc.vector.tensor_tensor, X[:, t, :], ps[:, bank, 0:D], X[:, t, :],
                                     ALU.add, after=[t_mm, t_row])
        self.phase()

    def add_transposed(self, src, after=()):
        nc, ps, X = self.nc, self.ps, self.X
        free = [None] * 4
        for tp in range(T // 2):
            bank = tp % 4
            for u in range(2):
                for c in range(C):
                    t = 2 * tp + u
                    t_tr = self.pe.do(nc.tensor.transpose, ps[:, bank, u * D + c * P:u * D + (c + 1) * P],
                                      src[:, c, t * P:(t + 1) * P], self.cst['ident'][:],
                                      after=[free[bank], *after])
            xs = X[:, 2 * tp:2 * tp + 2, :].rearrange("p t d -> p (t d)")
            free[bank] = self.dve.do(nc.vector.tensor_tensor, xs, ps[:, bank, :], xs, ALU.add, after=[t_tr])
        self.phase()

    def cross_attention(self, L, scale, mask=None, wo='Wo', bo='bo'):
        nc, ps = self.nc, self.ps
        pe, dve, act, pool, sp = self.pe, self.dve, self.act, self.pool, self.sp
        V, A, G, M = nc.vector, nc.scalar, nc.gpsimd, nc.tensor
        name = f"L{L}_xattn_"
        st = ExitStack()
        wq, wk, wv = (self.weight(st, name + w) for w in ('Wq', 'Wk', 'Wv'))
        wo = self.weight(st, name + wo)
        self.layernorm()
        ctx_t = [self.tile(st, f"ctx{i}", [P, C, KEYS]) for i in range(2)]
        keys = [self.tile(st, f"keys{i}", [P, C, KEYS]) for i in range(2)]
        vals = [self.tile(st, f"vals{i}", [P, KT, D]) for i in range(2)]
        prob = [self.tile(st, f"prob{i}", [P, ROWS, KEYS]) for i in range(2)]
        prob_t = self.tile(st, "prob_t", [P, 3, 512])
        qp = [self.tile(st, f"qp{i}", [P, C, ROWS, P]) for i in range(2)]
        mx = [self.tile(st, f"mx{i}", [P, ROWS, len(KCH)]) for i in range(2)]
        nmx = [self.tile(st, f"nmx{i}", [P, ROWS]) for i in range(2)]
        den = [self.tile(st, f"den{i}", [P, ROWS]) for i in range(2)]
        rden = self.tile(st, "rden", [P, ROWS])
        diag = self.tile(st, "diag", [P, ROWS, P])
        rmask = self.tile(st, "rmask", [P, P])
        both = self.tile(st, "both", [P, P])
        mk = [self.tile(st, f"mk{i}", [P, KEYS]) for i in range(2)] if mask else None
        keep = [self.tile(st, f"keep{i}", [P, KEYS]) for i in range(2)] if mask == 'fill' else None
        qt = self.XNT

        def load_ctx(b, p, c):
            sp.dma(ctx_t[p][:, c, :], self.dram['ctx_t'][bass.ds(b, 1), c * P:(c + 1) * P, :]
                   .rearrange("o p k -> p (o k)"))

        def load_mask(b, p):
            if mask == 'add':
                src = self.dram['mask_f'][bass.ds(b, 1), :, :].rearrange("o q k -> q (o k)")
                sp.dma(mk[p][0:S, :], src)
                t = sp.dma(mk[p][S:P, :], src)
                pool.do(G.tensor_scalar, mk[p][:], mk[p][:], -1.0e9, None, ALU.mult, after=[t])
            elif mask == 'fill':
                raw = mk[p][:].bitcast(I32)
                src = self.dram['mask_i'][bass.ds(b, 1), :].rearrange("o k -> (o k)").partition_broadcast(P)
                t = sp.dma(raw, src)
                pool.do(G.tensor_scalar, keep[p][:], raw, 0, None, ALU.is_equal, after=[t])
                pool.do(G.tensor_scalar, mk[p][:], keep[p][:], -10000.0, None, ALU.mult)
                pool.do(G.tensor_scalar, keep[p][:], keep[p][:], -1.0, 1.0, ALU.mult, ALU.add)

        def slot(g, p, b, values=True, scores=True, project=True, load=True):
            n = 1 - p
            sg, sp_, sb = (1, p, b) if g == 0 else (0, n, b + 1)
            t = {}
            if load:
                load_ctx(b + 2, p, g)
                if g == 1 and mask:
                    load_mask(b + 2, p)
            if g == 0 and project:
                for c in range(C):
                    for h in range(2):
                        pool.do(G.tensor_tensor, qp[n][:, c, :, h * S:(h + 1) * S],
                                qt[:, c, bass.ds((b + 1) * S, S)].unsqueeze(1).broadcast_to([P, ROWS, S]),
                                self.cst['headmask'][:, h::2].unsqueeze(2).broadcast_to([P, ROWS, S]), ALU.mult)
            if values:
                dve.do(V.reciprocal, rden[:], den[g][:])
                t['rden'] = (dve.sem, dve.n)
                for r in range(ROWS):
                    t['diag'] = pool.do(G.tensor_tensor, diag[:, r, :], self.cst['ident'][:],
                                        rden[:, r:r + 1].broadcast_to([P, P]), ALU.mult, after=[t['rden']])

            s_free = [None] * ROWS

            def score_chunk(k):
                k0, kw = KCH[k]
                for r in range(ROWS):
                    t[('s', r)] = pe.do(M.matmul, ps[:, r, 0:kw], qp[sp_][:, sg, r, :], keys[sp_][:, sg, k0:k0 + kw],
                                        start=True, stop=True, after=[s_free[r]])
                for r in range(ROWS):
                    o = prob[sg][:, r, k0:k0 + kw]
                    if mask:
                        s_free[r] = dve.do(V.tensor_tensor_reduce, o, ps[:, r, 0:kw], mk[sp_][:, k0:k0 + kw],
                                           1.0, NEG, ALU.add, ALU.max, mx[sg][:, r, k:k + 1], after=[t[('s', r)]])
                    else:
                        s_free[r] = dve.do(V.tensor_scalar, o, ps[:, r, 0:kw], 0.0, NEG, ALU.add, ALU.max,
                                           accum_out=mx[sg][:, r, k:k + 1], after=[t[('s', r)]])
                if k == len(KCH) - 1:
                    t['nmx'] = dve.do(V.tensor_reduce, nmx[sg][:], mx[sg][:], AX, ALU.max, negate=True)

            def exponential(r):
                act.do(A.activation, prob[sg][:, r, :], prob[sg][:, r, :], ACT.Exp, bias=nmx[sg][:, r:r + 1],
                       accum_out=den[sg][:, r:r + 1], after=[t['nmx']])

            proj_free = [None]

            def keys_unit(i):
                m, k = i // len(KCH), i % len(KCH)
                k0, kw = KCH[k]
                for c in range(C):
                    t_mm = pe.do(M.matmul, ps[:, 7, 0:kw], wk[:, c, m * P:(m + 1) * P], ctx_t[n][:, c, k0:k0 + kw],
                                 start=(c == 0), stop=(c == C - 1), after=proj_free, signal=(c == C - 1))
                o = keys[n][:, m, k0:k0 + kw]
                t_k = proj_free[0] = act.do(A.activation, o, ps[:, 7, 0:kw], ACT.Identity,
                                            bias=self.col(name + 'bk')[:, m:m + 1], after=[t_mm])
                if mask == 'fill':
                    pool.do(G.tensor_tensor, o, o, keep[n][:, k0:k0 + kw], ALU.mult, after=[t_k])

            def values_unit(i):
                tiles = [x for x in (2 * i, 2 * i + 1) if x < KT]
                w = min(P, KEYS - tiles[-1] * P)
                for u, kt in enumerate(tiles):
                    for c in range(C):
                        t_mm = pe.do(M.matmul, ps[0:w, 7, u * D:(u + 1) * D], ctx_t[n][:, c, kt * P:kt * P + w],
                                     wv[:, c, :], start=(c == 0), stop=(c == C - 1), after=proj_free,
                                     signal=(c == C - 1))
                proj_free[0] = act.do(A.copy, vals[n][0:w, tiles[0]:tiles[-1] + 1, :],
                                      ps[0:w, 7, 0:len(tiles) * D].rearrange("p (t d) -> p t d", d=D), after=[t_mm])

            pt_free = [None] * 2
            sb_free = [None] * 3
            t_sb = [None] * 3

            def transposes(kt):
                w, bank = min(P, KEYS - kt * P), kt % 2
                for r in range(ROWS):
                    t_tr = pe.do(M.transpose, ps[0:w, 4 + bank, r * P:(r + 1) * P],
                                 prob[g][:, r, kt * P:kt * P + w], self.cst['ident'][:],
                                 after=[pt_free[bank]], signal=(r == ROWS - 1))
                q, fn = (act, A.copy) if kt in (0, 1, 2, 3, 4, 5) else (dve, V.tensor_copy)
                t_sb[kt % 3] = pt_free[bank] = q.do(fn, prob_t[0:w, kt % 3, :], ps[0:w, 4 + bank, :],
                                                    after=[t_tr, sb_free[kt % 3]])

            def weighted(kt):
                w = min(P, KEYS - kt * P)
                for r in range(ROWS):
                    t_pv = pe.do(M.matmul, ps[32 * r:32 * r + 32, 6, g * P:(g + 1) * P],
                                 vals[p][0:w, kt, (ROWS * g + r) * 32:(ROWS * g + r + 1) * 32],
                                 prob_t[0:w, kt % 3, r * P:(r + 1) * P], start=(kt == 0), stop=(kt == KT - 1),
                                 after=[t_sb[kt % 3]], signal=(r == ROWS - 1))
                sb_free[kt % 3] = t['pv'] = t_pv

            units = 8 if g == 0 else 7
            unit = keys_unit if g == 0 else values_unit
            done = 0
            for kt in range(KT + 1):
                if values and kt < KT:
                    transposes(kt)
                if scores and kt % 2 == 0 and kt // 2 < len(KCH):
                    score_chunk(kt // 2)
                if project:
                    while done < units and done * KT <= kt * units:
                        unit(done)
                        done += 1
                if scores and 7 <= kt < 7 + ROWS:
                    exponential(kt - 7)
                if values and kt:
                    weighted(kt - 1)
            if values:
                for r in range(ROWS):
                    t_rm = pe.do(M.matmul, ps[32 * r:32 * r + 32, 4, 0:P], self.cst['pairblk'][:], diag[:, r, :],
                                 start=True, stop=True, after=[t['diag'], pt_free[0]], signal=(r == ROWS - 1))
                t_rs = act.do(A.copy, rmask[:], ps[:, 4, 0:P], after=[t_rm])
                dve.do(V.tensor_tensor, both[:], ps[:, 6, g * P:(g + 1) * P], rmask[:], ALU.mult,
                       after=[t['pv'], t_rs])
                dve.do(V.scalar_tensor_tensor, self.OT[:, g, bass.ds(b * S, S)], both[:, 0:S],
                       self.col(name + 'bv')[:, g:g + 1], both[:, S:P], ALU.add, ALU.add)
            self.phase()

        load_ctx(0, 0, 0)
        load_ctx(0, 0, 1)
        if mask:
            load_mask(0, 0)
        qs = self.OT
        self.project(qs, wq, self.col(name + 'bq'), scale)
        self.phase()
        pool.do(G.tensor_copy, qt[:, 0, :], qs[:, 0, :])
        dve.do(V.tensor_copy, qt[:, 1, :], qs[:, 1, :])
        self.phase()
        slot(0, 1, -1, values=False, scores=False)
        slot(1, 1, -1, values=False, load=True)
        with nc.Fori(0, (B - 2) // 2) as i:
            for p in range(2):
                for g in range(2):
                    slot(g, p, i * 2 + p)
        slot(0, 0, B - 2, load=False)
        slot(1, 0, B - 2, load=False)
        slot(0, 1, B - 1, project=False, load=False)
        slot(1, 1, B - 1, scores=False, project=False, load=False)
        self.out_project(wo, name + bo)
        st.close()


    def self_attention(self, L, scale, table):
        nc, ps, cst, XNT, OT = self.nc, self.ps, self.cst, self.XNT, self.OT
        pe, dve, act, pool, sp = self.pe, self.dve, self.act, self.pool, self.sp
        V, A, G, M = nc.vector, nc.scalar, nc.gpsimd, nc.tensor
        name = f"L{L}_attn_"
        st = ExitStack()
        bias = self.tile(st, "table", [P, H * S])
        sp.dma(bias[:], self.dram[table])
        qt = self.tile(st, "qt", [P, C, NT])
        kt = self.tile(st, "kt", [P, C, NT])
        src = XNT
        bv = None
        if L == 3:
            wv, wo, src = self.latent_projections(st, name, qt, kt, scale)
        else:
            w = {n: self.weight(st, name + n) for n in ('Wq', 'Wk', 'Wv', 'Wo')}
            wv, wo = w['Wv'], w['Wo']
            if L == 1:
                w.update({n: self.weight(st, name + n) for n in ('Wqs', 'Wks')})
            self.layernorm()
            if L == 0:
                self.project(qt, w['Wq'], None, scale)
                self.project(kt, w['Wk'], None, banks=(2, 3))
            elif L == 1:
                self.rotated(st, name, w, qt, kt, scale)
                bv = self.col(name + 'bv')
            else:
                self.silu_normed(st, name, w, qt, kt)
            self.phase()
        nsrc = wv.shape[1]
        U = 2
        q2 = [self.tile(st, f"q2{u}", [P, C, P]) for u in range(U)]
        kb = [self.tile(st, f"kb{u}", [P, C, 2, 512]) for u in range(U)]
        xd = [self.tile(st, f"xd{u}", [P, nsrc, 2, 2, S]) for u in range(U)]
        vb = [self.tile(st, f"vb{u}", [P, 2, D]) for u in range(U)]
        pr = [self.tile(st, f"pr{u}", [P, H, S]) for u in range(U)]
        pt = [self.tile(st, f"pt{u}", [P, 2, 512]) for u in range(U)]
        mx = [self.tile(st, f"smx{u}", [P, H]) for u in range(U)]

        def tiles(t0):
            tk = [{} for _ in range(U)]
            for u in range(U):
                at = bass.ds((t0 + u) * P, P)
                tk[u]['q'] = dve.do(V.tensor_copy, q2[u][:], qt[:, :, at])
                for c in range(C):
                    for bb in range(2):
                        kk = kt[:, c, bass.ds((t0 + u) * P + bb * S, S)]
                        q, eng = (pool, G) if c else (dve, V)
                        tk[u]['k', c, bb] = q.do(
                            eng.tensor_tensor, kb[u][:, c, bb, :].rearrange("p (h k) -> p h k", k=S),
                            kk.unsqueeze(1).broadcast_to([P, H // 2, S]),
                            cst['headmask'][:].unsqueeze(2).broadcast_to([P, H // 2, S]), ALU.mult)
                for c in range(nsrc):
                    for bb in range(2):
                        tk[u]['x'] = act.do(A.copy, xd[u][:, c, bb], src[:, c, bass.ds((t0 + u) * P + bb * S, S)]
                                            .unsqueeze(1).broadcast_to([P, 2, S]))
            for u in range(U):
                for c in range(C):
                    for bb in range(2):
                        tk[u]['s', c] = pe.do(M.matmul, ps[bb * S:(bb + 1) * S, 4 * u + c, :],
                                              q2[u][:, c, bb * S:(bb + 1) * S], kb[u][:, c, bb, :], start=True,
                                              stop=True, after=[tk[u]['q'], tk[u]['k', c, bb]])
                for bb in range(2):
                    for c in range(nsrc):
                        tk[u]['v'] = pe.do(M.matmul, ps[:, 4 * u + 2, bb * D:(bb + 1) * D],
                                           xd[u][:, c, bb].rearrange("p r k -> p (r k)"), wv[:, c, :],
                                           start=(c == 0), stop=(c == nsrc - 1), after=[tk[u]['x']])
                if L == 2:
                    tk[u]['v'] = act.do(A.activation, vb[u][:].rearrange("p b d -> p (b d)"), ps[:, 4 * u + 2, :],
                                        ACT.Silu, after=[tk[u]['v']])
            for u in range(U):
                for c in range(C):
                    t_s = dve.do(V.tensor_tensor, pr[u][:, 8 * c:8 * c + 8, :].rearrange("p h k -> p (h k)"),
                                 ps[:, 4 * u + c, :], bias[:, c * 512:(c + 1) * 512], ALU.add,
                                 after=[tk[u]['s', c]])
                t_m = dve.do(V.tensor_reduce, mx[u][:], pr[u][:], AX, ALU.max)
                t_d = dve.do(V.tensor_tensor, pr[u][:], pr[u][:], mx[u][:].unsqueeze(2).broadcast_to([P, H, S]),
                             ALU.subtract)
                tk[u]['e'] = act.do(A.activation, pr[u][:], pr[u][:], ACT.Exp, after=[t_d])
            for u in range(U):
                v = vb[u][:] if L == 2 else ps[:, 4 * u + 2, :].rearrange("p (b d) -> p b d", b=2)
                tk[u]['vb'] = dve.do(V.tensor_tensor, vb[u][:], v,
                                     cst['vmask'][:].unsqueeze(1).broadcast_to([P, 2, D]), ALU.mult,
                                     after=[tk[u]['v']])
                dve.do(V.tensor_reduce, mx[u][:], pr[u][:], AX, ALU.add, after=[tk[u]['e']])
                dve.do(V.reciprocal, mx[u][:], mx[u][:])
                tk[u]['p'] = dve.do(V.tensor_tensor, pr[u][:], pr[u][:],
                                    mx[u][:].unsqueeze(2).broadcast_to([P, H, S]), ALU.mult)
            for u in range(U):
                for half in range(2):
                    for r in range(ROWS):
                        j = 4 * half + r
                        t_tr = pe.do(M.transpose, ps[:, 4 * u + half, r * P:(r + 1) * P],
                                     pr[u][:, 2 * j:2 * j + 2, :].rearrange("p h k -> p (h k)"), cst['ident'][:],
                                     after=[tk[u]['p']])
                    q, fn = (act, A.copy) if half else (dve, V.tensor_copy)
                    tk[u]['pt', half] = q.do(fn, pt[u][:, half, :], ps[:, 4 * u + half, :], after=[t_tr])
            for u in range(U):
                for half in range(2):
                    for bb in range(2):
                        for r in range(ROWS):
                            j = 4 * half + r
                            t_o = pe.do(M.matmul, ps[32 * r:32 * r + 32, 4 * u + 3, half * P + bb * S:half * P + bb * S + S],
                                        vb[u][:, bb, 32 * j:32 * j + 32], pt[u][:, half, r * P + bb * S:r * P + bb * S + S],
                                        start=True, stop=True, after=[tk[u]['pt', half], tk[u]['vb']])
                o, s = OT[:, :, bass.ds((t0 + u) * P, P)], ps[:, 4 * u + 3, 0:256].rearrange("p (c t) -> p c t", c=C)
                if bv is None:
                    dve.do(V.tensor_copy, o, s, after=[t_o])
                else:
                    for c in range(C):
                        dve.do(V.tensor_scalar, OT[:, c, bass.ds((t0 + u) * P, P)], s[:, c], bv[:, c:c + 1], None,
                               ALU.add, after=[t_o])
            self.phase()

        with nc.Fori(0, T // (2 * U)) as i:
            for half in range(2):
                tiles(i * (2 * U) + half * U)
        if wo is not None:
            self.out_project(wo, name + 'bo' if name + 'bo' in BIAS_ROWS else None)
        else:
            self.add_transposed(OT)
        st.close()

    def rotated(self, st, name, w, qt, kt, scale):
        nc, cst = self.nc, self.cst
        swapped = self.tile(st, "swapped", [P, C, NT])
        for x, n, b, s in ((qt, 'Wq', 'bq', scale), (kt, 'Wk', 'bk', 1.0)):
            t1 = self.project(x, w[n], self.col(name + b), s)
            t2 = self.project(swapped, w[n + 's'], self.col(name + b + 's'), s, banks=(2, 3))
            for c in range(C):
                for o, table in ((x, 'cosine'), (swapped, 'sine')):
                    o = o[:, c, :].rearrange("p (b s) -> p b s", s=S)
                    self.dve.do(nc.vector.tensor_tensor, o, o, cst[table][:].unsqueeze(1).broadcast_to([P, B, S]),
                                ALU.mult, after=[t1, t2])
                self.dve.do(nc.vector.tensor_tensor, x[:, c, :], x[:, c, :], swapped[:, c, :], ALU.add)
            self.phase()

    def silu_normed(self, st, name, w, qt, kt):
        nc, ps, cst = self.nc, self.ps, self.cst
        for x, n in ((qt, 'Wq'), (kt, 'Wk')):
            for m in range(C):
                for h in range(2):
                    bank = 2 * m + h
                    for c in range(C):
                        t_mm = self.pe.do(nc.tensor.matmul, ps[:, bank, :], w[n][:, c, m * P:(m + 1) * P],
                                          self.XNT[:, c, h * 512:(h + 1) * 512], start=(c == 0), stop=(c == C - 1))
                    self.act.do(nc.scalar.activation, x[:, m, h * 512:(h + 1) * 512], ps[:, bank, :], ACT.Silu,
                                after=[t_mm])
            self.phase()
        sq = self.tile(st, "sq", [P, 2, 512])
        rad = self.tile(st, "rad", [P, 512])
        free = {}
        for x, n in ((qt, 'q_scale'), (kt, 'k_scale')):
            for m in range(C):
                for h in range(2):
                    o, f = x[:, m, h * 512:(h + 1) * 512], sq[:, h, :]
                    t_sq = self.pool.do(nc.gpsimd.tensor_tensor, f, o, o, ALU.mult, after=[free.get(h)])
                    t_mm = self.pe.do(nc.tensor.matmul, ps[:, h, :], cst['headblk'][:], f, start=True, stop=True,
                                      after=[t_sq])
                    t_r = self.act.do(nc.scalar.activation, f, ps[:, h, :], ACT.Sqrt, after=[t_mm])
                    self.dve.do(nc.vector.tensor_scalar, rad[:], f, 1e-6, None, ALU.add, after=[t_r])
                    self.dve.do(nc.vector.reciprocal, rad[:], rad[:])
                    self.dve.do(nc.vector.tensor_tensor, f, f, rad[:], ALU.mult)
                    free[h] = self.dve.do(nc.vector.scalar_tensor_tensor, o, f, self.col(name + n)[:, m:m + 1], o,
                                          ALU.mult, ALU.mult)
        self.phase()

    def latent_projections(self, st, name, qt, kt, scale):
        nc, ps = self.nc, self.ps
        M, A = nc.tensor, nc.scalar
        w = {n: self.weight(st, name + n, r, m) for n, r, m in
             (('W_dqT', D, P), ('W_dq', P, D), ('W_uqT', P, D), ('W_dkvT', D, P), ('W_uk', D, P), ('W_uv', D, P),
              ('W_oT', D, D))}
        self.layernorm()
        a = self.tile(st, "uq_dq", [P, C, D])
        keff = self.tile(st, "keff", [P, 1, D])
        veff = self.tile(st, "veff", [P, 1, D])
        lat = self.tile(st, "lat", [P, 1, NT])
        ckv = self.tile(st, "ckv", [P, 1, NT])
        for m in range(C):
            t_mm = self.pe.do(M.matmul, ps[:, m, 0:D], w['W_uqT'][:, 0, m * P:(m + 1) * P], w['W_dq'][:, 0, :],
                              start=True, stop=True)
            t_a = self.act.do(A.copy, a[:, m, :], ps[:, m, 0:D], after=[t_mm])
        for c in range(C):
            t_k = self.pe.do(M.matmul, ps[:, 2, 0:D], w['W_uk'][:, c, :], a[:, c, :], start=(c == 0),
                             stop=(c == C - 1), after=[t_a])
        for c in range(C):
            t_v = self.pe.do(M.matmul, ps[:, 3, 0:D], w['W_uv'][:, c, :], w['W_oT'][:, c, :], start=(c == 0),
                             stop=(c == C - 1))
        t_k = self.act.do(A.copy, keff[:, 0, :], ps[:, 2, 0:D], after=[t_k])
        self.act.do(A.copy, veff[:, 0, :], ps[:, 3, 0:D], after=[t_v])
        self.project(lat, w['W_dqT'], banks=(4, 5))
        self.project(ckv, w['W_dkvT'], banks=(6, 7))
        self.phase()
        self.project(qt, w['W_uqT'], None, scale, src=lat)
        self.project(kt, keff, src=ckv, banks=(2, 3))
        self.phase()
        return veff, None, ckv

    def quantize_activation(self, x, tmp):
        nc, V = self.nc, self.nc.vector
        n = x.shape[1]
        st = ExitStack()
        big = self.tile(st, "amax", [P, n])
        one = self.tile(st, "amax1", [P, 4])
        for m in range(n):
            self.dve.do(V.tensor_reduce, big[:, m:m + 1], x[:, m], AX, ALU.max, apply_absolute_value=True)
        t = self.dve.do(V.tensor_reduce, one[:, 0:1], big[:], AX, ALU.max)
        t = self.pool.do(nc.gpsimd.partition_all_reduce, one[:, 1:2], one[:, 0:1], P, RMAX, after=[t])
        self.dve.do(V.tensor_scalar, one[:, 2:3], one[:, 1:2], 1.0 / 32767.0, 1e-12, ALU.mult, ALU.max, after=[t])
        self.dve.do(V.reciprocal, one[:, 3:4], one[:, 2:3])
        for m in range(n):
            self.dve.do(V.tensor_scalar, tmp[:], x[:, m], one[:, 3:4], BIG, ALU.mult, ALU.add)
            self.dve.do(V.tensor_scalar, tmp[:], tmp[:], -BIG, -32768.0, ALU.add, ALU.max)
            self.dve.do(V.tensor_scalar, x[:, m], tmp[:], 32767.0, one[:, 2:3], ALU.min, ALU.mult)
        st.close()

    def quantize_weight(self, w, tmp, sc):
        V, dve = self.nc.vector, self.dve
        wb = w[:].rearrange("p c (b i) -> p (c b) i", i=32)
        tb = tmp[:].rearrange("p c (b i) -> p (c b) i", i=32)
        nb = wb.shape[1]
        spread = lambda s: sc[:, s, :].unsqueeze(2).broadcast_to([P, nb, 32])
        dve.do(V.tensor_reduce, sc[:, 0, :], wb, AX, ALU.max, apply_absolute_value=True)
        dve.do(V.tensor_scalar, sc[:, 0, :], sc[:, 0, :], 1.0 / 7.0, 1e-12, ALU.mult, ALU.max)
        dve.do(V.reciprocal, sc[:, 1, :], sc[:, 0, :])
        dve.do(V.tensor_tensor, tb, wb, spread(1), ALU.mult)
        dve.do(V.tensor_scalar, tb, tb, BIG, -BIG, ALU.add, ALU.add)
        dve.do(V.tensor_scalar, tb, tb, -8.0, 7.0, ALU.max, ALU.min)
        return dve.do(V.tensor_tensor, wb, tb, spread(0), ALU.mult)

    def quantized_ffn(self):
        nc, ps, V, A, M = self.nc, self.ps, self.nc.vector, self.nc.scalar, self.nc.tensor
        F = 768
        NF = F // P
        st = ExitStack()
        inner = ExitStack()
        wg_t = self.tile(st, "wg_t", [P, C, F])
        wu_t = self.tile(st, "wu_t", [P, C, F])
        wd_t = self.tile(st, "wd_t", [P, NF, D])
        raw = [self.weight(inner, "L0_ffn_w_gate", F, D), self.weight(inner, "L0_ffn_w_up", F, D),
               self.weight(inner, "L0_ffn_w_down", D, F)]
        self.layernorm()
        tmp = self.tile(inner, "tmp", [P, NF, D])
        tmp2 = self.tile(inner, "tmp2", [P, C, F])
        sc = self.tile(inner, "sc", [P, 2, NF * D // 32])
        free = [None] * 4
        k = 0
        for w, wt, tm in ((raw[0], wg_t, tmp), (raw[1], wu_t, tmp), (raw[2], wd_t, tmp2)):
            t_w = self.quantize_weight(w, tm, sc)
            for o in range(w.shape[1]):
                for i in range(w.shape[2] // P):
                    bank = k % 4
                    k += 1
                    t_tr = self.pe.do(M.transpose, ps[:, bank, 0:P], w[:, o, i * P:(i + 1) * P],
                                      self.cst['ident'][:], after=[t_w, free[bank]])
                    free[bank] = self.act.do(A.copy, wt[:, i, o * P:(o + 1) * P], ps[:, bank, 0:P], after=[t_tr])
        self.phase()
        inner.close()
        tmp = self.tile(st, "qtmp", [P, NT])
        gate = self.tile(st, "gate", [P, NF, NT])
        up = self.tile(st, "up", [P, NF, NT])
        xq = self.OT
        self.dve.do(V.tensor_copy, xq[:, 0], self.XNT[:, 0])
        self.dve.do(V.tensor_copy, xq[:, 1], self.XNT[:, 1])
        self.quantize_activation(xq, tmp)
        self.phase()
        self.project(up, wu_t, src=xq, banks=(0, 1, 2, 3))
        self.project(gate, wg_t, src=xq, banks=(4, 5, 6, 7))
        self.phase()
        self.quantize_activation(up, tmp)
        self.quantize_activation(gate, tmp)
        for m in range(NF):
            t = self.act.do(A.activation, tmp[:], gate[:, m], ACT.Sigmoid, after=[(self.dve.sem, self.dve.n)])
            self.dve.do(V.tensor_scalar, tmp[:], tmp[:], 65536.0, BIG, ALU.mult, ALU.add, after=[t])
            self.dve.do(V.tensor_scalar, tmp[:], tmp[:], -BIG, 65535.0, ALU.add, ALU.min)
            self.dve.do(V.tensor_scalar, tmp[:], tmp[:], 0.0, 1.0 / 65536.0, ALU.max, ALU.mult)
            self.dve.do(V.tensor_tensor, gate[:, m], gate[:, m], tmp[:], ALU.mult)
        self.quantize_activation(gate, tmp)
        for m in range(NF):
            self.dve.do(V.tensor_tensor, gate[:, m], gate[:, m], up[:, m], ALU.mult)
        self.quantize_activation(gate, tmp)
        self.phase()
        free = [None] * 4
        for t in range(T):
            bank = t % 4
            for f in range(NF):
                t_mm = self.pe.do(M.matmul, ps[:, bank, 0:D], gate[:, f, t * P:(t + 1) * P], wd_t[:, f, :],
                                  start=(f == 0), stop=(f == NF - 1), after=[free[bank]], signal=(f == NF - 1))
            free[bank] = self.dve.do(V.tensor_tensor, self.X[:, t, :], ps[:, bank, 0:D], self.X[:, t, :], ALU.add,
                                     after=[t_mm])
        self.phase()
        st.close()

    def recurrent_ffn(self):
        nc, ps, V, A, M = self.nc, self.ps, self.nc.vector, self.nc.scalar, self.nc.tensor
        st = ExitStack()
        wx = [self.weight(st, 'L1_ffn_' + n) for n in ('wf', 'wi', 'wc')]
        wc = [self.weight(st, 'L1_ffn_' + n) for n in ('uf', 'ui', 'uc')]
        wo, uo = self.weight(st, 'L1_ffn_wo'), self.weight(st, 'L1_ffn_uo')
        self.layernorm()
        pre = self.tile(st, "pre", [P, 3, C, NT])
        out = self.tile(st, "out", [P, C, NT])
        cell = self.tile(st, "cell", [P, C, S])
        gates = self.tile(st, "gates", [P, 3, C, S])
        for k, b in enumerate(('bf', 'bi', 'bc')):
            self.project(pre[:, k], wx[k], self.col('L1_ffn_' + b), banks=(2 * k, 2 * k + 1))
        self.project(out, wo, self.col('L1_ffn_bo'), banks=(6, 7))
        self.dve.do(V.tensor_copy, cell[:], self.col('L1_ffn_in_c').unsqueeze(2).broadcast_to([P, C, S]))
        self.phase()

        def step(t):
            at = bass.ds(t * S, S)
            for k in range(3):
                for m in range(C):
                    for c in range(C):
                        t_mm = self.pe.do(M.matmul, ps[:, k, m * S:(m + 1) * S], wc[k][:, c, m * P:(m + 1) * P],
                                          cell[:, c, :], start=(c == 0), stop=(c == C - 1), signal=(c == C - 1))
                t_g = self.dve.do(V.tensor_tensor, gates[:, k], ps[:, k, 0:C * S].rearrange("p (c s) -> p c s", c=C),
                                  pre[:, k, :, at], ALU.add, after=[t_mm])
                t_a = self.act.do(A.activation, gates[:, k], gates[:, k], ACT.Tanh if k == 2 else ACT.Sigmoid,
                                  after=[t_g])
                if k == 0:
                    t_f = t_a
            self.dve.do(V.tensor_tensor, cell[:], cell[:], gates[:, 0], ALU.mult, after=[t_f, t_mm])
            self.dve.do(V.tensor_tensor, gates[:, 1], gates[:, 1], gates[:, 2], ALU.mult, after=[t_a])
            self.dve.do(V.tensor_tensor, cell[:], cell[:], gates[:, 1], ALU.add)
            self.phase()

        with nc.Fori(0, B // 2) as i:
            step(i * 2)
            step(i * 2 + 1)
        for m in range(C):
            for c in range(C):
                t_mm = self.pe.do(M.matmul, ps[:, 0, m * S:(m + 1) * S], uo[:, c, m * P:(m + 1) * P], cell[:, c, :],
                                  start=(c == 0), stop=(c == C - 1))
        t_u = self.act.do(A.copy, gates[:, 0], ps[:, 0, 0:C * S].rearrange("p (c s) -> p c s", c=C), after=[t_mm])
        for c in range(C):
            o = out[:, c, :].rearrange("p (b s) -> p b s", s=S)
            t_o = self.dve.do(V.tensor_tensor, o, o, gates[:, 0, c, :].unsqueeze(1).broadcast_to([P, B, S]), ALU.add,
                              after=[t_u])
            t_h = self.act.do(A.activation, out[:, c, :], out[:, c, :], ACT.Tanh, after=[t_o])
        self.add_transposed(out, after=[t_h])
        st.close()

    def expert_weights(self, st, logits):
        nc, V, cst, dve = self.nc, self.nc.vector, self.cst, self.dve
        n = E_MOE
        mine = lambda t: logits[:, t, :].unsqueeze(2).broadcast_to([P, n, n])
        others = lambda t: logits[:, t, :].unsqueeze(1).broadcast_to([P, n, n])
        rank = self.tile(st, "rank", [P, T, n])
        larger = self.tile(st, "larger", [P, n, n])
        equal = self.tile(st, "equal", [P, n, n])
        top = self.tile(st, "top", [P, T])
        for t in range(T):
            dve.do(V.tensor_tensor, larger[:], others(t), mine(t), ALU.is_gt)
            dve.do(V.tensor_tensor, equal[:], others(t), mine(t), ALU.is_equal)
            dve.do(V.tensor_tensor, equal[:], equal[:], cst['before'][:].rearrange("p (a b) -> p a b", a=n), ALU.mult)
            dve.do(V.tensor_tensor, larger[:], larger[:], equal[:], ALU.add)
            dve.do(V.tensor_reduce, rank[:, t, :], larger[:], AX, ALU.add)
        over = lambda a: a[:].unsqueeze(2).broadcast_to([P, T, n])
        dve.do(V.tensor_scalar, rank[:], rank[:], TOPK - 0.5, None, ALU.is_lt)
        dve.do(V.tensor_reduce, top[:], logits[:], AX, ALU.max)
        t = dve.do(V.tensor_tensor, logits[:], logits[:], over(top), ALU.subtract)
        t = self.act.do(nc.scalar.activation, logits[:], logits[:], ACT.Exp, after=[t])
        dve.do(V.tensor_tensor, logits[:], logits[:], rank[:], ALU.mult, after=[t])
        dve.do(V.tensor_reduce, top[:], logits[:], AX, ALU.add)
        dve.do(V.reciprocal, top[:], top[:])
        return dve.do(V.tensor_tensor, logits[:], logits[:], over(top), ALU.mult)

    def expert_ffn(self, L):
        nc, ps, V, A, M, G = self.nc, self.ps, self.nc.vector, self.nc.scalar, self.nc.tensor, self.nc.gpsimd
        pe, dve, act, pool, sp, cst = self.pe, self.dve, self.act, self.pool, self.sp, self.cst
        name, X, XNT = f"L{L}_ffn_", self.X, self.XNT
        gated = L == 2
        F, FT = (684, 114) if gated else (512, P)
        NF = F // FT
        n = E_MOE
        st = ExitStack()
        router = self.weight(st, name + ('centroidT' if gated else 'routerT'), D, n)
        bout = self.tile(st, "bout", [n, D])
        sp.dma(bout[:], self.dram[name + 'bout'])
        w1 = [self.tile(st, f"w1{i}", [P, C, F]) for i in range(2)]
        w2 = [self.tile(st, f"w2{i}", [P, C, F]) for i in range(2)] if gated else None
        wout = [self.tile(st, f"wout{i}", [FT, NF, D]) for i in range(2)]
        b1 = [self.tile(st, f"b1{i}", [FT, NF]) for i in range(2)]
        b2 = [self.tile(st, f"b2{i}", [FT, NF]) for i in range(2)] if gated else None

        def load_expert(e, p):
            def get(dst, key, pattern, **kw):
                sp.dma(dst, self.dram[name + key][bass.ds(e, 1)].rearrange(pattern, **kw))
            get(w1[p][:], 'w1', "o (c p) f -> p (o c) f", p=P)
            get(wout[p][:], 'wout', "o (m p) d -> p (o m) d", p=FT)
            get(b1[p][:], 'b1', "o p m -> p (o m)")
            if gated:
                get(w2[p][:], 'w2', "o (c p) f -> p (o c) f", p=P)
                get(b2[p][:], 'b2', "o p m -> p (o m)")

        load_expert(0, 0)
        self.layernorm()
        we = self.tile(st, "we", [P, T, n])
        wet = self.tile(st, "wet", [n, NT])
        hid = self.tile(st, "hid", [FT, NF, NT])
        act_o = [self.tile(st, f"act{i}", [FT, 512]) for i in range(2)]
        for t in range(T):
            for c in range(C):
                t_r = pe.do(M.matmul, ps[:, 0, t * n:(t + 1) * n], XNT[:, c, t * P:(t + 1) * P], router[:, c, :],
                            start=(c == 0), stop=(c == C - 1))
        if gated:
            sq = self.tile(st, "sq", [P, C, NT])
            csq = self.tile(st, "csq", [P, C, n])
            ones = self.tile(st, "ones", [P, P])
            dve.do(V.memset, ones[:], 1.0)
            dve.do(V.tensor_tensor, csq[:], router[:], router[:], ALU.mult)
            t_sq = dve.do(V.tensor_tensor, sq[:], XNT[:], XNT[:], ALU.mult)
            for t in range(T):
                for c in range(C):
                    pe.do(M.matmul, ps[:, 1, t * n:(t + 1) * n], sq[:, c, t * P:(t + 1) * P], ones[:, 0:n],
                          start=(c == 0), stop=False, after=[t_sq])
                for c in range(C):
                    t_d = pe.do(M.matmul, ps[:, 1, t * n:(t + 1) * n], ones[:], csq[:, c, :], start=False,
                                stop=(c == C - 1))
            w = we[:].rearrange("p t e -> p (t e)")
            t_c = act.do(A.copy, w, ps[:, 1, 0:T * n], after=[t_d])
            dve.do(V.scalar_tensor_tensor, w, ps[:, 0, 0:T * n], -2.0, w, ALU.mult, ALU.add, after=[t_c, t_r])
            t_d = dve.do(V.tensor_scalar, w, w, 1e-12, None, ALU.max)
            t_w = act.do(A.activation, w, w, ACT.Sqrt, after=[t_d])
        else:
            t_w = act.do(A.copy, we[:].rearrange("p t e -> p (t e)"), ps[:, 0, 0:T * n], after=[t_r])
        dve.wait(t_w)
        t_we = self.expert_weights(st, we)
        free = [None] * 2
        for t in range(T):
            bank = 2 + t % 2
            t_tr = pe.do(M.transpose, ps[0:n, bank, 0:P], we[:, t, :], cst['ident'][:], after=[t_we, free[t % 2]])
            t_c = act.do(A.copy, wet[:, t * P:(t + 1) * P], ps[0:n, bank, 0:P], after=[t_tr])
            t_b = pe.do(M.matmul, ps[:, bank, 256:512], wet[:, t * P:(t + 1) * P], bout[:], start=True, stop=True,
                        after=[t_c])
            free[t % 2] = dve.do(V.tensor_tensor, X[:, t, :], ps[:, bank, 256:512], X[:, t, :], ALU.add, after=[t_b])
        self.phase()

        def expert(e, p, load=True):
            if load:
                load_expert(e + 1, 1 - p)
            free, af, k, t_h = {}, [None] * 2, 0, {}
            for h in range(2):
                for m in range(NF):
                    toks = slice(h * 512, (h + 1) * 512)
                    bank, ms, i = 2 * (k % 2), slice(m * FT, (m + 1) * FT), k % 2
                    k += 1
                    for c in range(C):
                        t1 = pe.do(M.matmul, ps[0:FT, bank, :], w1[p][:, c, ms], XNT[:, c, toks], start=(c == 0),
                                   stop=(c == C - 1), after=[free.get(bank)], signal=(c == C - 1))
                    if gated:
                        for c in range(C):
                            t2 = pe.do(M.matmul, ps[0:FT, bank + 1, :], w2[p][:, c, ms], XNT[:, c, toks],
                                       start=(c == 0), stop=(c == C - 1), after=[free.get(bank + 1)],
                                       signal=(c == C - 1))
                        free[bank] = act.do(A.activation, act_o[i][:], ps[0:FT, bank, :], ACT.Silu,
                                            bias=b1[p][:, m:m + 1], after=[t1, af[i]])
                        t_h[h] = af[i] = free[bank + 1] = dve.do(
                            V.scalar_tensor_tensor, hid[:, m, toks], ps[0:FT, bank + 1, :], b2[p][:, m:m + 1],
                            act_o[i][:], ALU.add, ALU.mult, after=[t2, free[bank]])
                    else:
                        t_h[h] = free[bank] = act.do(A.activation, hid[:, m, toks], ps[0:FT, bank, :], ACT.Gelu,
                                                     bias=b1[p][:, m:m + 1], after=[t1])
            for t in range(T):
                bank = 4 + t % 4
                for m in range(NF):
                    t_y = pe.do(M.matmul, ps[:, bank, 0:D], hid[:, m, t * P:(t + 1) * P], wout[p][:, m, :],
                                start=(m == 0), stop=(m == NF - 1), after=[free.get(bank), t_h[t // 4]],
                                signal=(m == NF - 1))
                free[bank] = dve.do(V.scalar_tensor_tensor, X[:, t, :], ps[:, bank, 0:D], we_col(t, e, p),
                                    X[:, t, :], ALU.mult, ALU.add, after=[t_y])
            self.phase()

        now = [self.tile(st, f"now{i}", [P, T]) for i in range(2)]

        def we_col(t, e, p):
            return now[p][:, t:t + 1]

        def pick(e, p):
            dve.do(V.tensor_copy, now[p][:], we[:, :, bass.ds(e, 1)].rearrange("p t o -> p (t o)"))

        with nc.Fori(0, (n - 2) // 2) as i:
            for p in range(2):
                pick(i * 2 + p, p)
                expert(i * 2 + p, p)
        pick(n - 2, 0)
        expert(n - 2, 0)
        pick(n - 1, 1)
        expert(n - 1, 1, load=False)
        st.close()


def constants():
    p = np.arange(P)
    f = np.arange(D)
    out = {'ident': np.eye(P)}
    out['pairblk'] = (p[:, None] // S == np.arange(32)[None] // HD)
    out['pairmask'] = ((p[:, None] % 32) // HD == np.arange(P)[None] // S)
    out['headmask'] = (p[:, None] // HD == np.arange(H // 2)[None])
    out['vmask'] = (p[:, None] // S == (f[None] // HD) % 2)
    out['headblk'] = (p[:, None] // HD == p[None] // HD)
    d = p % HD
    freq = np.exp(-(np.float32(2 * (d // 2)) / np.float32(HD)) * np.log(np.float32(10000.0)), dtype=np.float32)
    angle = (np.arange(S, dtype=np.float32)[None] * freq[:, None]).astype(np.float32)
    out['cosine'] = np.cos(angle)
    out['sine'] = np.sin(angle) * np.where(d % 2 == 0, -1.0, 1.0)[:, None]
    e = np.arange(E_MOE)
    out['before'] = np.tile((e[None] < e[:, None]).reshape(1, -1), (P, 1))
    return {n: np.ascontiguousarray(out[n], np.float32) for n, _ in CONSTS}


def score_biases():
    q = (np.arange(P) % S)[:, None, None]
    h = np.arange(H)[None, :, None]
    k = np.arange(S)[None, None, :]
    slopes = (2.0 ** (-8.0 / H * (h + 1.0))).astype(np.float32)
    alibi = np.where(k > q, NEG, slopes * (k - q).astype(np.float32))
    causal = np.where(k > q, NEG, 0.0) + 0 * h
    return [np.ascontiguousarray(a.reshape(P, H * S), np.float32) for a in (alibi, causal)]


def lay_out(inp):
    a = {k: np.asarray(v) for k, v in inp.items()}
    cols = dict(a)
    swap = np.arange(D).reshape(-1, 2)[:, ::-1].reshape(-1)
    group = (np.arange(D) // HD // 4) * HD + np.arange(D) % HD
    cols['L1_attn_bqs'] = a['L1_attn_bq'][swap]
    for n in ('bk', 'bv'):
        cols[f'L1_attn_{n}'] = a[f'L1_attn_{n}'][group]
    cols['L1_attn_bks'] = a['L1_attn_bk'][group][swap]
    for n in ('q_scale', 'k_scale'):
        cols[f'L2_attn_{n}'] = np.repeat(a[f'L2_attn_{n}'], HD)
    out = {'x': a['x'].reshape(NT, D)}
    out['ctx_t'] = a['ctx_1024'].transpose(0, 2, 1)
    out['mask_f'] = a['mask_Bx1xSxS2_ff0'][:, 0]
    out['mask_i'] = a['mask_Bx1x1xS2_if1'][:, 0, 0]
    out['bias_cols'] = np.concatenate([cols[n].reshape(C, P).T for n in BIAS_COLS], axis=1)
    out['bias_rows'] = np.stack([a[n] for n in BIAS_ROWS])
    for L in (0, 1, 2, 3):
        for n in ('Wq', 'Wk', 'Wv', 'Wo' if L < 3 else 'Wp'):
            w = a[f'L{L}_xattn_{n}']
            out[f'L{L}_xattn_{n}'] = w.T if L == 1 else w
    w_in = a['L0_attn_w_in'].T
    for i, n in enumerate(('Wq', 'Wk', 'Wv')):
        out[f'L0_attn_{n}'] = w_in[:, i * D:(i + 1) * D]
        out[f'L2_attn_{n}'] = a[f'L2_attn_{n}'].T
    out['L0_attn_Wo'] = a['L0_attn_w_out'].T
    out['L2_attn_Wo'] = a['L2_attn_Wo'].T
    out['L1_attn_Wq'], out['L1_attn_Wqs'] = a['L1_attn_Wq'], a['L1_attn_Wq'][:, swap]
    out['L1_attn_Wk'], out['L1_attn_Wks'] = a['L1_attn_Wk'][:, group], a['L1_attn_Wk'][:, group][:, swap]
    out['L1_attn_Wv'], out['L1_attn_Wo'] = a['L1_attn_Wv'][:, group], a['L1_attn_Wo']
    for n in ('w_gate', 'w_up', 'w_down'):
        out[f'L0_ffn_{n}'] = a[f'L0_ffn_{n}']
    for n in ('wf', 'wi', 'wc', 'wo', 'uf', 'ui', 'uc', 'uo'):
        out[f'L1_ffn_{n}'] = a[f'L1_ffn_{n}'].T
    for n in ('W_dq', 'W_uk', 'W_uv'):
        out[f'L3_attn_{n}'] = a[f'L3_attn_{n}']
    for n in ('W_dq', 'W_uq', 'W_dkv', 'W_o'):
        out[f'L3_attn_{n}T'] = a[f'L3_attn_{n}'].T
    out['L2_ffn_centroidT'] = a['L2_ffn_centroid'].T
    out['L2_ffn_w1'], out['L2_ffn_w2'], out['L2_ffn_wout'] = a['L2_ffn_Wg'], a['L2_ffn_W1'], a['L2_ffn_W2']
    for n, m in (('b1', 'bg'), ('b2', 'b1')):
        out[f'L2_ffn_{n}'] = a[f'L2_ffn_{m}'].reshape(E_MOE, 6, 114).transpose(0, 2, 1)
    out['L2_ffn_bout'] = a['L2_ffn_b2']
    out['L3_ffn_routerT'] = a['L3_ffn_router_w'].T
    out['L3_ffn_w1'] = a['L3_ffn_w1'].transpose(0, 2, 1)
    out['L3_ffn_b1'] = a['L3_ffn_b1'].reshape(E_MOE, 4, P).transpose(0, 2, 1)
    out['L3_ffn_wout'] = a['L3_ffn_w2'].transpose(0, 2, 1)
    out['L3_ffn_bout'] = a['L3_ffn_b2']
    for n, v in constants().items():
        out[f'c_{n}'] = v
    out['c_alibi'], out['c_causal'] = score_biases()
    return {k: np.ascontiguousarray(v) for k, v in out.items()}


def build(nc, dram, stages=range(12)):
    pr = Program(nc, dram, stages)
    pr.load_state()
    steps = [lambda: pr.cross_attention(0, 1.0 / D ** 0.5, 'add'),
             lambda: pr.self_attention(0, HD ** -0.5, 'c_alibi'),
             lambda: pr.quantized_ffn(),
             lambda: pr.cross_attention(1, HD ** -0.5),
             lambda: pr.self_attention(1, HD ** -0.5, 'c_causal'),
             lambda: pr.recurrent_ffn(),
             lambda: pr.cross_attention(2, 1.0, 'fill'),
             lambda: pr.self_attention(2, 1.0, 'c_causal'),
             lambda: pr.expert_ffn(2),
             lambda: pr.cross_attention(3, HD ** -0.5, wo='Wp', bo='bp'),
             lambda: pr.self_attention(3, HD ** -0.5, 'c_causal'),
             lambda: pr.expert_ffn(3)]
    for s in stages:
        steps[s]()
    pr.store_state()


def kernel(**inputs):
    import concourse.bacc as bacc
    from concourse.bass_utils import run_bass_kernel_spmd

    nc = bacc.Bacc("TRN2", target_bir_lowering=False, num_devices=1)
    arrays = lay_out(inputs)
    dram = {n: nc.dram_tensor(f"in_{n}", a.shape, mybir.dt.from_np(a.dtype), kind="ExternalInput").ap()
            for n, a in arrays.items()}
    dram['out'] = nc.dram_tensor("out", (NT, D), F32, kind="ExternalOutput").ap()
    build(nc, dram)
    r = run_bass_kernel_spmd(nc, [{f"in_{n}": a for n, a in arrays.items()}], core_ids=[0])
    return r.results[0]["out"].reshape(B, S, D)
```

```python
from contextlib import ExitStack

import numpy as np

import concourse.bass as bass
from concourse import mybir
from concourse.alu_op_type import AluOpType as ALU

F32 = mybir.dt.float32
F32R = mybir.dt.float32r
I32 = mybir.dt.int32
ACT = mybir.ActivationFunctionType
AX = mybir.AxisListType.X
RMAX = bass.bass_isa.ReduceOp.max

P = 128
B, S, D, H = 16, 64, 256, 16
HD = D // H
C = D // P
T = B * S // P
NT = B * S
KEYS = 1601
PAIRS = H // 2
ROWS = 4
KT = -(-KEYS // P)
KEYS2 = KEYS + 1
KCH = [(0, 402), (402, 400), (802, 400), (1202, 400)]
BIG = 12582912.0
EPS = 1e-5
E_MOE, TOPK = 8, 2
NEG = -3.0e38

BIAS_COLS = ['L0_xattn_bq', 'L0_xattn_bk', 'L0_xattn_bv', 'L1_xattn_bq', 'L1_xattn_bk', 'L1_xattn_bv',
             'L1_attn_bq', 'L1_attn_bqs', 'L1_attn_bk', 'L1_attn_bks', 'L1_attn_bv',
             'L1_ffn_bf', 'L1_ffn_bi', 'L1_ffn_bc', 'L1_ffn_bo', 'L1_ffn_in_c',
             'L2_xattn_bq', 'L2_xattn_bk', 'L2_xattn_bv', 'L2_attn_q_scale', 'L2_attn_k_scale',
             'L3_xattn_bq', 'L3_xattn_bk', 'L3_xattn_bv']
BIAS_ROWS = ['L0_xattn_bo', 'L1_xattn_bo', 'L1_attn_bo', 'L2_xattn_bo', 'L3_xattn_bp']
CONSTS = [('ident', 128), ('pairblk', 32), ('pairmask', 2), ('headmask', 8), ('cosine', 64), ('sine', 64), ('before', 64)]

LOW_AT = (1, 2, 3, 4)
SCORES_AT = {5: [(0, (0, 1))], 6: [(0, (2, 3))], 7: [(1, (0, 1))], 8: [(1, (2, 3))], 10: [(2, (0, 1))],
             11: [(2, (2, 3))], 13: [(3, (0, 1, 2, 3))]}
ECH = [(0, 3 * P), (3 * P, 8 * P), (8 * P, KEYS)]


class Queue:

    def __init__(self, engine, sems, in_order):
        self.engine, self.sems, self.in_order = engine, sems, in_order
        self.begin(0)

    def begin(self, which):
        self.sem, self.n, self.seen = self.sems[which], 0, {}

    def wait(self, *tokens):
        for token in tokens:
            if token is None:
                continue
            sem, count = token
            if self.seen.get(sem.name, 0) < count:
                self.engine.wait_ge(sem, count)
                self.seen[sem.name] = count

    def do(self, build, *args, after=(), signal=True, alone=False, **kw):
        self.wait(*after)
        if self.in_order and self.n and not alone:
            self.wait((self.sem, self.n))
        instruction = build(*args, **kw)
        if not signal:
            return None
        instruction.then_inc(self.sem, 1)
        self.n += 1
        return self.sem, self.n

    def dma(self, dst, src, after=()):
        self.wait(*after)
        self.engine.dma_start(dst, src).then_inc(self.sem, 16)
        self.n += 16
        return self.sem, self.n


class Program:
    def __init__(self, nc, dram, stages):
        self.nc, self.dram, self.stages = nc, dram, stages
        names = [('pe', nc.tensor, False), ('dve', nc.vector, True), ('act', nc.scalar, True),
                 ('pool', nc.gpsimd, True), ('sp', nc.sync, False), ('sp_early', nc.sync, False)]
        self.sets = [{n: nc.alloc_semaphore(f"s_{n}_{'ab'[i]}") for n, _, _ in names} for i in range(2)]
        queues = {n: Queue(e, [self.sets[0][n], self.sets[1][n]], o) for n, e, o in names}
        self.pe, self.dve, self.act = queues['pe'], queues['dve'], queues['act']
        self.pool, self.sp = queues['pool'], queues['sp']
        self.sp_early = queues['sp_early']
        self.queues, self.which = queues, 0
        self.ps = nc.alloc_psum_tensor("ps", [P, 8, 512], F32)
        self.X = nc.alloc_sbuf_tensor("X", [P, T, D], F32)
        self.XNT = nc.alloc_sbuf_tensor("XNT", [P, C, NT], F32)
        self.cols = nc.alloc_sbuf_tensor("cols", [P, 2 * len(BIAS_COLS)], F32)
        self.cst = {n: nc.alloc_sbuf_tensor(f"c_{n}", [P, w], F32) for n, w in CONSTS}
        self.stats = nc.alloc_sbuf_tensor("stats", [P, T, 6], F32)
        self.mv = nc.alloc_sbuf_tensor("mv", [P, T, 2], F32)
        self.rstd = nc.alloc_sbuf_tensor("rstd", [P, T], F32)
        self.row = nc.alloc_sbuf_tensor("row", [P, D], F32)
        self.nm = 0

    def phase(self):
        for q in (self.sp, self.sp_early):
            if q.n:
                q.wait((q.sem, q.n))
        self.nc.all_engine_barrier()
        last, self.which = self.which, 1 - self.which
        for name, q in self.queues.items():
            q.engine.sem_clear(self.sets[last][name])
            q.begin(self.which)

    def tile(self, stack, name, shape, dt=F32):
        self.nm += 1
        return stack.enter_context(self.nc.sbuf_tensor(f"{name}_{self.nm}", shape, dt))

    def col(self, name):
        k = 2 * BIAS_COLS.index(name)
        return self.cols[:, k:k + 2]

    def weight(self, stack, name, rows=D, n=D):
        w = self.tile(stack, name, [P, rows // P, n])
        self.sp.dma(w[:], self.dram[name].rearrange("(c p) n -> p c n", p=P))
        return w

    def load_state(self):
        for name, w in CONSTS:
            self.sp.dma(self.cst[name][:], self.dram[f"c_{name}"])
        self.sp.dma(self.cols[:], self.dram["bias_cols"])
        t_x = self.sp.dma(self.X[:], self.dram["x"].rearrange("(t p) d -> p t d", p=P))
        for t in range(T):
            self.take_stats(t, after=[t_x])
        self.phase()

    def store_state(self):
        self.phase()
        self.sp.dma(self.dram["out"].rearrange("(t p) d -> p t d", p=P), self.X[:])
        self.sp.wait((self.sp.sem, self.sp.n))

    def take_stats(self, t, after=()):
        self.dve.do(self.nc.vector.bn_stats, self.stats[:, t, :], self.X[:, t, :], after=after, alone=True)

    def layernorm(self, st=None):
        nc, ps, X, V, mv, rstd = self.nc, self.ps, self.X, self.nc.vector, self.mv, self.rstd
        with ExitStack() as own:
            xn = self.tile(st or own, "xn", [P, T, D])
            for t in range(T):
                t_mv = self.dve.do(V.bn_aggr, mv[:, t, :], self.stats[:, t, :], alone=True)
            t_var = self.dve.do(V.tensor_scalar, rstd[:], mv[:, :, 1], EPS, None, ALU.add)
            t_std = self.act.do(nc.scalar.activation, rstd[:], rstd[:], ACT.Sqrt, after=[t_var])
            t_r = self.dve.do(V.reciprocal, rstd[:], rstd[:], after=[t_std])
            free = [None] * 2
            for tp in range(T // 2):
                bank = 6 + tp % 2
                for u in range(2):
                    t = 2 * tp + u
                    t_xn = self.dve.do(V.tensor_scalar, xn[:, t, :], X[:, t, :], mv[:, t, 0:1],
                                       rstd[:, t:t + 1], ALU.subtract, ALU.mult, after=[t_r], alone=True)
                    for c in range(C):
                        t_tr = self.pe.do(nc.tensor.transpose,
                                          ps[:, bank, c * 256 + u * P:c * 256 + (u + 1) * P],
                                          xn[:, t, c * P:(c + 1) * P], self.cst['ident'][:],
                                          after=[t_xn, free[tp % 2]])
                free[tp % 2] = self.act.do(nc.scalar.copy, self.XNT[:, :, tp * 256:(tp + 1) * 256],
                                           ps[:, bank, :].rearrange("p (c t) -> p c t", c=C), after=[t_tr],
                                           alone=True)
            if st is None:
                self.phase()
            return free[(T // 2 - 1) % 2]

    def project(self, dst, w, bias=None, scale=None, src=None, banks=(0, 1), free=None, after=()):
        nc, ps = self.nc, self.ps
        src = self.XNT if src is None else src
        free = free if free is not None else {}
        nin, nout, out = w.shape[1], w.shape[2] // P, None
        k = 0
        for m in range(nout):
            for n in range(NT // 512):
                bank = banks[k % len(banks)]
                k += 1
                for c in range(nin):
                    t_mm = self.pe.do(nc.tensor.matmul, ps[:, bank, :], w[:, c, m * P:(m + 1) * P],
                                      src[:, c, n * 512:(n + 1) * 512], start=(c == 0), stop=(c == nin - 1),
                                      after=[free.get(bank), *after], signal=(c == nin - 1))
                o = dst[:, m, n * 512:(n + 1) * 512]
                if scale is not None:
                    b = bias[:, m:m + 1] if bias is not None else 0.0
                    out = free[bank] = self.dve.do(nc.vector.tensor_scalar, o, ps[:, bank, :], b, scale,
                                                   ALU.add, ALU.mult, after=[t_mm], alone=True)
                elif bias is not None:
                    out = free[bank] = self.act.do(nc.scalar.activation, o, ps[:, bank, :], ACT.Identity,
                                                   bias=bias[:, m:m + 1], after=[t_mm], alone=True)
                else:
                    out = free[bank] = self.act.do(nc.scalar.copy, o, ps[:, bank, :], after=[t_mm], alone=True)
        return out

    def add_bias_row(self, name):
        t_row = self.sp.dma(self.row[:], self.dram['bias_rows'][BIAS_ROWS.index(name)].partition_broadcast(P))
        self.pool.do(self.nc.gpsimd.tensor_tensor, self.X[:], self.X[:],
                     self.row[:].unsqueeze(1).broadcast_to([P, T, D]), ALU.add, after=[t_row])

    def out_project(self, src, w):
        nc, ps, X = self.nc, self.ps, self.X
        free = [None] * 4
        for t in range(T):
            bank = t % 4
            for c in range(C):
                t_mm = self.pe.do(nc.tensor.matmul, ps[:, bank, 0:D], src[:, c, t * P:(t + 1) * P],
                                  w[:, c, :], start=(c == 0), stop=(c == C - 1), after=[free[bank]],
                                  signal=(c == C - 1))
            free[bank] = self.dve.do(nc.vector.tensor_tensor, X[:, t, :], ps[:, bank, 0:D], X[:, t, :],
                                     ALU.add, after=[t_mm], alone=True)
            self.take_stats(t, after=[free[bank]])
        self.phase()

    def add_transposed(self, src, after=()):
        nc, ps, X = self.nc, self.ps, self.X
        free = [None] * 4
        for tp in range(T // 2):
            bank = tp % 4
            for u in range(2):
                for c in range(C):
                    t = 2 * tp + u
                    t_tr = self.pe.do(nc.tensor.transpose, ps[:, bank, u * D + c * P:u * D + (c + 1) * P],
                                      src[:, c, t * P:(t + 1) * P], self.cst['ident'][:],
                                      after=[free[bank], *after])
            xs = X[:, 2 * tp:2 * tp + 2, :].rearrange("p t d -> p (t d)")
            free[bank] = self.dve.do(nc.vector.tensor_tensor, xs, ps[:, bank, :], xs, ALU.add, after=[t_tr])
            for u in range(2):
                self.take_stats(2 * tp + u, after=[free[bank]])
        self.phase()

    def cross_attention(self, L, scale, mask=None, wo='Wo', bo='bo'):
        nc, ps = self.nc, self.ps
        pe, dve, act, pool, sp = self.pe, self.dve, self.act, self.pool, self.sp
        V, A, G, M = nc.vector, nc.scalar, nc.gpsimd, nc.tensor
        name = f"L{L}_xattn_"
        st = ExitStack()
        wk, wv = (self.weight(st, name + w) for w in ('Wk', 'Wv'))
        wo = self.weight(st, name + wo)
        ctx_t = [self.tile(st, f"ctx{i}", [P, C, KEYS]) for i in range(2)]
        key_parts = self.tile(st, "key_parts", [P, 2, KEYS2], F32R)
        spread = self.tile(st, "spread", [P, ROWS, 2, P], F32R)
        kept = self.tile(st, "kept", [P, KEYS]) if mask == 'fill' else None
        mk = [self.tile(st, f"mk{i}", [P, KEYS]) for i in range(2)] if mask else None
        early = ExitStack()
        raw_spread = self.tile(early, "raw_spread", [P, ROWS * 2 * P])
        sp.dma(raw_spread[:], self.dram['spread'])
        wq = self.weight(early, name + 'Wq')

        def load_ctx(b, p, c):
            sp.dma(ctx_t[p][:, c, :], self.dram['ctx_t'][bass.ds(b, 1), c * P:(c + 1) * P, :]
                   .rearrange("o p k -> p (o k)"))

        def load_mask(b, p):
            if mask == 'add':
                src = self.dram['mask_f'][bass.ds(b, 1), :, :].rearrange("o q k -> q (o k)")
                self.sp_early.dma(mk[p][0:S, :], src)
                return self.sp_early.dma(mk[p][S:P, :], src)
            src = self.dram['mask_i'][bass.ds(b, 1), :].rearrange("o k -> (o k)").partition_broadcast(P)
            return self.sp_early.dma(mk[p][:].bitcast(I32), src)

        def mask_row(p, t_load=None):
            if mask == 'add':
                dve.do(V.tensor_scalar, mk[p][:], mk[p][:], -1.0e9, None, ALU.mult, after=[t_load], alone=True)
            else:
                dve.do(V.tensor_scalar, mk[p][:], mk[p][:].bitcast(I32), 0, -10000.0, ALU.is_equal, ALU.mult,
                       after=[t_load], alone=True)
                dve.do(V.tensor_scalar, kept[:], mk[p][:], -1.0, None, ALU.is_ge)

        for c in range(C):
            load_ctx(0, 0, c)
        if mask:
            load_mask(0, 0)
        self.layernorm()
        self.add_bias_row(name + bo)
        act.do(A.copy, spread[:].rearrange("p r i m -> p (r i m)"), raw_spread[:])
        dve.do(V.memset, key_parts[:, :, KEYS:KEYS2].bitcast(F32), 0.0)
        if mask:
            mask_row(0)
        qt = self.XNT
        t_mm = {}
        for n in range(2):
            for m in range(C):
                for c in range(C):
                    t_mm[n] = pe.do(M.matmul, ps[:, 2 * n + m, :], wq[:, c, m * P:(m + 1) * P],
                                    qt[:, c, n * 512:(n + 1) * 512], start=(c == 0), stop=(c == C - 1),
                                    signal=(c == C - 1))
        for n in range(2):
            for m in range(C):
                dve.do(V.tensor_scalar, qt[:, m, n * 512:(n + 1) * 512], ps[:, 2 * n + m, :],
                       self.col(name + 'bq')[:, m:m + 1], scale, ALU.add, ALU.mult, after=[t_mm[n]], alone=True)
        self.phase()
        early.close()

        key_stack = [self.tile(st, f"key_stack{g}", [P, ROWS, KEYS2], F32R) for g in range(2)]
        vals = [self.tile(st, f"vals{i}", [P, KT, D]) for i in range(2)]
        prob = self.tile(st, "prob", [P, ROWS, KEYS])
        prob_t = self.tile(st, "prob_t", [P, 3, 512])
        q_parts = self.tile(st, "q_parts", [P, 2, C, S], F32R)
        q_stack = [self.tile(st, f"q_stack{i}", [P, ROWS, C, P], F32R) for i in range(2)]
        mx = self.tile(st, "mx", [P, ROWS, len(KCH)])
        nmx = self.tile(st, "nmx", [P, ROWS])
        den = self.tile(st, "den", [P, ROWS, len(ECH)])
        rden = self.tile(st, "rden", [P, ROWS])
        diag = self.tile(st, "diag", [P, ROWS, P])
        rmask = self.tile(st, "rmask", [P, P])
        both = self.tile(st, "both", [P, P])
        kf = self.tile(st, "kf", [P, 2, KCH[0][1]]) if mask == 'fill' else None

        def slot(g, p, b, values=True, scores=True, project=True, load=True):
            n = 1 - p
            sg, sp_ = (1, p) if g == 0 else (0, n)
            t = {}
            if load:
                load_ctx(b + 2, p, g)
                if g == 1 and mask:
                    t['mask'] = load_mask(b + 2, p)
            if g == 0 and project:
                q_next = qt[:, :, bass.ds((b + 1) * S, S)]
                pool.do(G.tensor_copy, q_parts[:, 0], q_next)
                t_q = pool.do(G.tensor_tensor, q_parts[:, 1], q_next, q_parts[:, 0].bitcast(F32), ALU.subtract)

            def queries():
                for r in range(ROWS):
                    for part in range(2):
                        t_mm = pe.do(M.matmul, ps[:, 7, r * P:(r + 1) * P], spread[:, r, part, :],
                                     q_parts[:, part], start=(part == 0), stop=(part == 1), after=[t_q],
                                     signal=(part == 1))
                for h in range(2):
                    own = self.cst['pairmask'][:, h:h + 1]
                    bank_free[7] = act.do(A.activation, q_stack[n][:, :, :, h * S:(h + 1) * S],
                                          ps[:, 7, :].rearrange("p (r c q) -> p r c q", r=ROWS, c=C),
                                          ACT.Copy, scale=own, after=[t_mm], alone=True)

            s_free, t_read = [None] * ROWS, {}

            def score_chunk(k, pairs):
                k0, kw = KCH[k]
                vw = min(kw, KEYS - k0)
                read = t_read.get(min(KT - 1, (k0 + kw - 1) // P))
                t_s = {}
                for r in pairs:
                    t_s[r] = (pe.do(M.matmul, ps[:, r, 0:kw], q_stack[sp_][:, r, sg, :],
                                     key_stack[sg][:, r, k0:k0 + kw], start=True, stop=True, after=[s_free[r]]))
                for r in pairs:
                    o = prob[:, r, k0:k0 + vw]
                    if mask:
                        s_free[r] = dve.do(V.tensor_tensor_reduce, o, ps[:, r, 0:vw], mk[sp_][:, k0:k0 + vw],
                                           1.0, NEG, ALU.add, ALU.max, mx[:, r, k:k + 1], after=[t_s[r], read],
                                           alone=True)
                    else:
                        s_free[r] = dve.do(V.tensor_scalar, o, ps[:, r, 0:vw], 0.0, NEG, ALU.add, ALU.max,
                                           accum_out=mx[:, r, k:k + 1], after=[t_s[r], read], alone=True)
                if k == len(KCH) - 1 and pairs[-1] == ROWS - 1:
                    dve.do(V.tensor_reduce, nmx[:], mx[:], AX, ALU.max, negate=True)

            def exponentials(i):
                e0, e1 = ECH[i]
                for r in range(ROWS):
                    t['e', i] = act.do(A.activation, prob[:, r, e0:e1], prob[:, r, e0:e1], ACT.Exp,
                                       bias=nmx[:, r:r + 1], accum_out=den[:, r, i:i + 1], alone=True)

            def denominators():
                dve.do(V.tensor_reduce, rden[:], den[:], AX, ALU.add, after=[t['e', len(ECH) - 1]])
                t_rd = dve.do(V.reciprocal, rden[:], rden[:])
                for r in range(ROWS):
                    t['diag'] = pool.do(G.tensor_tensor, diag[:, r, :], self.cst['ident'][:],
                                        rden[:, r:r + 1].broadcast_to([P, P]), ALU.mult, after=[t_rd], alone=r > 0)

            bank_free = {}

            def keys_unit(k):
                k0, kw = KCH[k]
                vw = min(kw, KEYS - k0)
                for c in range(C):
                    t_mm = pe.do(M.matmul, ps[:, k, 0:vw], wk[:, c, g * P:(g + 1) * P], ctx_t[n][:, c, k0:k0 + vw],
                                 start=(c == 0), stop=(c == C - 1), signal=(c == C - 1))
                hi, lo = key_parts[:, 0, k0:k0 + vw], key_parts[:, 1, k0:k0 + vw]
                bias = self.col(name + 'bk')[:, g:g + 1]
                if mask == 'fill':
                    f = kf[:, k % 2, 0:vw]
                    t_f = s_free[k] = dve.do(V.scalar_tensor_tensor, f, ps[:, k, 0:vw], bias, kept[:, k0:k0 + vw],
                                             ALU.add, ALU.mult, after=[t_mm, t.get(('kf', k % 2))], alone=True)
                    t['hi', k] = act.do(A.copy, hi, f, after=[t_f], alone=True)
                    t['parts'] = t['kf', k % 2] = pool.do(G.tensor_tensor, lo, f, hi.bitcast(F32), ALU.subtract,
                                                          after=[t['hi', k]])
                else:
                    if k % 2:
                        t['hi', k] = dve.do(V.tensor_scalar, hi, ps[:, k, 0:vw], bias, None, ALU.add, after=[t_mm],
                                            alone=True)
                    else:
                        t['hi', k] = act.do(A.activation, hi, ps[:, k, 0:vw], ACT.Identity, bias=bias, after=[t_mm],
                                            alone=True)

            def keys_low(k):
                k0, kw = KCH[k]
                vw = min(kw, KEYS - k0)
                hi, lo = key_parts[:, 0, k0:k0 + vw], key_parts[:, 1, k0:k0 + vw]
                if mask != 'fill':
                    t['parts'] = s_free[k] = dve.do(V.scalar_tensor_tensor, lo, ps[:, k, 0:vw],
                                                    self.col(name + 'bk')[:, g:g + 1], hi.bitcast(F32),
                                                    ALU.add, ALU.subtract, after=[t['hi', k]], alone=True)
                if k == len(KCH) - 1:
                    for q in range(4):
                        for r in range(ROWS):
                            sp.dma(key_stack[g][32 * q:32 * q + 32, r, :].bitcast(F32),
                                   key_parts[32 * r:32 * r + 32, q // 2, :].bitcast(F32), after=[t['parts'], t['hi', k]])

            def values_unit(i, bank=7):
                tiles = [x for x in (2 * i, 2 * i + 1) if x < KT]
                w = min(P, KEYS - tiles[-1] * P)
                for u, kt in enumerate(tiles):
                    for c in range(C):
                        t_mm = pe.do(M.matmul, ps[0:w, bank, u * D:(u + 1) * D], ctx_t[n][:, c, kt * P:kt * P + w],
                                     wv[:, c, :], start=(c == 0), stop=(c == C - 1), after=[bank_free.get(bank)],
                                     signal=(c == C - 1))
                q, fn = (act, A.copy) if i % 2 else (dve, V.tensor_copy)
                bank_free[bank] = q.do(fn, vals[n][0:w, tiles[0]:tiles[-1] + 1, :],
                                       ps[0:w, bank, 0:len(tiles) * D].rearrange("p (t d) -> p t d", d=D),
                                       after=[t_mm], alone=True)

            pt_free = [None] * 2
            sb_free = [None] * 3
            t_sb = [None] * 3

            def chunk_of(kt):
                return t['e', [i for i, (e0, e1) in enumerate(ECH) if e0 <= kt * P < e1][0]]

            def transposes(kt):
                w, bank = min(P, KEYS - kt * P), kt % 2
                for r in range(ROWS):
                    t_tr = pe.do(M.transpose, ps[0:w, 4 + bank, r * P:(r + 1) * P],
                                 prob[:, r, kt * P:kt * P + w], self.cst['ident'][:],
                                 after=[pt_free[bank], chunk_of(kt)], signal=(r == ROWS - 1))
                t_read[kt] = t_tr
                q, fn = (act, A.copy) if kt >= 5 else (dve, V.tensor_copy)
                t_sb[kt % 3] = pt_free[bank] = q.do(fn, prob_t[0:w, kt % 3, :], ps[0:w, 4 + bank, :],
                                                    after=[t_tr, sb_free[kt % 3]], alone=True)

            def weighted(kt):
                w = min(P, KEYS - kt * P)
                for r in range(ROWS):
                    t_pv = pe.do(M.matmul, ps[32 * r:32 * r + 32, 6, g * P:(g + 1) * P],
                                 vals[p][0:w, kt, (ROWS * g + r) * 32:(ROWS * g + r + 1) * 32],
                                 prob_t[0:w, kt % 3, r * P:(r + 1) * P], start=(kt == 0), stop=(kt == KT - 1),
                                 after=[t_sb[kt % 3]], signal=(r == ROWS - 1))
                sb_free[kt % 3] = t['pv'] = t_pv

            v_units = range(0, 4) if g == 0 else range(4, 7)
            if values:
                exponentials(0)
            if project:
                keys_unit(0)
            if values:
                exponentials(1)
            if project:
                keys_unit(1)
            for kt in range(KT + 1):
                if values and kt < KT:
                    transposes(kt)
                if project and kt in (0, 1):
                    keys_unit(2 + kt)
                if project and kt in LOW_AT:
                    keys_low(LOW_AT.index(kt))
                if values and kt == 0:
                    exponentials(2)
                if project and g == 0 and kt == 3:
                    queries()
                if kt == 12 and 'mask' in t:
                    mask_row(p, t['mask'])
                if values and kt == 9:
                    denominators()
                if scores:
                    for k, pairs in SCORES_AT.get(kt, ()):
                        score_chunk(k, pairs)
                if values and kt:
                    weighted(kt - 1)
            if values:
                for r in range(ROWS):
                    t_rm = pe.do(M.matmul, ps[32 * r:32 * r + 32, 4, 0:P], self.cst['pairblk'][:], diag[:, r, :],
                                 start=True, stop=True, after=[t['diag'], pt_free[0]], signal=(r == ROWS - 1))
                t_rs = dve.do(V.tensor_copy, rmask[:], ps[:, 4, 0:P], after=[t_rm])
                dve.do(V.tensor_tensor, both[:], ps[:, 6, g * P:(g + 1) * P], rmask[:], ALU.mult,
                       after=[t['pv'], t_rs])
                dve.do(V.scalar_tensor_tensor, qt[:, g, bass.ds(b * S, S)], both[:, 0:S],
                       self.col(name + 'bv')[:, g:g + 1], both[:, S:P], ALU.add, ALU.add)
            if project:
                bank_free[5] = pt_free[1]
                for k, i in enumerate(v_units):
                    values_unit(i, (7, 5)[k % 2])
            self.phase()

        slot(0, 1, -1, values=False, scores=False)
        slot(1, 1, -1, values=False)
        with nc.Fori(0, (B - 2) // 2) as i:
            for p in range(2):
                for g in range(2):
                    slot(g, p, i * 2 + p)
        slot(0, 0, B - 2, load=False)
        slot(1, 0, B - 2, load=False)
        slot(0, 1, B - 1, project=False, load=False)
        slot(1, 1, B - 1, scores=False, project=False, load=False)
        self.out_project(qt, wo)
        st.close()

    def self_attention(self, L, scale, table):
        nc, ps, cst, XNT = self.nc, self.ps, self.cst, self.XNT
        pe, dve, act, pool, sp = self.pe, self.dve, self.act, self.pool, self.sp
        V, A, G, M = nc.vector, nc.scalar, nc.gpsimd, nc.tensor
        name = f"L{L}_attn_"
        st = ExitStack()
        bias = self.tile(st, "table", [P, H * S])
        sp.dma(bias[:], self.dram[table])
        vmask = self.tile(st, "vmask", [P, D])
        sp.dma(vmask[:], self.dram['c_vmask'])
        qt = self.tile(st, "qt", [P, C, NT])
        kt = self.tile(st, "kt", [P, C, NT])
        src = XNT
        bv = None
        if L == 3:
            wv, wo, src = self.latent_projections(st, name, qt, kt, scale)
        else:
            w = {n: self.weight(st, name + n) for n in ('Wq', 'Wk', 'Wv', 'Wo')}
            wv, wo = w['Wv'], w['Wo']
            if L == 1:
                w.update({n: self.weight(st, name + n) for n in ('Wqs', 'Wks')})
            self.layernorm()
            if name + 'bo' in BIAS_ROWS:
                self.add_bias_row(name + 'bo')
            if L == 0:
                self.project(qt, w['Wq'], None, scale)
                self.project(kt, w['Wk'], None, banks=(2, 3))
            elif L == 1:
                self.rotated(st, name, w, qt, kt, scale)
                bv = self.col(name + 'bv')
            else:
                self.silu_normed(st, name, w, qt, kt)
            self.phase()
        nsrc = wv.shape[1]
        OT = self.tile(st, "heads_out", [P, C, NT])
        U = 2
        q2 = [self.tile(st, f"q2{u}", [P, C, P]) for u in range(U)]
        kb = [self.tile(st, f"kb{u}", [P, C, 2, 512]) for u in range(U)]
        xd = [self.tile(st, f"xd{u}", [P, nsrc, 2, 2, S]) for u in range(U)]
        vb = [self.tile(st, f"vb{u}", [P, 2, D]) for u in range(U)]
        pr = [self.tile(st, f"pr{u}", [P, H, S]) for u in range(U)]
        pt = [self.tile(st, f"pt{u}", [P, 2, 512]) for u in range(U)]
        mx = [self.tile(st, f"smx{u}", [P, H]) for u in range(U)]

        def tiles(t0):
            tk = [{} for _ in range(U)]
            for u in range(U):
                at = bass.ds((t0 + u) * P, P)
                tk[u]['q'] = dve.do(V.tensor_copy, q2[u][:], qt[:, :, at])
                for c in range(C):
                    for bb in range(2):
                        kk = kt[:, c, bass.ds((t0 + u) * P + bb * S, S)]
                        q, eng = (pool, G) if c else (dve, V)
                        tk[u]['k', c, bb] = q.do(
                            eng.tensor_tensor, kb[u][:, c, bb, :].rearrange("p (h k) -> p h k", k=S),
                            kk.unsqueeze(1).broadcast_to([P, H // 2, S]),
                            cst['headmask'][:].unsqueeze(2).broadcast_to([P, H // 2, S]), ALU.mult)
                for c in range(nsrc):
                    for bb in range(2):
                        tk[u]['x'] = act.do(A.copy, xd[u][:, c, bb], src[:, c, bass.ds((t0 + u) * P + bb * S, S)]
                                            .unsqueeze(1).broadcast_to([P, 2, S]))
            for u in range(U):
                for c in range(C):
                    for bb in range(2):
                        tk[u]['s', c] = pe.do(M.matmul, ps[bb * S:(bb + 1) * S, 4 * u + c, :],
                                              q2[u][:, c, bb * S:(bb + 1) * S], kb[u][:, c, bb, :], start=True,
                                              stop=True, after=[tk[u]['q'], tk[u]['k', c, bb]])
                for bb in range(2):
                    for c in range(nsrc):
                        tk[u]['v'] = pe.do(M.matmul, ps[:, 4 * u + 2, bb * D:(bb + 1) * D],
                                           xd[u][:, c, bb].rearrange("p r k -> p (r k)"), wv[:, c, :],
                                           start=(c == 0), stop=(c == nsrc - 1), after=[tk[u]['x']])
                if L == 2:
                    tk[u]['v'] = act.do(A.activation, vb[u][:].rearrange("p b d -> p (b d)"), ps[:, 4 * u + 2, :],
                                        ACT.Silu, after=[tk[u]['v']])
            for u in range(U):
                for c in range(C):
                    t_s = dve.do(V.tensor_tensor, pr[u][:, 8 * c:8 * c + 8, :].rearrange("p h k -> p (h k)"),
                                 ps[:, 4 * u + c, :], bias[:, c * 512:(c + 1) * 512], ALU.add,
                                 after=[tk[u]['s', c]])
                t_m = dve.do(V.tensor_reduce, mx[u][:], pr[u][:], AX, ALU.max)
                t_d = dve.do(V.tensor_tensor, pr[u][:], pr[u][:], mx[u][:].unsqueeze(2).broadcast_to([P, H, S]),
                             ALU.subtract)
                tk[u]['e'] = act.do(A.activation, pr[u][:], pr[u][:], ACT.Exp, after=[t_d])
            for u in range(U):
                v = vb[u][:] if L == 2 else ps[:, 4 * u + 2, :].rearrange("p (b d) -> p b d", b=2)
                tk[u]['vb'] = dve.do(V.tensor_tensor, vb[u][:], v,
                                     vmask[:].unsqueeze(1).broadcast_to([P, 2, D]), ALU.mult,
                                     after=[tk[u]['v']])
                dve.do(V.tensor_reduce, mx[u][:], pr[u][:], AX, ALU.add, after=[tk[u]['e']])
                dve.do(V.reciprocal, mx[u][:], mx[u][:])
                tk[u]['p'] = dve.do(V.tensor_tensor, pr[u][:], pr[u][:],
                                    mx[u][:].unsqueeze(2).broadcast_to([P, H, S]), ALU.mult)
            for u in range(U):
                for half in range(2):
                    for r in range(ROWS):
                        j = 4 * half + r
                        t_tr = pe.do(M.transpose, ps[:, 4 * u + half, r * P:(r + 1) * P],
                                     pr[u][:, 2 * j:2 * j + 2, :].rearrange("p h k -> p (h k)"), cst['ident'][:],
                                     after=[tk[u]['p']])
                    q, fn = (act, A.copy) if half else (dve, V.tensor_copy)
                    tk[u]['pt', half] = q.do(fn, pt[u][:, half, :], ps[:, 4 * u + half, :], after=[t_tr])
            for u in range(U):
                for half in range(2):
                    for bb in range(2):
                        for r in range(ROWS):
                            j = 4 * half + r
                            t_o = pe.do(M.matmul, ps[32 * r:32 * r + 32, 4 * u + 3, half * P + bb * S:half * P + bb * S + S],
                                        vb[u][:, bb, 32 * j:32 * j + 32], pt[u][:, half, r * P + bb * S:r * P + bb * S + S],
                                        start=True, stop=True, after=[tk[u]['pt', half], tk[u]['vb']])
                o, s = OT[:, :, bass.ds((t0 + u) * P, P)], ps[:, 4 * u + 3, 0:256].rearrange("p (c t) -> p c t", c=C)
                if bv is None:
                    dve.do(V.tensor_copy, o, s, after=[t_o])
                else:
                    for c in range(C):
                        dve.do(V.tensor_scalar, OT[:, c, bass.ds((t0 + u) * P, P)], s[:, c], bv[:, c:c + 1], None,
                               ALU.add, after=[t_o])
            self.phase()

        with nc.Fori(0, T // (2 * U)) as i:
            for half in range(2):
                tiles(i * (2 * U) + half * U)
        if wo is not None:
            self.out_project(OT, wo)
        else:
            self.add_transposed(OT)
        st.close()

    def rotated(self, st, name, w, qt, kt, scale):
        nc, cst = self.nc, self.cst
        swapped = self.tile(st, "swapped", [P, C, NT])
        for x, n, b, s in ((qt, 'Wq', 'bq', scale), (kt, 'Wk', 'bk', 1.0)):
            t1 = self.project(x, w[n], self.col(name + b), s)
            t2 = self.project(swapped, w[n + 's'], self.col(name + b + 's'), s, banks=(2, 3))
            for c in range(C):
                for o, table in ((x, 'cosine'), (swapped, 'sine')):
                    o = o[:, c, :].rearrange("p (b s) -> p b s", s=S)
                    self.dve.do(nc.vector.tensor_tensor, o, o, cst[table][:].unsqueeze(1).broadcast_to([P, B, S]),
                                ALU.mult, after=[t1, t2])
                self.dve.do(nc.vector.tensor_tensor, x[:, c, :], x[:, c, :], swapped[:, c, :], ALU.add)
            self.phase()

    def silu_normed(self, st, name, w, qt, kt):
        nc, ps, cst = self.nc, self.ps, self.cst
        for x, n in ((qt, 'Wq'), (kt, 'Wk')):
            for m in range(C):
                for h in range(2):
                    bank = 2 * m + h
                    for c in range(C):
                        t_mm = self.pe.do(nc.tensor.matmul, ps[:, bank, :], w[n][:, c, m * P:(m + 1) * P],
                                          self.XNT[:, c, h * 512:(h + 1) * 512], start=(c == 0), stop=(c == C - 1))
                    self.act.do(nc.scalar.activation, x[:, m, h * 512:(h + 1) * 512], ps[:, bank, :], ACT.Silu,
                                after=[t_mm])
            self.phase()
        sq = self.tile(st, "sq", [P, 2, 512])
        rad = self.tile(st, "rad", [P, 512])
        headblk = self.tile(st, "headblk", [P, P])
        t_hb = self.sp.dma(headblk[:], self.dram['c_headblk'])
        free = {}
        for x, n in ((qt, 'q_scale'), (kt, 'k_scale')):
            for m in range(C):
                for h in range(2):
                    o, f = x[:, m, h * 512:(h + 1) * 512], sq[:, h, :]
                    t_sq = self.pool.do(nc.gpsimd.tensor_tensor, f, o, o, ALU.mult, after=[free.get(h)])
                    t_mm = self.pe.do(nc.tensor.matmul, ps[:, h, :], headblk[:], f, start=True, stop=True,
                                      after=[t_sq, t_hb])
                    t_r = self.act.do(nc.scalar.activation, f, ps[:, h, :], ACT.Sqrt, after=[t_mm])
                    self.dve.do(nc.vector.tensor_scalar, rad[:], f, 1e-6, None, ALU.add, after=[t_r])
                    self.dve.do(nc.vector.reciprocal, rad[:], rad[:])
                    self.dve.do(nc.vector.tensor_tensor, f, f, rad[:], ALU.mult)
                    free[h] = self.dve.do(nc.vector.scalar_tensor_tensor, o, f, self.col(name + n)[:, m:m + 1], o,
                                          ALU.mult, ALU.mult)
        self.phase()

    def latent_projections(self, st, name, qt, kt, scale):
        nc, ps = self.nc, self.ps
        M, A = nc.tensor, nc.scalar
        w = {n: self.weight(st, name + n, r, m) for n, r, m in
             (('W_dqT', D, P), ('W_dq', P, D), ('W_uqT', P, D), ('W_dkvT', D, P), ('W_uk', D, P), ('W_uv', D, P),
              ('W_oT', D, D))}
        self.layernorm()
        a = self.tile(st, "uq_dq", [P, C, D])
        keff = self.tile(st, "keff", [P, 1, D])
        veff = self.tile(st, "veff", [P, 1, D])
        lat = self.tile(st, "lat", [P, 1, NT])
        ckv = self.tile(st, "ckv", [P, 1, NT])
        for m in range(C):
            t_mm = self.pe.do(M.matmul, ps[:, m, 0:D], w['W_uqT'][:, 0, m * P:(m + 1) * P], w['W_dq'][:, 0, :],
                              start=True, stop=True)
            t_a = self.act.do(A.copy, a[:, m, :], ps[:, m, 0:D], after=[t_mm])
        for c in range(C):
            t_k = self.pe.do(M.matmul, ps[:, 2, 0:D], w['W_uk'][:, c, :], a[:, c, :], start=(c == 0),
                             stop=(c == C - 1), after=[t_a])
        for c in range(C):
            t_v = self.pe.do(M.matmul, ps[:, 3, 0:D], w['W_uv'][:, c, :], w['W_oT'][:, c, :], start=(c == 0),
                             stop=(c == C - 1))
        t_k = self.act.do(A.copy, keff[:, 0, :], ps[:, 2, 0:D], after=[t_k])
        self.act.do(A.copy, veff[:, 0, :], ps[:, 3, 0:D], after=[t_v])
        self.project(lat, w['W_dqT'], banks=(4, 5))
        self.project(ckv, w['W_dkvT'], banks=(6, 7))
        self.phase()
        self.project(qt, w['W_uqT'], None, scale, src=lat)
        self.project(kt, keff, src=ckv, banks=(2, 3))
        self.phase()
        return veff, None, ckv

    def largest(self, x, m, big, after=()):
        self.dve.do(self.nc.vector.tensor_reduce, big[:, m:m + 1], x[:, m], AX, ALU.max,
                    apply_absolute_value=True, after=after, alone=True)

    def steps(self, big, name):
        V, one = self.nc.vector, self.tile(self.ffn_stack, name, [P, 4])
        t = self.dve.do(V.tensor_reduce, one[:, 0:1], big[:], AX, ALU.max)
        t = self.pool.do(self.nc.gpsimd.partition_all_reduce, one[:, 1:2], one[:, 0:1], P, RMAX, after=[t])
        self.dve.do(V.tensor_scalar, one[:, 2:3], one[:, 1:2], 1.0 / 32767.0, 1e-12, ALU.mult, ALU.max, after=[t])
        return one, self.dve.do(V.reciprocal, one[:, 3:4], one[:, 2:3])

    def quantize_rows(self, x, m, one, t_one, after=()):
        V, k = self.nc.vector, self.round_no % len(self.rounded)
        self.round_no += 1
        tmp = self.rounded[k]
        t = self.act.do(self.nc.scalar.activation, tmp[:], x[:, m], ACT.Identity, bias=self.big_col[:],
                        scale=one[:, 3:4], after=[t_one, self.round_free[k], *after], alone=True)
        t = self.dve.do(V.tensor_scalar, tmp[:], tmp[:], -BIG, -32768.0, ALU.add, ALU.max, after=[t], alone=True)
        self.round_free[k] = self.dve.do(V.tensor_scalar, x[:, m], tmp[:], 32767.0, one[:, 2:3], ALU.min, ALU.mult,
                                         after=[t], alone=True)
        return self.round_free[k]

    def quantize_weight(self, w, tmp, sc):
        V, dve = self.nc.vector, self.dve
        wb = w[:].rearrange("p c (b i) -> p (c b) i", i=32)
        tb = tmp[:].rearrange("p c (b i) -> p (c b) i", i=32)
        nb = wb.shape[1]
        spread = lambda s: sc[:, s, :].unsqueeze(2).broadcast_to([P, nb, 32])
        dve.do(V.tensor_reduce, sc[:, 0, :], wb, AX, ALU.max, apply_absolute_value=True)
        dve.do(V.tensor_scalar, sc[:, 0, :], sc[:, 0, :], 1.0 / 7.0, 1e-12, ALU.mult, ALU.max)
        dve.do(V.reciprocal, sc[:, 1, :], sc[:, 0, :])
        dve.do(V.tensor_tensor, tb, wb, spread(1), ALU.mult)
        dve.do(V.tensor_scalar, tb, tb, BIG, -BIG, ALU.add, ALU.add)
        dve.do(V.tensor_scalar, tb, tb, -8.0, 7.0, ALU.max, ALU.min)
        return dve.do(V.tensor_tensor, wb, tb, spread(0), ALU.mult)

    def quantized_ffn(self):
        nc, ps, V, A, M = self.nc, self.ps, self.nc.vector, self.nc.scalar, self.nc.tensor
        pe, dve, act, X, xq = self.pe, self.dve, self.act, self.X, self.XNT
        F = 768
        NF = F // P
        st = self.ffn_stack = ExitStack()
        raw = {n: self.weight(st, "L0_ffn_w_" + n, *shape) for n, shape in
               (('up', (F, D)), ('gate', (F, D)), ('down', (D, F)))}
        turned = {'up': self.tile(st, "wu_t", [P, C, F]), 'gate': self.tile(st, "wg_t", [P, C, F]),
                  'down': self.tile(st, "wd_t", [P, NF, D])}
        tmp, tmp2 = self.tile(st, "tmp", [P, NF, D]), self.tile(st, "tmp2", [P, C, F])
        sc = self.tile(st, "sc", [P, 2, NF * D // 32])
        up, gate = self.tile(st, "up", [P, NF, NT]), self.tile(st, "gate", [P, NF, NT])
        self.rounded = [self.tile(st, f"rounded{i}", [P, NT]) for i in range(4)]
        self.round_free, self.round_no = [None] * 4, 0
        self.big_col = self.tile(st, "big_col", [P, 1])
        big = {n: self.tile(st, "big_" + n, [P, k]) for n, k in (('x', C), ('up', NF), ('gate', NF), ('act', NF),
                                                                 ('hid', NF))}
        dve.do(V.memset, self.big_col[:], BIG)
        self.layernorm()

        bank_free, t_w = [None] * 4, {}

        def turn(n):
            w, flat = raw[n], turned[n][:].rearrange("p i o -> p (i o)")
            blocks = [(i, o) for i in range(w.shape[2] // P) for o in range(w.shape[1])]
            for j in range(0, len(blocks), 4):
                bank = (j // 4) % 4
                for u, (i, o) in enumerate(blocks[j:j + 4]):
                    t = pe.do(M.transpose, ps[:, bank, u * P:(u + 1) * P], w[:, o, i * P:(i + 1) * P],
                              self.cst['ident'][:], after=[t_w[n], bank_free[bank]], signal=(u == 3))
                bank_free[bank] = t_w['t', n] = act.do(A.copy, flat[:, j * P:(j + 4) * P], ps[:, bank, :], after=[t],
                                                       alone=True)

        for c in range(C):
            self.largest(xq, c, big['x'])
        one, t_one = self.steps(big['x'], "one_x")
        t_w['up'] = self.quantize_weight(raw['up'], tmp, sc)
        for c in range(C):
            t_x = self.quantize_rows(xq, c, one, t_one)
        t_w['gate'] = self.quantize_weight(raw['gate'], tmp, sc)
        turn('up')
        free = {}
        for m in range(NF):
            t = self.project(up[:, m:m + 1], turned['up'][:, :, m * P:(m + 1) * P], src=xq, banks=(4, 5), free=free,
                             after=[t_x, t_w['t', 'up']])
            self.largest(up, m, big['up'], after=[t])
        one, t_one = self.steps(big['up'], "one_up")
        turn('gate')
        t_w['down'] = self.quantize_weight(raw['down'], tmp2, sc)
        free = {}
        for m in range(NF):
            t = self.project(gate[:, m:m + 1], turned['gate'][:, :, m * P:(m + 1) * P], src=xq, banks=(6, 7),
                             free=free, after=[t_w['t', 'gate']])
            self.quantize_rows(up, m, one, t_one)
            self.largest(gate, m, big['gate'], after=[t])
        turn('down')
        one, t_one = self.steps(big['gate'], "one_gate")
        k = len(self.rounded)
        for m in range(NF + 1):
            if m < NF:
                t_g = self.quantize_rows(gate, m, one, t_one)
                i = self.round_no % k
                self.round_no += 1
                sig = self.rounded[i]
                t_s = act.do(A.activation, sig[:], gate[:, m], ACT.Sigmoid, after=[t_g, self.round_free[i]],
                             alone=True)
                self.round_free[i] = t_s
                now = (m, sig, i, t_s)
            if m:
                j, sig, i, t_s = before
                t = dve.do(V.tensor_scalar, sig[:], sig[:], BIG / 65536.0, None, ALU.add, after=[t_s], alone=True)
                t = dve.do(V.tensor_scalar, sig[:], sig[:], -BIG / 65536.0, 65535.0 / 65536.0, ALU.add, ALU.min)
                t = self.round_free[i] = dve.do(V.scalar_tensor_tensor, gate[:, j], sig[:], 0.0, gate[:, j], ALU.max,
                                                ALU.mult)
                self.largest(gate, j, big['act'], after=[t])
            before = now
        one, t_one = self.steps(big['act'], "one_act")
        for m in range(NF):
            t = self.quantize_rows(gate, m, one, t_one)
            t = dve.do(V.tensor_tensor, gate[:, m], gate[:, m], up[:, m], ALU.mult, after=[t])
            self.largest(gate, m, big['hid'], after=[t])
        one, t_one = self.steps(big['hid'], "one_hid")
        for m in range(NF):
            t_g = self.quantize_rows(gate, m, one, t_one)
            for t in range(T):
                t_mm = pe.do(M.matmul, ps[:, t, 0:D], gate[:, m, t * P:(t + 1) * P], turned['down'][:, m, :],
                             start=(m == 0), stop=(m == NF - 1), after=[t_g, t_w['t', 'down']])
                if m == NF - 1:
                    t_a = dve.do(V.tensor_tensor, X[:, t, :], ps[:, t, 0:D], X[:, t, :], ALU.add, after=[t_mm],
                                 alone=True)
                    self.take_stats(t, after=[t_a])
        self.phase()
        st.close()

    def recurrent_ffn(self):
        nc, ps, V, A, M = self.nc, self.ps, self.nc.vector, self.nc.scalar, self.nc.tensor
        st = ExitStack()
        wx = [self.weight(st, 'L1_ffn_' + n) for n in ('wf', 'wi', 'wc')]
        wc = [self.weight(st, 'L1_ffn_' + n) for n in ('uf', 'ui', 'uc')]
        wo, uo = self.weight(st, 'L1_ffn_wo'), self.weight(st, 'L1_ffn_uo')
        self.layernorm()
        pre = self.tile(st, "pre", [P, 3, C, NT])
        out = self.tile(st, "out", [P, C, NT])
        cell = self.tile(st, "cell", [P, C, S])
        gates = self.tile(st, "gates", [P, 3, C, S])
        for k, b in enumerate(('bf', 'bi', 'bc')):
            self.project(pre[:, k], wx[k], self.col('L1_ffn_' + b), banks=(2 * k, 2 * k + 1))
        self.project(out, wo, self.col('L1_ffn_bo'), banks=(6, 7))
        self.dve.do(V.tensor_copy, cell[:], self.col('L1_ffn_in_c').unsqueeze(2).broadcast_to([P, C, S]))
        self.phase()

        def step(t):
            at = bass.ds(t * S, S)
            for k in range(3):
                for m in range(C):
                    for c in range(C):
                        t_mm = self.pe.do(M.matmul, ps[:, k, m * S:(m + 1) * S], wc[k][:, c, m * P:(m + 1) * P],
                                          cell[:, c, :], start=(c == 0), stop=(c == C - 1), signal=(c == C - 1))
                t_g = self.dve.do(V.tensor_tensor, gates[:, k], ps[:, k, 0:C * S].rearrange("p (c s) -> p c s", c=C),
                                  pre[:, k, :, at], ALU.add, after=[t_mm])
                t_a = self.act.do(A.activation, gates[:, k], gates[:, k], ACT.Tanh if k == 2 else ACT.Sigmoid,
                                  after=[t_g])
                if k == 0:
                    t_f = t_a
            self.dve.do(V.tensor_tensor, cell[:], cell[:], gates[:, 0], ALU.mult, after=[t_f, t_mm])
            self.dve.do(V.tensor_tensor, gates[:, 1], gates[:, 1], gates[:, 2], ALU.mult, after=[t_a])
            self.dve.do(V.tensor_tensor, cell[:], cell[:], gates[:, 1], ALU.add)
            self.phase()

        with nc.Fori(0, B // 2) as i:
            step(i * 2)
            step(i * 2 + 1)
        for m in range(C):
            for c in range(C):
                t_mm = self.pe.do(M.matmul, ps[:, 0, m * S:(m + 1) * S], uo[:, c, m * P:(m + 1) * P], cell[:, c, :],
                                  start=(c == 0), stop=(c == C - 1))
        t_u = self.act.do(A.copy, gates[:, 0], ps[:, 0, 0:C * S].rearrange("p (c s) -> p c s", c=C), after=[t_mm])
        for c in range(C):
            o = out[:, c, :].rearrange("p (b s) -> p b s", s=S)
            t_o = self.dve.do(V.tensor_tensor, o, o, gates[:, 0, c, :].unsqueeze(1).broadcast_to([P, B, S]), ALU.add,
                              after=[t_u])
            t_h = self.act.do(A.activation, out[:, c, :], out[:, c, :], ACT.Tanh, after=[t_o])
        self.add_transposed(out, after=[t_h])
        st.close()

    def expert_weights(self, st, logits):
        nc, V, cst, dve = self.nc, self.nc.vector, self.cst, self.dve
        n = E_MOE
        mine = lambda t: logits[:, t, :].unsqueeze(2).broadcast_to([P, n, n])
        others = lambda t: logits[:, t, :].unsqueeze(1).broadcast_to([P, n, n])
        rank = self.tile(st, "rank", [P, T, n])
        larger = self.tile(st, "larger", [P, n, n])
        equal = self.tile(st, "equal", [P, n, n])
        top = self.tile(st, "top", [P, T])
        for t in range(T):
            dve.do(V.tensor_tensor, larger[:], others(t), mine(t), ALU.is_gt)
            dve.do(V.tensor_tensor, equal[:], others(t), mine(t), ALU.is_equal)
            dve.do(V.tensor_tensor, equal[:], equal[:], cst['before'][:].rearrange("p (a b) -> p a b", a=n), ALU.mult)
            dve.do(V.tensor_tensor, larger[:], larger[:], equal[:], ALU.add)
            dve.do(V.tensor_reduce, rank[:, t, :], larger[:], AX, ALU.add)
        over = lambda a: a[:].unsqueeze(2).broadcast_to([P, T, n])
        dve.do(V.tensor_scalar, rank[:], rank[:], TOPK - 0.5, None, ALU.is_lt)
        dve.do(V.tensor_reduce, top[:], logits[:], AX, ALU.max)
        t = dve.do(V.tensor_tensor, logits[:], logits[:], over(top), ALU.subtract)
        t = self.act.do(nc.scalar.activation, logits[:], logits[:], ACT.Exp, after=[t])
        dve.do(V.tensor_tensor, logits[:], logits[:], rank[:], ALU.mult, after=[t])
        dve.do(V.tensor_reduce, top[:], logits[:], AX, ALU.add)
        dve.do(V.reciprocal, top[:], top[:])
        return dve.do(V.tensor_tensor, logits[:], logits[:], over(top), ALU.mult)

    def expert_ffn(self, L):
        nc, ps, V, A, M, G = self.nc, self.ps, self.nc.vector, self.nc.scalar, self.nc.tensor, self.nc.gpsimd
        pe, dve, act, pool, sp, cst = self.pe, self.dve, self.act, self.pool, self.sp, self.cst
        name, X, XNT = f"L{L}_ffn_", self.X, self.XNT
        gated = L == 2
        F, FT = (684, 114) if gated else (512, P)
        NF = F // FT
        n = E_MOE
        st = ExitStack()
        router = self.weight(st, name + ('centroidT' if gated else 'routerT'), D, n)
        bout = self.tile(st, "bout", [n, D])
        sp.dma(bout[:], self.dram[name + 'bout'])
        keys = ('w1', 'w2', 'wout') if gated else ('w1', 'wout')
        raw = {k: self.tile(st, "raw_" + k, [FT, NF, D] if k == 'wout' else [P, C, F]) for k in keys}
        parts = {k: [self.tile(st, f"parts_{k}{i}", [raw[k].shape[0], 2, *raw[k].shape[1:]], F32R)
                     for i in range(2)] for k in keys}
        b1 = [self.tile(st, f"b1{i}", [FT, NF]) for i in range(2)]
        b2 = [self.tile(st, f"b2{i}", [FT, NF]) for i in range(2)] if gated else None

        def load_expert(e, read=()):
            for k in keys:
                pattern = "o (m p) d -> p (o m) d" if k == 'wout' else "o (c p) f -> p (o c) f"
                sp.dma(raw[k][:], self.dram[name + k][bass.ds(e, 1)].rearrange(pattern, p=FT if k == 'wout' else P),
                       after=read)

        def load_biases(e, p):
            for k, tiles in (('b1', b1), ('b2', b2)):
                if tiles:
                    sp.dma(tiles[p][:], self.dram[name + k][bass.ds(e, 1)].rearrange("o p m -> p (o m)"))

        def cut(dst, src, after=()):
            t = act.do(A.copy, dst[:, 0], src, after=after, alone=True)
            return t, pool.do(G.tensor_tensor, dst[:, 1], src, dst[:, 0].bitcast(F32), ALU.subtract, after=[t],
                              alone=True)

        def cut_part(k, p):
            return cut(parts[k][p], raw[k][:])[1]

        PASSES = ((0, 0), (1, 0), (0, 1))

        load_expert(0)
        load_biases(0, 0)
        self.layernorm()
        we = self.tile(st, "we", [P, T, n])
        wet = self.tile(st, "wet", [n, NT])
        x_parts = self.tile(st, "x_parts", [P, 2, C, NT], F32R)
        hid = self.tile(st, "hid", [FT, 2, NF, NT], F32R)
        hid_f = [self.tile(st, f"hid_f{i}", [FT, 512]) for i in range(3)]
        act_o = [self.tile(st, f"act{i}", [FT, 512]) for i in range(2)]
        cut(x_parts, XNT[:])
        load_expert(1, [cut_part(k, 0) for k in keys])
        for t in range(T):
            for c in range(C):
                t_r = pe.do(M.matmul, ps[:, 0, t * n:(t + 1) * n], XNT[:, c, t * P:(t + 1) * P], router[:, c, :],
                            start=(c == 0), stop=(c == C - 1))
        if gated:
            sq = self.tile(st, "sq", [P, C, NT])
            csq = self.tile(st, "csq", [P, C, n])
            ones = self.tile(st, "ones", [P, P])
            dve.do(V.memset, ones[:], 1.0)
            dve.do(V.tensor_tensor, csq[:], router[:], router[:], ALU.mult)
            t_sq = dve.do(V.tensor_tensor, sq[:], XNT[:], XNT[:], ALU.mult)
            for t in range(T):
                for c in range(C):
                    pe.do(M.matmul, ps[:, 1, t * n:(t + 1) * n], sq[:, c, t * P:(t + 1) * P], ones[:, 0:n],
                          start=(c == 0), stop=False, after=[t_sq])
                for c in range(C):
                    t_d = pe.do(M.matmul, ps[:, 1, t * n:(t + 1) * n], ones[:], csq[:, c, :], start=False,
                                stop=(c == C - 1))
            w = we[:].rearrange("p t e -> p (t e)")
            t_c = act.do(A.copy, w, ps[:, 1, 0:T * n], after=[t_d])
            dve.do(V.scalar_tensor_tensor, w, ps[:, 0, 0:T * n], -2.0, w, ALU.mult, ALU.add, after=[t_c, t_r])
            t_d = dve.do(V.tensor_scalar, w, w, 1e-12, None, ALU.max)
            t_w = act.do(A.activation, w, w, ACT.Sqrt, after=[t_d])
        else:
            t_w = act.do(A.copy, we[:].rearrange("p t e -> p (t e)"), ps[:, 0, 0:T * n], after=[t_r])
        dve.wait(t_w)
        t_we = self.expert_weights(st, we)
        free = [None] * 2
        for t in range(T):
            bank = 2 + t % 2
            t_tr = pe.do(M.transpose, ps[0:n, bank, 0:P], we[:, t, :], cst['ident'][:], after=[t_we, free[t % 2]])
            t_c = act.do(A.copy, wet[:, t * P:(t + 1) * P], ps[0:n, bank, 0:P], after=[t_tr])
            t_b = pe.do(M.matmul, ps[:, bank, 256:512], wet[:, t * P:(t + 1) * P], bout[:], start=True, stop=True,
                        after=[t_c])
            free[t % 2] = dve.do(V.tensor_tensor, X[:, t, :], ps[:, bank, 256:512], X[:, t, :], ALU.add, after=[t_b])
        self.phase()

        def expert(e, p, load=True, last=False):
            if not last:
                load_biases(e + 1, 1 - p)
            free, af, k, t_h, hf_free, t_cut = {}, [None] * 2, 0, {}, [None] * 3, []

            def hidden(bank, w, m, toks):
                for c in range(C):
                    for i, (a, b) in enumerate(PASSES):
                        t = pe.do(M.matmul, ps[0:FT, bank, :], w[:, a, c, m * FT:(m + 1) * FT],
                                  x_parts[:, b, c, toks], start=(c == 0 and i == 0),
                                  stop=(c == C - 1 and i == 2), after=[free.get(bank)],
                                  signal=(c == C - 1 and i == 2))
                return t

            for h in range(2):
                for m in range(NF):
                    if k < len(keys) and not last:
                        t_cut += [cut_part(keys[k], 1 - p)]
                        if load and k == len(keys) - 1:
                            load_expert(e + 2, t_cut)
                    toks = slice(h * 512, (h + 1) * 512)
                    bank, i, hf = 2 * (k % 2), k % 2, hid_f[k % 3]
                    t1 = hidden(bank, parts['w1'][p], m, toks)
                    if gated:
                        t2 = hidden(bank + 1, parts['w2'][p], m, toks)
                        free[bank] = act.do(A.activation, act_o[i][:], ps[0:FT, bank, :], ACT.Silu,
                                            bias=b1[p][:, m:m + 1], after=[t1, af[i]], alone=True)
                        t = af[i] = free[bank + 1] = dve.do(
                            V.scalar_tensor_tensor, hf[:], ps[0:FT, bank + 1, :], b2[p][:, m:m + 1],
                            act_o[i][:], ALU.add, ALU.mult, after=[t2, free[bank], hf_free[k % 3]], alone=True)
                    else:
                        t = free[bank] = act.do(A.activation, hf[:], ps[0:FT, bank, :], ACT.Gelu,
                                                bias=b1[p][:, m:m + 1], after=[t1, hf_free[k % 3]], alone=True)
                    t_hi = act.do(A.copy, hid[:, 0, m, toks], hf[:], after=[t], alone=True)
                    t_h[h] = hf_free[k % 3] = dve.do(V.tensor_tensor, hid[:, 1, m, toks], hf[:],
                                                     hid[:, 0, m, toks].bitcast(F32), ALU.subtract, after=[t_hi],
                                                     alone=True)
                    k += 1
            for t in range(T):
                bank = 4 + t % 4
                for m in range(NF):
                    for i, (a, b) in enumerate(PASSES):
                        t_y = pe.do(M.matmul, ps[:, bank, 0:D], hid[:, a, m, t * P:(t + 1) * P],
                                    parts['wout'][p][:, b, m, :], start=(m == 0 and i == 0),
                                    stop=(m == NF - 1 and i == 2), after=[free.get(bank), t_h[t // 4]],
                                    signal=(m == NF - 1 and i == 2))
                free[bank] = dve.do(V.scalar_tensor_tensor, X[:, t, :], ps[:, bank, 0:D], we_col(t, e, p),
                                    X[:, t, :], ALU.mult, ALU.add, after=[t_y], alone=True)
                if last and gated:
                    self.take_stats(t, after=[free[bank]])
            self.phase()

        now = [self.tile(st, f"now{i}", [P, T]) for i in range(2)]

        def we_col(t, e, p):
            return now[p][:, t:t + 1]

        def pick(e, p):
            dve.do(V.tensor_copy, now[p][:], we[:, :, bass.ds(e, 1)].rearrange("p t o -> p (t o)"))

        with nc.Fori(0, (n - 2) // 2) as i:
            for p in range(2):
                pick(i * 2 + p, p)
                expert(i * 2 + p, p)
        pick(n - 2, 0)
        expert(n - 2, 0, load=False)
        pick(n - 1, 1)
        expert(n - 1, 1, last=True)
        st.close()


def constants():
    p = np.arange(P)
    f = np.arange(D)
    out = {'ident': np.eye(P)}
    out['pairblk'] = (p[:, None] // S == np.arange(32)[None] // HD)
    out['pairmask'] = ((p[:, None] % 32) // HD == np.arange(2)[None])
    out['headmask'] = (p[:, None] // HD == np.arange(H // 2)[None])
    out['vmask'] = (p[:, None] // S == (f[None] // HD) % 2)
    out['headblk'] = (p[:, None] // HD == p[None] // HD)
    d = p % HD
    freq = np.exp(-(np.float32(2 * (d // 2)) / np.float32(HD)) * np.log(np.float32(10000.0)), dtype=np.float32)
    angle = (np.arange(S, dtype=np.float32)[None] * freq[:, None]).astype(np.float32)
    out['cosine'] = np.cos(angle)
    out['sine'] = np.sin(angle) * np.where(d % 2 == 0, -1.0, 1.0)[:, None]
    e = np.arange(E_MOE)
    out['before'] = np.tile((e[None] < e[:, None]).reshape(1, -1), (P, 1))
    return {n: np.ascontiguousarray(a, np.float32) for n, a in out.items()}


def spread_matrix():
    m = np.zeros((P, ROWS, 2, P), np.float32)
    for r in range(ROWS):
        for k in range(P):
            m[32 * r + k % 32, r, (k // 32) % 2, k] = 1.0
    return m.reshape(P, -1)


def score_biases():
    q = (np.arange(P) % S)[:, None, None]
    h = np.arange(H)[None, :, None]
    k = np.arange(S)[None, None, :]
    slopes = (2.0 ** (-8.0 / H * (h + 1.0))).astype(np.float32)
    alibi = np.where(k > q, NEG, slopes * (k - q).astype(np.float32))
    causal = np.where(k > q, NEG, 0.0) + 0 * h
    return [np.ascontiguousarray(a.reshape(P, H * S), np.float32) for a in (alibi, causal)]


def lay_out(inp):
    a = {k: np.asarray(v) for k, v in inp.items()}
    cols = dict(a)
    swap = np.arange(D).reshape(-1, 2)[:, ::-1].reshape(-1)
    group = (np.arange(D) // HD // 4) * HD + np.arange(D) % HD
    cols['L1_attn_bqs'] = a['L1_attn_bq'][swap]
    for n in ('bk', 'bv'):
        cols[f'L1_attn_{n}'] = a[f'L1_attn_{n}'][group]
    cols['L1_attn_bks'] = a['L1_attn_bk'][group][swap]
    for n in ('q_scale', 'k_scale'):
        cols[f'L2_attn_{n}'] = np.repeat(a[f'L2_attn_{n}'], HD)
    out = {'x': a['x'].reshape(NT, D)}
    out['ctx_t'] = a['ctx_1024'].transpose(0, 2, 1)
    out['spread'] = spread_matrix()
    out['mask_f'] = a['mask_Bx1xSxS2_ff0'][:, 0]
    out['mask_i'] = a['mask_Bx1x1xS2_if1'][:, 0, 0]
    out['bias_cols'] = np.concatenate([cols[n].reshape(C, P).T for n in BIAS_COLS], axis=1)
    out['bias_rows'] = np.stack([a[n] for n in BIAS_ROWS])
    for L in (0, 1, 2, 3):
        for n in ('Wq', 'Wk', 'Wv', 'Wo' if L < 3 else 'Wp'):
            w = a[f'L{L}_xattn_{n}']
            out[f'L{L}_xattn_{n}'] = w.T if L == 1 else w
    w_in = a['L0_attn_w_in'].T
    for i, n in enumerate(('Wq', 'Wk', 'Wv')):
        out[f'L0_attn_{n}'] = w_in[:, i * D:(i + 1) * D]
        out[f'L2_attn_{n}'] = a[f'L2_attn_{n}'].T
    out['L0_attn_Wo'] = a['L0_attn_w_out'].T
    out['L2_attn_Wo'] = a['L2_attn_Wo'].T
    out['L1_attn_Wq'], out['L1_attn_Wqs'] = a['L1_attn_Wq'], a['L1_attn_Wq'][:, swap]
    out['L1_attn_Wk'], out['L1_attn_Wks'] = a['L1_attn_Wk'][:, group], a['L1_attn_Wk'][:, group][:, swap]
    out['L1_attn_Wv'], out['L1_attn_Wo'] = a['L1_attn_Wv'][:, group], a['L1_attn_Wo']
    for n in ('w_gate', 'w_up', 'w_down'):
        out[f'L0_ffn_{n}'] = a[f'L0_ffn_{n}']
    for n in ('wf', 'wi', 'wc', 'wo', 'uf', 'ui', 'uc', 'uo'):
        out[f'L1_ffn_{n}'] = a[f'L1_ffn_{n}'].T
    for n in ('W_dq', 'W_uk', 'W_uv'):
        out[f'L3_attn_{n}'] = a[f'L3_attn_{n}']
    for n in ('W_dq', 'W_uq', 'W_dkv', 'W_o'):
        out[f'L3_attn_{n}T'] = a[f'L3_attn_{n}'].T
    out['L2_ffn_centroidT'] = a['L2_ffn_centroid'].T
    out['L2_ffn_w1'], out['L2_ffn_w2'], out['L2_ffn_wout'] = a['L2_ffn_Wg'], a['L2_ffn_W1'], a['L2_ffn_W2']
    for n, m in (('b1', 'bg'), ('b2', 'b1')):
        out[f'L2_ffn_{n}'] = a[f'L2_ffn_{m}'].reshape(E_MOE, 6, 114).transpose(0, 2, 1)
    out['L2_ffn_bout'] = a['L2_ffn_b2']
    out['L3_ffn_routerT'] = a['L3_ffn_router_w'].T
    out['L3_ffn_w1'] = a['L3_ffn_w1'].transpose(0, 2, 1)
    out['L3_ffn_b1'] = a['L3_ffn_b1'].reshape(E_MOE, 4, P).transpose(0, 2, 1)
    out['L3_ffn_wout'] = a['L3_ffn_w2'].transpose(0, 2, 1)
    out['L3_ffn_bout'] = a['L3_ffn_b2']
    for n, v in constants().items():
        out[f'c_{n}'] = v
    out['c_alibi'], out['c_causal'] = score_biases()
    return {k: np.ascontiguousarray(v) for k, v in out.items()}


def build(nc, dram, stages=range(12)):
    pr = Program(nc, dram, stages)
    pr.load_state()
    steps = [lambda: pr.cross_attention(0, 1.0 / D ** 0.5, 'add'),
             lambda: pr.self_attention(0, HD ** -0.5, 'c_alibi'),
             lambda: pr.quantized_ffn(),
             lambda: pr.cross_attention(1, HD ** -0.5),
             lambda: pr.self_attention(1, HD ** -0.5, 'c_causal'),
             lambda: pr.recurrent_ffn(),
             lambda: pr.cross_attention(2, 1.0, 'fill'),
             lambda: pr.self_attention(2, 1.0, 'c_causal'),
             lambda: pr.expert_ffn(2),
             lambda: pr.cross_attention(3, HD ** -0.5, wo='Wp', bo='bp'),
             lambda: pr.self_attention(3, HD ** -0.5, 'c_causal'),
             lambda: pr.expert_ffn(3)]
    for s in stages:
        steps[s]()
    pr.store_state()


def kernel(**inputs):
    import concourse.bacc as bacc
    from concourse.bass_utils import run_bass_kernel_spmd

    nc = bacc.Bacc("TRN2", target_bir_lowering=False, num_devices=1)
    arrays = lay_out(inputs)
    dram = {n: nc.dram_tensor(f"in_{n}", a.shape, mybir.dt.from_np(a.dtype), kind="ExternalInput").ap()
            for n, a in arrays.items()}
    dram['out'] = nc.dram_tensor("out", (NT, D), F32, kind="ExternalOutput").ap()
    build(nc, dram)
    r = run_bass_kernel_spmd(nc, [{f"in_{n}": a for n, a in arrays.items()}], core_ids=[0])
    return r.results[0]["out"].reshape(B, S, D)
```

```python
from contextlib import ExitStack

import numpy as np

import concourse.bass as bass
from concourse import mybir
from concourse.alu_op_type import AluOpType as ALU

F32 = mybir.dt.float32
F32R = mybir.dt.float32r
I32 = mybir.dt.int32
ACT = mybir.ActivationFunctionType
AX = mybir.AxisListType.X
RMAX = bass.bass_isa.ReduceOp.max

P = 128
B, S, D, H = 16, 64, 256, 16
HD = D // H
C = D // P
T = B * S // P
NT = B * S
KEYS = 1601
PAIRS = H // 2
ROWS = 4
KT = -(-KEYS // P)
KEYS2 = KEYS + 1
KCH = [(0, 402), (402, 400), (802, 400), (1202, 400)]
BIG = 12582912.0
EPS = 1e-5
E_MOE, TOPK = 8, 2
NEG = -3.0e38

BIAS_COLS = ['L0_xattn_bq', 'L0_xattn_bk', 'L0_xattn_bv', 'L1_xattn_bq', 'L1_xattn_bk', 'L1_xattn_bv',
             'L1_attn_bq', 'L1_attn_bqs', 'L1_attn_bk', 'L1_attn_bks', 'L1_attn_bv',
             'L1_ffn_bf', 'L1_ffn_bi', 'L1_ffn_bc', 'L1_ffn_bo', 'L1_ffn_in_c',
             'L2_xattn_bq', 'L2_xattn_bk', 'L2_xattn_bv', 'L2_attn_q_scale', 'L2_attn_k_scale',
             'L3_xattn_bq', 'L3_xattn_bk', 'L3_xattn_bv']
BIAS_ROWS = ['L0_xattn_bo', 'L1_xattn_bo', 'L1_attn_bo', 'L2_xattn_bo', 'L3_xattn_bp']
CONSTS = [('ident', 128), ('pairblk', 32), ('pairmask', 2), ('headmask', 8), ('cosine', 64), ('sine', 64), ('before', 64)]

LOW_AT = (1, 2, 3, 4)
SCORES_AT = {5: [(0, (0, 1))], 6: [(0, (2, 3))], 7: [(1, (0, 1))], 8: [(1, (2, 3))], 10: [(2, (0, 1))],
             11: [(2, (2, 3))], 13: [(3, (0, 1, 2, 3))]}
ECH = [(0, 2 * P), (2 * P, 6 * P), (6 * P, KEYS)]


class Queue:

    def __init__(self, engine, sems, in_order):
        self.engine, self.sems, self.in_order = engine, sems, in_order
        self.begin(0)

    def begin(self, which):
        self.sem, self.n, self.seen = self.sems[which], 0, {}

    def wait(self, *tokens):
        for token in tokens:
            if token is None:
                continue
            sem, count = token
            if self.seen.get(sem.name, 0) < count:
                self.engine.wait_ge(sem, count)
                self.seen[sem.name] = count

    def do(self, build, *args, after=(), signal=True, alone=False, **kw):
        self.wait(*after)
        if self.in_order and self.n and not alone:
            self.wait((self.sem, self.n))
        instruction = build(*args, **kw)
        if not signal:
            return None
        instruction.then_inc(self.sem, 1)
        self.n += 1
        return self.sem, self.n

    def dma(self, dst, src, after=()):
        self.wait(*after)
        self.engine.dma_start(dst, src).then_inc(self.sem, 16)
        self.n += 16
        return self.sem, self.n


class Program:
    def __init__(self, nc, dram, stages):
        self.nc, self.dram, self.stages = nc, dram, stages
        names = [('pe', nc.tensor, False), ('dve', nc.vector, True), ('act', nc.scalar, True),
                 ('pool', nc.gpsimd, True), ('sp', nc.sync, False), ('sp_early', nc.sync, False), ('sp_keys', nc.sync, False)]
        self.sets = [{n: nc.alloc_semaphore(f"s_{n}_{'ab'[i]}") for n, _, _ in names} for i in range(2)]
        queues = {n: Queue(e, [self.sets[0][n], self.sets[1][n]], o) for n, e, o in names}
        self.pe, self.dve, self.act = queues['pe'], queues['dve'], queues['act']
        self.pool, self.sp = queues['pool'], queues['sp']
        self.sp_early = queues['sp_early']
        self.sp_keys = queues['sp_keys']
        self.queues, self.which = queues, 0
        self.ps = nc.alloc_psum_tensor("ps", [P, 8, 512], F32)
        self.X = nc.alloc_sbuf_tensor("X", [P, T, D], F32)
        self.XNT = nc.alloc_sbuf_tensor("XNT", [P, C, NT], F32)
        self.cols = nc.alloc_sbuf_tensor("cols", [P, 2 * len(BIAS_COLS)], F32)
        self.cst = {n: nc.alloc_sbuf_tensor(f"c_{n}", [P, w], F32) for n, w in CONSTS}
        self.stats = nc.alloc_sbuf_tensor("stats", [P, T, 6], F32)
        self.mv = nc.alloc_sbuf_tensor("mv", [P, T, 2], F32)
        self.rstd = nc.alloc_sbuf_tensor("rstd", [P, T], F32)
        self.row = nc.alloc_sbuf_tensor("row", [P, D], F32)
        self.nm = 0

    def phase(self):
        for q in (self.sp, self.sp_early, self.sp_keys):
            if q.n:
                q.wait((q.sem, q.n))
        self.nc.all_engine_barrier()
        last, self.which = self.which, 1 - self.which
        for name, q in self.queues.items():
            q.engine.sem_clear(self.sets[last][name])
            q.begin(self.which)

    def tile(self, stack, name, shape, dt=F32):
        self.nm += 1
        return stack.enter_context(self.nc.sbuf_tensor(f"{name}_{self.nm}", shape, dt))

    def col(self, name):
        k = 2 * BIAS_COLS.index(name)
        return self.cols[:, k:k + 2]

    def weight(self, stack, name, rows=D, n=D):
        w = self.tile(stack, name, [P, rows // P, n])
        self.sp.dma(w[:], self.dram[name].rearrange("(c p) n -> p c n", p=P))
        return w

    def load_state(self):
        for name, w in CONSTS:
            self.sp.dma(self.cst[name][:], self.dram[f"c_{name}"])
        self.sp.dma(self.cols[:], self.dram["bias_cols"])
        t_x = self.sp.dma(self.X[:], self.dram["x"].rearrange("(t p) d -> p t d", p=P))
        for t in range(T):
            self.take_stats(t, after=[t_x])
        self.phase()

    def store_state(self):
        self.phase()
        self.sp.dma(self.dram["out"].rearrange("(t p) d -> p t d", p=P), self.X[:])
        self.sp.wait((self.sp.sem, self.sp.n))

    def take_stats(self, t, after=()):
        self.dve.do(self.nc.vector.bn_stats, self.stats[:, t, :], self.X[:, t, :], after=after, alone=True)

    def layernorm(self, st=None):
        nc, ps, X, V, mv, rstd = self.nc, self.ps, self.X, self.nc.vector, self.mv, self.rstd
        with ExitStack() as own:
            xn = self.tile(st or own, "xn", [P, T, D])
            for t in range(T):
                t_mv = self.dve.do(V.bn_aggr, mv[:, t, :], self.stats[:, t, :], alone=True)
            t_var = self.dve.do(V.tensor_scalar, rstd[:], mv[:, :, 1], EPS, None, ALU.add)
            t_std = self.act.do(nc.scalar.activation, rstd[:], rstd[:], ACT.Sqrt, after=[t_var])
            t_r = self.dve.do(V.reciprocal, rstd[:], rstd[:], after=[t_std])
            free = [None] * 2
            for tp in range(T // 2):
                bank = 6 + tp % 2
                for u in range(2):
                    t = 2 * tp + u
                    t_xn = self.dve.do(V.tensor_scalar, xn[:, t, :], X[:, t, :], mv[:, t, 0:1],
                                       rstd[:, t:t + 1], ALU.subtract, ALU.mult, after=[t_r], alone=True)
                    for c in range(C):
                        t_tr = self.pe.do(nc.tensor.transpose,
                                          ps[:, bank, c * 256 + u * P:c * 256 + (u + 1) * P],
                                          xn[:, t, c * P:(c + 1) * P], self.cst['ident'][:],
                                          after=[t_xn, free[tp % 2]])
                free[tp % 2] = self.act.do(nc.scalar.copy, self.XNT[:, :, tp * 256:(tp + 1) * 256],
                                           ps[:, bank, :].rearrange("p (c t) -> p c t", c=C), after=[t_tr],
                                           alone=True)
            if st is None:
                self.phase()
            return free[(T // 2 - 1) % 2]

    def project(self, dst, w, bias=None, scale=None, src=None, banks=(0, 1), free=None, after=()):
        nc, ps = self.nc, self.ps
        src = self.XNT if src is None else src
        free = free if free is not None else {}
        nin, nout, out = w.shape[1], w.shape[2] // P, None
        k = 0
        for m in range(nout):
            for n in range(NT // 512):
                bank = banks[k % len(banks)]
                k += 1
                for c in range(nin):
                    t_mm = self.pe.do(nc.tensor.matmul, ps[:, bank, :], w[:, c, m * P:(m + 1) * P],
                                      src[:, c, n * 512:(n + 1) * 512], start=(c == 0), stop=(c == nin - 1),
                                      after=[free.get(bank), *after], signal=(c == nin - 1))
                o = dst[:, m, n * 512:(n + 1) * 512]
                if scale is not None:
                    b = bias[:, m:m + 1] if bias is not None else 0.0
                    out = free[bank] = self.dve.do(nc.vector.tensor_scalar, o, ps[:, bank, :], b, scale,
                                                   ALU.add, ALU.mult, after=[t_mm], alone=True)
                elif bias is not None:
                    out = free[bank] = self.act.do(nc.scalar.activation, o, ps[:, bank, :], ACT.Identity,
                                                   bias=bias[:, m:m + 1], after=[t_mm], alone=True)
                else:
                    out = free[bank] = self.act.do(nc.scalar.copy, o, ps[:, bank, :], after=[t_mm], alone=True)
        return out

    def add_bias_row(self, name):
        t_row = self.sp.dma(self.row[:], self.dram['bias_rows'][BIAS_ROWS.index(name)].partition_broadcast(P))
        self.pool.do(self.nc.gpsimd.tensor_tensor, self.X[:], self.X[:],
                     self.row[:].unsqueeze(1).broadcast_to([P, T, D]), ALU.add, after=[t_row])

    def out_project(self, src, w):
        nc, ps, X = self.nc, self.ps, self.X
        free = [None] * 4
        for t in range(T):
            bank = t % 4
            for c in range(C):
                t_mm = self.pe.do(nc.tensor.matmul, ps[:, bank, 0:D], src[:, c, t * P:(t + 1) * P],
                                  w[:, c, :], start=(c == 0), stop=(c == C - 1), after=[free[bank]],
                                  signal=(c == C - 1))
            free[bank] = self.dve.do(nc.vector.tensor_tensor, X[:, t, :], ps[:, bank, 0:D], X[:, t, :],
                                     ALU.add, after=[t_mm], alone=True)
            self.take_stats(t, after=[free[bank]])
        self.phase()

    def add_transposed(self, src, after=()):
        nc, ps, X = self.nc, self.ps, self.X
        free = [None] * 4
        for tp in range(T // 2):
            bank = tp % 4
            for u in range(2):
                for c in range(C):
                    t = 2 * tp + u
                    t_tr = self.pe.do(nc.tensor.transpose, ps[:, bank, u * D + c * P:u * D + (c + 1) * P],
                                      src[:, c, t * P:(t + 1) * P], self.cst['ident'][:],
                                      after=[free[bank], *after])
            xs = X[:, 2 * tp:2 * tp + 2, :].rearrange("p t d -> p (t d)")
            free[bank] = self.dve.do(nc.vector.tensor_tensor, xs, ps[:, bank, :], xs, ALU.add, after=[t_tr])
            for u in range(2):
                self.take_stats(2 * tp + u, after=[free[bank]])
        self.phase()

    def cross_attention(self, L, scale, mask=None, wo='Wo', bo='bo'):
        nc, ps = self.nc, self.ps
        pe, dve, act, pool, sp = self.pe, self.dve, self.act, self.pool, self.sp
        V, A, G, M = nc.vector, nc.scalar, nc.gpsimd, nc.tensor
        name = f"L{L}_xattn_"
        st = ExitStack()
        wk, wv = (self.weight(st, name + w) for w in ('Wk', 'Wv'))
        wo = self.weight(st, name + wo)
        ctx_t = [self.tile(st, f"ctx{i}", [P, C, KEYS]) for i in range(2)]
        key_parts = self.tile(st, "key_parts", [P, 2, KEYS2], F32R)
        spread = self.tile(st, "spread", [P, ROWS, 2, P], F32R)
        kept = self.tile(st, "kept", [P, KEYS]) if mask == 'fill' else None
        mk = [self.tile(st, f"mk{i}", [P, KEYS]) for i in range(2)] if mask else None
        early = ExitStack()
        raw_spread = self.tile(early, "raw_spread", [P, ROWS * 2 * P])
        sp.dma(raw_spread[:], self.dram['spread'])
        wq = self.weight(early, name + 'Wq')

        def load_ctx(b, p, c):
            sp.dma(ctx_t[p][:, c, :], self.dram['ctx_t'][bass.ds(b, 1), c * P:(c + 1) * P, :]
                   .rearrange("o p k -> p (o k)"))

        def load_mask(b, p, t_read=None):
            if mask == 'add':
                src = self.dram['mask_f'][bass.ds(b, 1), :, :].rearrange("o q k -> q (o k)")
                self.sp_early.dma(mk[p][0:S, :], src, after=[t_read])
                return self.sp_early.dma(mk[p][S:P, :], src)
            src = self.dram['mask_i'][bass.ds(b, 1), :].rearrange("o k -> (o k)").partition_broadcast(P)
            return self.sp_early.dma(mk[p][:].bitcast(I32), src, after=[t_read])

        def mask_row(p, t_load=None):
            if mask == 'add':
                dve.do(V.tensor_scalar, mk[p][:], mk[p][:], -1.0e9, None, ALU.mult, after=[t_load], alone=True)
            else:
                dve.do(V.tensor_scalar, mk[p][:], mk[p][:].bitcast(I32), 0, -10000.0, ALU.is_equal, ALU.mult,
                       after=[t_load], alone=True)
                dve.do(V.tensor_scalar, kept[:], mk[p][:], -1.0, None, ALU.is_ge)

        for c in range(C):
            load_ctx(0, 0, c)
        if mask:
            load_mask(0, 0)
        self.layernorm()
        self.add_bias_row(name + bo)
        act.do(A.copy, spread[:].rearrange("p r i m -> p (r i m)"), raw_spread[:])
        dve.do(V.memset, key_parts[:, :, KEYS:KEYS2].bitcast(F32), 0.0)
        if mask:
            mask_row(0)
        qt = self.XNT
        t_mm = {}
        for n in range(2):
            for m in range(C):
                for c in range(C):
                    t_mm[n] = pe.do(M.matmul, ps[:, 2 * n + m, :], wq[:, c, m * P:(m + 1) * P],
                                    qt[:, c, n * 512:(n + 1) * 512], start=(c == 0), stop=(c == C - 1),
                                    signal=(c == C - 1))
        for n in range(2):
            for m in range(C):
                dve.do(V.tensor_scalar, qt[:, m, n * 512:(n + 1) * 512], ps[:, 2 * n + m, :],
                       self.col(name + 'bq')[:, m:m + 1], scale, ALU.add, ALU.mult, after=[t_mm[n]], alone=True)
        self.phase()
        early.close()

        key_stack = [self.tile(st, f"key_stack{g}", [P, ROWS, KEYS2], F32R) for g in range(2)]
        vals = [self.tile(st, f"vals{i}", [P, KT, D]) for i in range(2)]
        prob = self.tile(st, "prob", [P, ROWS, KEYS])
        prob_t = self.tile(st, "prob_t", [P, 3, 512])
        q_parts = self.tile(st, "q_parts", [P, 2, C, S], F32R)
        q_stack = [self.tile(st, f"q_stack{i}", [P, ROWS, C, P], F32R) for i in range(2)]
        mx = self.tile(st, "mx", [P, ROWS, len(KCH)])
        nmx = self.tile(st, "nmx", [P, ROWS])
        den = self.tile(st, "den", [P, ROWS, len(ECH)])
        rden = self.tile(st, "rden", [P, ROWS])
        diag = self.tile(st, "diag", [P, ROWS, P])
        rmask = self.tile(st, "rmask", [P, P])
        both = self.tile(st, "both", [P, P])
        kf = self.tile(st, "kf", [P, 2, KCH[0][1]]) if mask == 'fill' else None

        def slot(g, p, b, t, values=True, scores=True, project=True, load=True):
            n = 1 - p
            sg, sp_ = (1, p) if g == 0 else (0, n)
            if load:
                load_ctx(b + 2, p, g)
                if g == 1 and mask:
                    t['mask'] = load_mask(b + 2, p, t.get('nmx'))
            if g == 0 and project:
                q_next = qt[:, :, bass.ds((b + 1) * S, S)]
                pool.do(G.tensor_copy, q_parts[:, 0], q_next)
                t_q = pool.do(G.tensor_tensor, q_parts[:, 1], q_next, q_parts[:, 0].bitcast(F32), ALU.subtract)

            def queries():
                for r in range(ROWS):
                    for part in range(2):
                        t_mm = pe.do(M.matmul, ps[:, 7, r * P:(r + 1) * P], spread[:, r, part, :],
                                     q_parts[:, part], start=(part == 0), stop=(part == 1), after=[t_q],
                                     signal=(part == 1))
                for h in range(2):
                    own = self.cst['pairmask'][:, h:h + 1]
                    bank_free[7] = act.do(A.activation, q_stack[n][:, :, :, h * S:(h + 1) * S],
                                          ps[:, 7, :].rearrange("p (r c q) -> p r c q", r=ROWS, c=C),
                                          ACT.Copy, scale=own, after=[t_mm], alone=True)
                t['queries'] = bank_free[7]

            s_free, t_read = t.setdefault('s_free', [None] * ROWS), {}
            bank_free = t.setdefault('bank_free', {})
            t_scored = t.get('scored')

            def score_chunk(k, pairs):
                k0, kw = KCH[k]
                vw = min(kw, KEYS - k0)
                read = t_read.get(min(KT - 1, (k0 + kw - 1) // P))
                t_s = {}
                for r in pairs:
                    t_s[r] = (pe.do(M.matmul, ps[:, r, 0:kw], q_stack[sp_][:, r, sg, :],
                                     key_stack[sg][:, r, k0:k0 + kw], start=True, stop=True,
                                     after=[s_free[r], *([t['queries'], t['stack', 0]] if g else [])]))
                t['scored'] = t_s[pairs[-1]]
                for r in pairs:
                    o = prob[:, r, k0:k0 + vw]
                    if mask:
                        s_free[r] = dve.do(V.tensor_tensor_reduce, o, ps[:, r, 0:vw], mk[sp_][:, k0:k0 + vw],
                                           1.0, NEG, ALU.add, ALU.max, mx[:, r, k:k + 1], after=[t_s[r], read, t.get('nmx')],
                                           alone=True)
                    else:
                        s_free[r] = dve.do(V.tensor_scalar, o, ps[:, r, 0:vw], 0.0, NEG, ALU.add, ALU.max,
                                           accum_out=mx[:, r, k:k + 1], after=[t_s[r], read, t.get('nmx')],
                                           alone=True)
                if k == len(KCH) - 1 and pairs[-1] == ROWS - 1:
                    t['nmx'] = dve.do(V.tensor_reduce, nmx[:], mx[:], AX, ALU.max, negate=True)

            def exponentials(i):
                e0, e1 = ECH[i]
                for r in range(ROWS):
                    t['e', i] = act.do(A.activation, prob[:, r, e0:e1], prob[:, r, e0:e1], ACT.Exp,
                                       bias=nmx[:, r:r + 1], accum_out=den[:, r, i:i + 1],
                                       after=[t.get('nmx')], alone=True)

            def denominators():
                dve.do(V.tensor_reduce, rden[:], den[:], AX, ALU.add, after=[t['e', len(ECH) - 1], t.get('diag')])
                t_rd = dve.do(V.reciprocal, rden[:], rden[:])
                for r in range(ROWS):
                    t['diag'] = pool.do(G.tensor_tensor, diag[:, r, :], self.cst['ident'][:],
                                        rden[:, r:r + 1].broadcast_to([P, P]), ALU.mult, after=[t_rd, t.get('spread')],
                                        alone=r > 0)

            def keys_unit(k):
                k0, kw = KCH[k]
                vw = min(kw, KEYS - k0)
                for c in range(C):
                    t_mm = pe.do(M.matmul, ps[:, k, 0:vw], wk[:, c, g * P:(g + 1) * P], ctx_t[n][:, c, k0:k0 + vw],
                                 start=(c == 0), stop=(c == C - 1), after=[s_free[k]], signal=(c == C - 1))
                t_sent = t.get(('stack', 0)) if g else None
                hi, lo = key_parts[:, 0, k0:k0 + vw], key_parts[:, 1, k0:k0 + vw]
                bias = self.col(name + 'bk')[:, g:g + 1]
                if mask == 'fill':
                    f = kf[:, k % 2, 0:vw]
                    t_f = s_free[k] = dve.do(V.scalar_tensor_tensor, f, ps[:, k, 0:vw], bias, kept[:, k0:k0 + vw],
                                             ALU.add, ALU.mult, after=[t_mm, t.get(('kf', k % 2))], alone=True)
                    t['hi', k] = act.do(A.copy, hi, f, after=[t_f, t_sent], alone=True)
                    t['parts'] = t['kf', k % 2] = pool.do(G.tensor_tensor, lo, f, hi.bitcast(F32), ALU.subtract,
                                                          after=[t['hi', k]])
                else:
                    if k % 2:
                        t['hi', k] = dve.do(V.tensor_scalar, hi, ps[:, k, 0:vw], bias, None, ALU.add,
                                            after=[t_mm, t_sent], alone=True)
                    else:
                        t['hi', k] = act.do(A.activation, hi, ps[:, k, 0:vw], ACT.Identity, bias=bias,
                                            after=[t_mm, t_sent], alone=True)

            def keys_low(k):
                k0, kw = KCH[k]
                vw = min(kw, KEYS - k0)
                hi, lo = key_parts[:, 0, k0:k0 + vw], key_parts[:, 1, k0:k0 + vw]
                if mask != 'fill':
                    t['parts'] = s_free[k] = dve.do(V.scalar_tensor_tensor, lo, ps[:, k, 0:vw],
                                                    self.col(name + 'bk')[:, g:g + 1], hi.bitcast(F32),
                                                    ALU.add, ALU.subtract, after=[t['hi', k]], alone=True)
                if k == len(KCH) - 1:
                    for q in range(4):
                        for r in range(ROWS):
                            t['stack', g] = (sp if g else self.sp_keys).dma(
                                key_stack[g][32 * q:32 * q + 32, r, :].bitcast(F32),
                                key_parts[32 * r:32 * r + 32, q // 2, :].bitcast(F32),
                                after=[t['parts'], t['hi', k], t_scored])

            def values_unit(i, bank=7):
                tiles = [x for x in (2 * i, 2 * i + 1) if x < KT]
                w = min(P, KEYS - tiles[-1] * P)
                for u, kt in enumerate(tiles):
                    for c in range(C):
                        t_mm = pe.do(M.matmul, ps[0:w, bank, u * D:(u + 1) * D], ctx_t[n][:, c, kt * P:kt * P + w],
                                     wv[:, c, :], start=(c == 0), stop=(c == C - 1), after=[bank_free.get(bank)],
                                     signal=(c == C - 1))
                q, fn = (act, A.copy) if i % 2 else (dve, V.tensor_copy)
                bank_free[bank] = q.do(fn, vals[n][0:w, tiles[0]:tiles[-1] + 1, :],
                                       ps[0:w, bank, 0:len(tiles) * D].rearrange("p (t d) -> p t d", d=D),
                                       after=[t_mm], alone=True)

            pt_free = t.setdefault('pt_free', [None] * 2)
            sb_free = t.setdefault('sb_free', [None] * 3)
            t_sb = [None] * 3

            def chunk_of(kt):
                return t['e', [i for i, (e0, e1) in enumerate(ECH) if e0 <= kt * P < e1][0]]

            def transposes(kt):
                w, bank = min(P, KEYS - kt * P), kt % 2
                for r in range(ROWS):
                    t_tr = pe.do(M.transpose, ps[0:w, 4 + bank, r * P:(r + 1) * P],
                                 prob[:, r, kt * P:kt * P + w], self.cst['ident'][:],
                                 after=[pt_free[bank], chunk_of(kt)], signal=(r == ROWS - 1))
                t_read[kt] = t_tr
                q, fn = (act, A.copy) if kt >= 5 else (dve, V.tensor_copy)
                t_sb[kt % 3] = pt_free[bank] = q.do(fn, prob_t[0:w, kt % 3, :], ps[0:w, 4 + bank, :],
                                                    after=[t_tr, sb_free[kt % 3]], alone=True)

            def weighted(kt):
                w = min(P, KEYS - kt * P)
                for r in range(ROWS):
                    t_pv = pe.do(M.matmul, ps[32 * r:32 * r + 32, 6, g * P:(g + 1) * P],
                                 vals[p][0:w, kt, (ROWS * g + r) * 32:(ROWS * g + r + 1) * 32],
                                 prob_t[0:w, kt % 3, r * P:(r + 1) * P], start=(kt == 0), stop=(kt == KT - 1),
                                 after=[t_sb[kt % 3], t.get('both')], signal=(r == ROWS - 1))
                sb_free[kt % 3] = t['pv'] = t_pv

            v_units = range(0, 4) if g == 0 else range(4, 7)
            if values:
                exponentials(0)
            if project:
                keys_unit(0)
            if values:
                exponentials(1)
            if project:
                keys_unit(1)
            for kt in range(KT + 1):
                if values and kt < KT:
                    transposes(kt)
                if project and kt in (0, 1):
                    keys_unit(2 + kt)
                if project and kt in LOW_AT:
                    keys_low(LOW_AT.index(kt))
                if values and kt == 0:
                    exponentials(2)
                if project and g == 0 and kt == 3:
                    queries()
                if kt == 12 and 'mask' in t:
                    mask_row(p, t['mask'])
                if values and kt == 9:
                    denominators()
                if scores:
                    for k, pairs in SCORES_AT.get(kt, ()):
                        score_chunk(k, pairs)
                if values and kt:
                    weighted(kt - 1)
            if values:
                for r in range(ROWS):
                    t_rm = pe.do(M.matmul, ps[32 * r:32 * r + 32, 4, 0:P], self.cst['pairblk'][:], diag[:, r, :],
                                 start=True, stop=True, after=[t['diag'], pt_free[0]], signal=(r == ROWS - 1))
                t['spread'] = t_rm
                t_rs = pt_free[0] = dve.do(V.tensor_copy, rmask[:], ps[:, 4, 0:P], after=[t_rm])
                t['both'] = dve.do(V.tensor_tensor, both[:], ps[:, 6, g * P:(g + 1) * P], rmask[:], ALU.mult,
                       after=[t['pv'], t_rs])
                dve.do(V.scalar_tensor_tensor, qt[:, g, bass.ds(b * S, S)], both[:, 0:S],
                       self.col(name + 'bv')[:, g:g + 1], both[:, S:P], ALU.add, ALU.add)
            if project:
                bank_free[5] = pt_free[1]
                for k, i in enumerate(v_units):
                    values_unit(i, (7, 5)[k % 2])
                pt_free[1] = bank_free[5]

        def batch(p, b, first={}, second={}, **both):
            t = {}
            slot(0, p, b, t, **first, **both)
            slot(1, p, b, t, **second, **both)
            self.phase()

        batch(1, -1, first={'scores': False}, values=False)
        with nc.Fori(0, (B - 2) // 2) as i:
            for p in range(2):
                batch(p, i * 2 + p)
        batch(0, B - 2, load=False)
        batch(1, B - 1, second={'scores': False}, project=False, load=False)
        self.out_project(qt, wo)
        st.close()

    def self_attention(self, L, scale, table):
        nc, ps, cst, XNT = self.nc, self.ps, self.cst, self.XNT
        pe, dve, act, pool, sp = self.pe, self.dve, self.act, self.pool, self.sp
        V, A, G, M = nc.vector, nc.scalar, nc.gpsimd, nc.tensor
        name = f"L{L}_attn_"
        st = ExitStack()
        bias = self.tile(st, "table", [P, H * S])
        sp.dma(bias[:], self.dram[table])
        vmask = self.tile(st, "vmask", [P, D])
        sp.dma(vmask[:], self.dram['c_vmask'])
        qt = self.tile(st, "qt", [P, C, NT])
        kt = self.tile(st, "kt", [P, C, NT])
        src = XNT
        bv = None
        if L == 3:
            wv, wo, src = self.latent_projections(st, name, qt, kt, scale)
        else:
            w = {n: self.weight(st, name + n) for n in ('Wq', 'Wk', 'Wv', 'Wo')}
            wv, wo = w['Wv'], w['Wo']
            if L == 1:
                w.update({n: self.weight(st, name + n) for n in ('Wqs', 'Wks')})
            self.layernorm()
            if name + 'bo' in BIAS_ROWS:
                self.add_bias_row(name + 'bo')
            if L == 0:
                self.project(qt, w['Wq'], None, scale)
                self.project(kt, w['Wk'], None, banks=(2, 3))
            elif L == 1:
                self.rotated(st, name, w, qt, kt, scale)
                bv = self.col(name + 'bv')
            else:
                self.silu_normed(st, name, w, qt, kt)
            if L != 2:
                self.phase()
        nsrc = wv.shape[1]
        OT = self.tile(st, "heads_out", [P, C, NT])
        q2 = [self.tile(st, f"q2{u}", [P, C, P]) for u in range(2)]
        kb = [self.tile(st, f"kb{u}", [P, C, 2, 512]) for u in range(2)]
        xd = [self.tile(st, f"xd{u}", [P, nsrc, 2, 2, S]) for u in range(2)]
        vb = [self.tile(st, f"vb{u}", [P, 2, D]) for u in range(3)]
        pr = [self.tile(st, f"pr{u}", [P, H, S]) for u in range(3)]
        pt = [self.tile(st, f"pt{u}", [P, 2, 512]) for u in range(2)]
        mx = [self.tile(st, f"smx{u}", [P, H]) for u in range(3)]
        silu_v = self.tile(st, "silu_v", [P, T, 2 * D]) if L == 2 else None
        TURN, VALUES, OUT = 4, 6, 7

        tk = {u: {} for u in range(-3, T)}

        def operands(u):
            i, got, old = u % 2, tk[u], tk[u - 2]
            got['q'] = dve.do(V.tensor_copy, q2[i][:], qt[:, :, bass.ds(u * P, P)], after=[old.get('s')],
                              alone=True)
            for c in range(C):
                for bb in range(2):
                    kk = kt[:, c, bass.ds(u * P + bb * S, S)]
                    q, eng = (pool, G) if c else (dve, V)
                    got['k', c, bb] = q.do(
                        eng.tensor_tensor, kb[i][:, c, bb, :].rearrange("p (h k) -> p h k", k=S),
                        kk.unsqueeze(1).broadcast_to([P, H // 2, S]),
                        cst['headmask'][:].unsqueeze(2).broadcast_to([P, H // 2, S]), ALU.mult,
                        after=[old.get('s')], alone=True)

        def double(u):
            i = u % 2
            for c in range(nsrc):
                for bb in range(2):
                    tk[u]['x'] = act.do(A.copy, xd[i][:, c, bb], src[:, c, bass.ds(u * P + bb * S, S)]
                                        .unsqueeze(1).broadcast_to([P, 2, S]), after=[tk[u - 2].get('v')], alone=True)

        def scores(u):
            i, got = u % 2, tk[u]
            for c in range(C):
                for bb in range(2):
                    got['s'] = pe.do(M.matmul, ps[bb * S:(bb + 1) * S, 2 * i + c, :],
                                     q2[i][:, c, bb * S:(bb + 1) * S], kb[i][:, c, bb, :], start=True,
                                     stop=True, after=[got['q'], got['k', c, bb], tk[u - 2].get('pr')])

        def values(u):
            i, got = u % 2, tk[u]
            for bb in range(2):
                for c in range(nsrc):
                    got['v'] = pe.do(M.matmul, ps[:, VALUES, bb * D:(bb + 1) * D],
                                     xd[i][:, c, bb].rearrange("p r k -> p (r k)"), wv[:, c, :],
                                     start=(c == 0), stop=(c == nsrc - 1),
                                     after=[got['x'], tk[u - 1].get('vs')])

        def exponentials(u):
            i, got = u % 2, tk[u]
            if L == 2:
                v = silu_v[:, u].rearrange("p (b d) -> p b d", b=2)
            else:
                v = ps[:, VALUES, :].rearrange("p (b d) -> p b d", b=2)
            got['vs'] = got['vb'] = dve.do(V.tensor_tensor, vb[u % 3][:], v,
                                           vmask[:].unsqueeze(1).broadcast_to([P, 2, D]), ALU.mult,
                                           after=[got.get('v'), tk[u - 3].get('o')], alone=True)
            for c in range(C):
                t = dve.do(V.tensor_tensor, pr[u % 3][:, 8 * c:8 * c + 8, :].rearrange("p h k -> p (h k)"),
                           ps[:, 2 * i + c, :], bias[:, c * 512:(c + 1) * 512], ALU.add,
                           after=[got['s'], tk[u - 3].get('tr')], alone=True)
            got['pr'] = t
            t = dve.do(V.tensor_reduce, mx[u % 3][:], pr[u % 3][:], AX, ALU.max, after=[tk[u - 3].get('p')])
            t = dve.do(V.tensor_tensor, pr[u % 3][:], pr[u % 3][:], mx[u % 3][:].unsqueeze(2).broadcast_to([P, H, S]),
                       ALU.subtract)
            got['e'] = act.do(A.activation, pr[u % 3][:], pr[u % 3][:], ACT.Exp, after=[t], alone=True)

        def normalize(u):
            got = tk[u]
            dve.do(V.tensor_reduce, mx[u % 3][:], pr[u % 3][:], AX, ALU.add, after=[got['e']], alone=True)
            t = dve.do(V.reciprocal, mx[u % 3][:], mx[u % 3][:])
            got['p'] = pool.do(G.tensor_tensor, pr[u % 3][:], pr[u % 3][:],
                               mx[u % 3][:].unsqueeze(2).broadcast_to([P, H, S]), ALU.mult, after=[t], alone=True)

        def transposes(u):
            i, got = u % 2, tk[u]
            for half in range(2):
                for r in range(ROWS):
                    j = 4 * half + r
                    got['tr'] = pe.do(M.transpose, ps[:, TURN + half, r * P:(r + 1) * P],
                                      pr[u % 3][:, 2 * j:2 * j + 2, :].rearrange("p h k -> p (h k)"),
                                      cst['ident'][:], after=[got['p'], tk[u - 1].get(('pt', half))])
                got['pt', half] = act.do(A.copy, pt[i][:, half, :], ps[:, TURN + half, :],
                                         after=[got['tr'], tk[u - 2].get('o')], alone=True)

        def weighted(u):
            i, got = u % 2, tk[u]
            for half in range(2):
                for bb in range(2):
                    for r in range(ROWS):
                        j = 4 * half + r
                        cols = slice(r * P + bb * S, r * P + bb * S + S)
                        got['o'] = pe.do(M.matmul, ps[32 * r:32 * r + 32, OUT, half * P + bb * S:half * P + bb * S + S],
                                         vb[u % 3][:, bb, 32 * j:32 * j + 32], pt[i][:, half, cols], start=True,
                                         stop=True, after=[got['pt', half], got['vb'], tk[u - 1].get('out')])

        def outputs(u):
            got, s = tk[u], ps[:, OUT, 0:256].rearrange("p (c t) -> p c t", c=C)
            for c in range(C):
                o = OT[:, c, bass.ds(u * P, P)]
                if bv is None:
                    got['out'] = dve.do(V.tensor_copy, o, s[:, c], after=[got['o']], alone=True)
                else:
                    got['out'] = dve.do(V.tensor_scalar, o, s[:, c], bv[:, c:c + 1], None, ALU.add,
                                        after=[got['o']], alone=True)

        steps = ((scores, 1), (weighted, 4), (exponentials, 2), (operands, 0), (double, 0), (values, 1),
                 (normalize, 3), (transposes, 3), (outputs, 4))
        if L == 2:
            for u in range(T):
                double(u)
                values(u)
                tk[u]['vs'] = act.do(A.activation, silu_v[:, u], ps[:, VALUES, :], ACT.Silu, after=[tk[u]['v']],
                                     alone=True)
            self.phase()
            tk = {u: {} for u in range(-3, T)}
            steps = [s for s in steps if s[0] not in (double, values)]
        for rnd in range(T + 4):
            for step, behind in steps:
                if 0 <= rnd - behind < T:
                    step(rnd - behind)
        self.phase()
        if wo is not None:
            self.out_project(OT, wo)
        else:
            self.add_transposed(OT)
        st.close()

    def rotated(self, st, name, w, qt, kt, scale):
        nc, cst = self.nc, self.cst
        for i, (x, n, b, s) in enumerate(((qt, 'Wq', 'bq', scale), (kt, 'Wk', 'bk', 1.0))):
            swapped = self.tile(st, f"swapped{i}", [P, C, NT])
            t1 = self.project(x, w[n], self.col(name + b), s, banks=(4 * i, 4 * i + 1))
            t2 = self.project(swapped, w[n + 's'], self.col(name + b + 's'), s, banks=(4 * i + 2, 4 * i + 3))
            for c in range(C):
                def by(queue, engine, o, table):
                    o = o[:, c, :].rearrange("p (b s) -> p b s", s=S)
                    return queue.do(engine.tensor_tensor, o, o, cst[table][:].unsqueeze(1).broadcast_to([P, B, S]),
                                    ALU.mult, after=[t1, t2], alone=True)
                t_s = by(self.pool, nc.gpsimd, swapped, 'sine')
                t_c = by(self.dve, nc.vector, x, 'cosine')
                self.pool.do(nc.gpsimd.tensor_tensor, x[:, c, :], x[:, c, :], swapped[:, c, :], ALU.add,
                             after=[t_c, t_s], alone=True)

    def silu_normed(self, st, name, w, qt, kt):
        nc, ps, cst = self.nc, self.ps, self.cst
        for i, (x, n) in enumerate(((qt, 'Wq'), (kt, 'Wk'))):
            for m in range(C):
                for h in range(2):
                    bank = 4 * i + 2 * m + h
                    for c in range(C):
                        t_mm = self.pe.do(nc.tensor.matmul, ps[:, bank, :], w[n][:, c, m * P:(m + 1) * P],
                                          self.XNT[:, c, h * 512:(h + 1) * 512], start=(c == 0), stop=(c == C - 1))
                    self.act.do(nc.scalar.activation, x[:, m, h * 512:(h + 1) * 512], ps[:, bank, :], ACT.Silu,
                                after=[t_mm], alone=True)
        self.phase()
        blocks = [(x, n, m, slice(h * 512, (h + 1) * 512)) for x, n in ((qt, 'q_scale'), (kt, 'k_scale'))
                  for m in range(C) for h in range(2)]
        norm = self.tile(st, "norm", [P, len(blocks), 512])
        rad = self.tile(st, "rad", [P, 2, 512])
        headblk = self.tile(st, "headblk", [P, P])
        t_hb = self.sp.dma(headblk[:], self.dram['c_headblk'])
        t_norm, free = [], [None] * 2
        for k, (x, n, m, cols) in enumerate(blocks):
            r = norm[:, k, :]
            t_sq = self.pool.do(nc.gpsimd.tensor_tensor, r, x[:, m, cols], x[:, m, cols], ALU.mult, alone=True)
            t_mm = self.pe.do(nc.tensor.matmul, ps[:, k % 4, :], headblk[:], r, start=True, stop=True,
                              after=[t_sq, t_hb, t_norm[k - 4] if k >= 4 else None])
            t_norm.append(self.act.do(nc.scalar.activation, r, ps[:, k % 4, :], ACT.Sqrt, after=[t_mm], alone=True))
        for k, (x, n, m, cols) in enumerate(blocks):
            r, q, o = norm[:, k, :], rad[:, k % 2, :], x[:, m, cols]
            t_p = self.pool.do(nc.gpsimd.tensor_tensor, o, o, r, ALU.mult, after=[t_norm[k]], alone=True)
            t = self.dve.do(nc.vector.tensor_scalar, q, r, 1e-6, None, ALU.add, after=[t_norm[k], free[k % 2]],
                            alone=True)
            self.dve.do(nc.vector.reciprocal, q, q)
            free[k % 2] = self.dve.do(nc.vector.scalar_tensor_tensor, o, q, self.col(name + n)[:, m:m + 1], o,
                                      ALU.mult, ALU.mult, after=[t_p])

    def latent_projections(self, st, name, qt, kt, scale):
        nc, ps = self.nc, self.ps
        M, A = nc.tensor, nc.scalar
        w = {n: self.weight(st, name + n, r, m) for n, r, m in
             (('W_dqT', D, P), ('W_dq', P, D), ('W_uqT', P, D), ('W_dkvT', D, P), ('W_uk', D, P), ('W_uv', D, P),
              ('W_oT', D, D))}
        self.layernorm()
        a = self.tile(st, "uq_dq", [P, C, D])
        keff = self.tile(st, "keff", [P, 1, D])
        veff = self.tile(st, "veff", [P, 1, D])
        lat = self.tile(st, "lat", [P, 1, NT])
        ckv = self.tile(st, "ckv", [P, 1, NT])
        for m in range(C):
            t_mm = self.pe.do(M.matmul, ps[:, m, 0:D], w['W_uqT'][:, 0, m * P:(m + 1) * P], w['W_dq'][:, 0, :],
                              start=True, stop=True)
            t_a = self.act.do(A.copy, a[:, m, :], ps[:, m, 0:D], after=[t_mm])
        for c in range(C):
            t_k = self.pe.do(M.matmul, ps[:, 2, 0:D], w['W_uk'][:, c, :], a[:, c, :], start=(c == 0),
                             stop=(c == C - 1), after=[t_a])
        for c in range(C):
            t_v = self.pe.do(M.matmul, ps[:, 3, 0:D], w['W_uv'][:, c, :], w['W_oT'][:, c, :], start=(c == 0),
                             stop=(c == C - 1))
        t_k = self.act.do(A.copy, keff[:, 0, :], ps[:, 2, 0:D], after=[t_k])
        self.act.do(A.copy, veff[:, 0, :], ps[:, 3, 0:D], after=[t_v])
        self.project(lat, w['W_dqT'], banks=(4, 5))
        self.project(ckv, w['W_dkvT'], banks=(6, 7))
        self.phase()
        self.project(qt, w['W_uqT'], None, scale, src=lat)
        self.project(kt, keff, src=ckv, banks=(2, 3))
        self.phase()
        return veff, None, ckv

    def largest(self, x, m, big, after=()):
        self.dve.do(self.nc.vector.tensor_reduce, big[:, m:m + 1], x[:, m], AX, ALU.max,
                    apply_absolute_value=True, after=after, alone=True)

    def steps(self, big, name):
        V, one = self.nc.vector, self.tile(self.ffn_stack, name, [P, 4])
        t = self.dve.do(V.tensor_reduce, one[:, 0:1], big[:], AX, ALU.max)
        t = self.pool.do(self.nc.gpsimd.partition_all_reduce, one[:, 1:2], one[:, 0:1], P, RMAX, after=[t])
        self.dve.do(V.tensor_scalar, one[:, 2:3], one[:, 1:2], 1.0 / 32767.0, 1e-12, ALU.mult, ALU.max, after=[t])
        return one, self.dve.do(V.reciprocal, one[:, 3:4], one[:, 2:3])

    def quantize_rows(self, x, m, one, t_one, after=()):
        V, k = self.nc.vector, self.round_no % len(self.rounded)
        self.round_no += 1
        tmp = self.rounded[k]
        t = self.act.do(self.nc.scalar.activation, tmp[:], x[:, m], ACT.Identity, bias=self.big_col[:],
                        scale=one[:, 3:4], after=[t_one, self.round_free[k], *after], alone=True)
        t = self.dve.do(V.tensor_scalar, tmp[:], tmp[:], -BIG, -32768.0, ALU.add, ALU.max, after=[t], alone=True)
        self.round_free[k] = self.dve.do(V.tensor_scalar, x[:, m], tmp[:], 32767.0, one[:, 2:3], ALU.min, ALU.mult,
                                         after=[t], alone=True)
        return self.round_free[k]

    def quantize_weight(self, w, tmp, sc):
        V, dve = self.nc.vector, self.dve
        wb = w[:].rearrange("p c (b i) -> p (c b) i", i=32)
        tb = tmp[:].rearrange("p c (b i) -> p (c b) i", i=32)
        nb = wb.shape[1]
        spread = lambda s: sc[:, s, :].unsqueeze(2).broadcast_to([P, nb, 32])
        dve.do(V.tensor_reduce, sc[:, 0, :], wb, AX, ALU.max, apply_absolute_value=True)
        dve.do(V.tensor_scalar, sc[:, 0, :], sc[:, 0, :], 1.0 / 7.0, 1e-12, ALU.mult, ALU.max)
        dve.do(V.reciprocal, sc[:, 1, :], sc[:, 0, :])
        dve.do(V.tensor_tensor, tb, wb, spread(1), ALU.mult)
        dve.do(V.tensor_scalar, tb, tb, BIG, -BIG, ALU.add, ALU.add)
        dve.do(V.tensor_scalar, tb, tb, -8.0, 7.0, ALU.max, ALU.min)
        return dve.do(V.tensor_tensor, wb, tb, spread(0), ALU.mult)

    def quantized_ffn(self):
        nc, ps, V, A, M = self.nc, self.ps, self.nc.vector, self.nc.scalar, self.nc.tensor
        pe, dve, act, X, xq = self.pe, self.dve, self.act, self.X, self.XNT
        F = 768
        NF = F // P
        st = self.ffn_stack = ExitStack()
        raw = {n: self.weight(st, "L0_ffn_w_" + n, *shape) for n, shape in
               (('up', (F, D)), ('gate', (F, D)), ('down', (D, F)))}
        turned = {'up': self.tile(st, "wu_t", [P, C, F]), 'gate': self.tile(st, "wg_t", [P, C, F]),
                  'down': self.tile(st, "wd_t", [P, NF, D])}
        tmp, tmp2 = self.tile(st, "tmp", [P, NF, D]), self.tile(st, "tmp2", [P, C, F])
        sc = self.tile(st, "sc", [P, 2, NF * D // 32])
        up, gate = self.tile(st, "up", [P, NF, NT]), self.tile(st, "gate", [P, NF, NT])
        self.rounded = [self.tile(st, f"rounded{i}", [P, NT]) for i in range(4)]
        self.round_free, self.round_no = [None] * 4, 0
        self.big_col = self.tile(st, "big_col", [P, 1])
        big = {n: self.tile(st, "big_" + n, [P, k]) for n, k in (('x', C), ('up', NF), ('gate', NF), ('act', NF),
                                                                 ('hid', NF))}
        dve.do(V.memset, self.big_col[:], BIG)
        self.layernorm()

        bank_free, t_w = [None] * 4, {}

        def turn(n):
            w, flat = raw[n], turned[n][:].rearrange("p i o -> p (i o)")
            blocks = [(i, o) for i in range(w.shape[2] // P) for o in range(w.shape[1])]
            for j in range(0, len(blocks), 4):
                bank = (j // 4) % 4
                for u, (i, o) in enumerate(blocks[j:j + 4]):
                    t = pe.do(M.transpose, ps[:, bank, u * P:(u + 1) * P], w[:, o, i * P:(i + 1) * P],
                              self.cst['ident'][:], after=[t_w[n], bank_free[bank]], signal=(u == 3))
                bank_free[bank] = t_w['t', n] = act.do(A.copy, flat[:, j * P:(j + 4) * P], ps[:, bank, :], after=[t],
                                                       alone=True)

        for c in range(C):
            self.largest(xq, c, big['x'])
        one, t_one = self.steps(big['x'], "one_x")
        t_w['up'] = self.quantize_weight(raw['up'], tmp, sc)
        for c in range(C):
            t_x = self.quantize_rows(xq, c, one, t_one)
        t_w['gate'] = self.quantize_weight(raw['gate'], tmp, sc)
        turn('up')
        free = {}
        for m in range(NF):
            t = self.project(up[:, m:m + 1], turned['up'][:, :, m * P:(m + 1) * P], src=xq, banks=(4, 5), free=free,
                             after=[t_x, t_w['t', 'up']])
            self.largest(up, m, big['up'], after=[t])
        one, t_one = self.steps(big['up'], "one_up")
        turn('gate')
        t_w['down'] = self.quantize_weight(raw['down'], tmp2, sc)
        free = {}
        for m in range(NF):
            t = self.project(gate[:, m:m + 1], turned['gate'][:, :, m * P:(m + 1) * P], src=xq, banks=(6, 7),
                             free=free, after=[t_w['t', 'gate']])
            self.quantize_rows(up, m, one, t_one)
            self.largest(gate, m, big['gate'], after=[t])
        turn('down')
        one, t_one = self.steps(big['gate'], "one_gate")
        k = len(self.rounded)
        for m in range(NF + 1):
            if m < NF:
                t_g = self.quantize_rows(gate, m, one, t_one)
                i = self.round_no % k
                self.round_no += 1
                sig = self.rounded[i]
                t_s = act.do(A.activation, sig[:], gate[:, m], ACT.Sigmoid, after=[t_g, self.round_free[i]],
                             alone=True)
                self.round_free[i] = t_s
                now = (m, sig, i, t_s)
            if m:
                j, sig, i, t_s = before
                t = dve.do(V.tensor_scalar, sig[:], sig[:], BIG / 65536.0, None, ALU.add, after=[t_s], alone=True)
                t = dve.do(V.tensor_scalar, sig[:], sig[:], -BIG / 65536.0, 65535.0 / 65536.0, ALU.add, ALU.min)
                t = self.round_free[i] = dve.do(V.scalar_tensor_tensor, gate[:, j], sig[:], 0.0, gate[:, j], ALU.max,
                                                ALU.mult)
                self.largest(gate, j, big['act'], after=[t])
            before = now
        one, t_one = self.steps(big['act'], "one_act")
        for m in range(NF):
            t = self.quantize_rows(gate, m, one, t_one)
            t = dve.do(V.tensor_tensor, gate[:, m], gate[:, m], up[:, m], ALU.mult, after=[t])
            self.largest(gate, m, big['hid'], after=[t])
        one, t_one = self.steps(big['hid'], "one_hid")
        for m in range(NF):
            t_g = self.quantize_rows(gate, m, one, t_one)
            for t in range(T):
                t_mm = pe.do(M.matmul, ps[:, t, 0:D], gate[:, m, t * P:(t + 1) * P], turned['down'][:, m, :],
                             start=(m == 0), stop=(m == NF - 1), after=[t_g, t_w['t', 'down']])
                if m == NF - 1:
                    t_a = dve.do(V.tensor_tensor, X[:, t, :], ps[:, t, 0:D], X[:, t, :], ALU.add, after=[t_mm],
                                 alone=True)
                    self.take_stats(t, after=[t_a])
        self.phase()
        st.close()

    def recurrent_ffn(self):
        nc, ps, V, A, M = self.nc, self.ps, self.nc.vector, self.nc.scalar, self.nc.tensor
        st = ExitStack()
        wx = [self.weight(st, 'L1_ffn_' + n) for n in ('wf', 'wi', 'wc')]
        wc = [self.weight(st, 'L1_ffn_' + n) for n in ('uf', 'ui', 'uc')]
        wo, uo = self.weight(st, 'L1_ffn_wo'), self.weight(st, 'L1_ffn_uo')
        self.layernorm()
        pre = self.tile(st, "pre", [P, 3, C, NT])
        out = self.tile(st, "out", [P, C, NT])
        cell = self.tile(st, "cell", [P, C, S])
        gates = self.tile(st, "gates", [P, 3, C, S])
        for k, b in enumerate(('bf', 'bi', 'bc')):
            self.project(pre[:, k], wx[k], self.col('L1_ffn_' + b), banks=(2 * k, 2 * k + 1))
        self.project(out, wo, self.col('L1_ffn_bo'), banks=(6, 7))
        self.dve.do(V.tensor_copy, cell[:], self.col('L1_ffn_in_c').unsqueeze(2).broadcast_to([P, C, S]))
        self.phase()

        def step(t, t_cell):
            at = bass.ds(t * S, S)
            for k in range(3):
                for m in range(C):
                    for c in range(C):
                        t_mm = self.pe.do(M.matmul, ps[:, k, m * S:(m + 1) * S], wc[k][:, c, m * P:(m + 1) * P],
                                          cell[:, c, :], start=(c == 0), stop=(c == C - 1), after=[t_cell],
                                          signal=(c == C - 1))
                t_g = self.dve.do(V.tensor_tensor, gates[:, k], ps[:, k, 0:C * S].rearrange("p (c s) -> p c s", c=C),
                                  pre[:, k, :, at], ALU.add, after=[t_mm, t_cell], alone=True)
                t_a = self.act.do(A.activation, gates[:, k], gates[:, k], ACT.Tanh if k == 2 else ACT.Sigmoid,
                                  after=[t_g], alone=True)
                if k == 0:
                    t_f = t_a
            t_c = self.dve.do(V.tensor_tensor, cell[:], cell[:], gates[:, 0], ALU.mult, after=[t_f, t_mm], alone=True)
            t_i = self.dve.do(V.tensor_tensor, gates[:, 1], gates[:, 1], gates[:, 2], ALU.mult, after=[t_a], alone=True)
            return self.dve.do(V.tensor_tensor, cell[:], cell[:], gates[:, 1], ALU.add, after=[t_c, t_i])

        with nc.Fori(0, B // 8) as i:
            for half in range(2):
                t_cell = None
                for k in range(4):
                    t_cell = step(i * 8 + 4 * half + k, t_cell)
                self.phase()
        for m in range(C):
            for c in range(C):
                t_mm = self.pe.do(M.matmul, ps[:, 0, m * S:(m + 1) * S], uo[:, c, m * P:(m + 1) * P], cell[:, c, :],
                                  start=(c == 0), stop=(c == C - 1))
        t_u = self.act.do(A.copy, gates[:, 0], ps[:, 0, 0:C * S].rearrange("p (c s) -> p c s", c=C), after=[t_mm])
        for c in range(C):
            o = out[:, c, :].rearrange("p (b s) -> p b s", s=S)
            t_o = self.dve.do(V.tensor_tensor, o, o, gates[:, 0, c, :].unsqueeze(1).broadcast_to([P, B, S]), ALU.add,
                              after=[t_u])
            t_h = self.act.do(A.activation, out[:, c, :], out[:, c, :], ACT.Tanh, after=[t_o])
        self.add_transposed(out, after=[t_h])
        st.close()

    def expert_weights(self, st, logits):
        nc, V, cst, dve = self.nc, self.nc.vector, self.cst, self.dve
        n = E_MOE
        mine = logits[:].unsqueeze(3).broadcast_to([P, T, n, n])
        others = logits[:].unsqueeze(2).broadcast_to([P, T, n, n])
        before = cst['before'][:].rearrange("p (a b) -> p a b", a=n).unsqueeze(1).broadcast_to([P, T, n, n])
        rank = self.tile(st, "rank", [P, T, n])
        larger = self.tile(st, "larger", [P, T, n, n])
        equal = self.tile(st, "equal", [P, T, n, n])
        top = self.tile(st, "top", [P, T])
        dve.do(V.tensor_tensor, larger[:], others, mine, ALU.is_gt)
        dve.do(V.tensor_tensor, equal[:], others, mine, ALU.is_equal)
        dve.do(V.tensor_tensor, equal[:], equal[:], before, ALU.mult)
        dve.do(V.tensor_tensor, larger[:], larger[:], equal[:], ALU.add)
        dve.do(V.tensor_reduce, rank[:], larger[:], AX, ALU.add)
        over = lambda a: a[:].unsqueeze(2).broadcast_to([P, T, n])
        dve.do(V.tensor_scalar, rank[:], rank[:], TOPK - 0.5, None, ALU.is_lt)
        dve.do(V.tensor_reduce, top[:], logits[:], AX, ALU.max)
        t = dve.do(V.tensor_tensor, logits[:], logits[:], over(top), ALU.subtract)
        t = self.act.do(nc.scalar.activation, logits[:], logits[:], ACT.Exp, after=[t])
        dve.do(V.tensor_tensor, logits[:], logits[:], rank[:], ALU.mult, after=[t])
        dve.do(V.tensor_reduce, top[:], logits[:], AX, ALU.add)
        dve.do(V.reciprocal, top[:], top[:])
        return dve.do(V.tensor_tensor, logits[:], logits[:], over(top), ALU.mult)

    def expert_ffn(self, L):
        nc, ps, V, A, M, G = self.nc, self.ps, self.nc.vector, self.nc.scalar, self.nc.tensor, self.nc.gpsimd
        pe, dve, act, pool, sp, cst = self.pe, self.dve, self.act, self.pool, self.sp, self.cst
        name, X, XNT = f"L{L}_ffn_", self.X, self.XNT
        gated = L == 2
        F, FT = (684, 114) if gated else (512, P)
        NF = F // FT
        n = E_MOE
        st = ExitStack()
        router = self.weight(st, name + ('centroidT' if gated else 'routerT'), D, n)
        bout = self.tile(st, "bout", [n, D])
        sp.dma(bout[:], self.dram[name + 'bout'])
        keys = ('w1', 'w2', 'wout') if gated else ('w1', 'wout')
        raw = {k: self.tile(st, "raw_" + k, [FT, NF, D] if k == 'wout' else [P, C, F]) for k in keys}
        parts = {k: [self.tile(st, f"parts_{k}{i}", [raw[k].shape[0], 2, *raw[k].shape[1:]], F32R)
                     for i in range(2)] for k in keys}
        b1 = [self.tile(st, f"b1{i}", [FT, NF]) for i in range(2)]
        b2 = [self.tile(st, f"b2{i}", [FT, NF]) for i in range(2)] if gated else None

        def load_expert(e, read=()):
            for k in keys:
                pattern = "o (m p) d -> p (o m) d" if k == 'wout' else "o (c p) f -> p (o c) f"
                sp.dma(raw[k][:], self.dram[name + k][bass.ds(e, 1)].rearrange(pattern, p=FT if k == 'wout' else P),
                       after=read)

        def load_biases(e, p):
            for k, tiles in (('b1', b1), ('b2', b2)):
                if tiles:
                    sp.dma(tiles[p][:], self.dram[name + k][bass.ds(e, 1)].rearrange("o p m -> p (o m)"))

        def cut(dst, src, after=()):
            t = act.do(A.copy, dst[:, 0], src, after=after, alone=True)
            return t, pool.do(G.tensor_tensor, dst[:, 1], src, dst[:, 0].bitcast(F32), ALU.subtract, after=[t],
                              alone=True)

        def cut_part(k, p):
            return cut(parts[k][p], raw[k][:])[1]

        PASSES = ((0, 0), (1, 0), (0, 1))

        load_expert(0)
        load_biases(0, 0)
        self.layernorm()
        we = self.tile(st, "we", [P, T, n])
        wet = self.tile(st, "wet", [n, NT])
        x_parts = self.tile(st, "x_parts", [P, 2, C, NT], F32R)
        hid = self.tile(st, "hid", [FT, 2, NF, NT], F32R)
        hid_f = [self.tile(st, f"hid_f{i}", [FT, 512]) for i in range(3)]
        act_o = [self.tile(st, f"act{i}", [FT, 512]) for i in range(2)]
        cut(x_parts, XNT[:])
        load_expert(1, [cut_part(k, 0) for k in keys])
        for t in range(T):
            for c in range(C):
                t_r = pe.do(M.matmul, ps[:, 0, t * n:(t + 1) * n], XNT[:, c, t * P:(t + 1) * P], router[:, c, :],
                            start=(c == 0), stop=(c == C - 1))
        if gated:
            sq = self.tile(st, "sq", [P, C, NT])
            csq = self.tile(st, "csq", [P, C, n])
            ones = self.tile(st, "ones", [P, P])
            dve.do(V.memset, ones[:], 1.0)
            dve.do(V.tensor_tensor, csq[:], router[:], router[:], ALU.mult)
            t_sq = dve.do(V.tensor_tensor, sq[:], XNT[:], XNT[:], ALU.mult)
            for t in range(T):
                for c in range(C):
                    pe.do(M.matmul, ps[:, 1, t * n:(t + 1) * n], sq[:, c, t * P:(t + 1) * P], ones[:, 0:n],
                          start=(c == 0), stop=False, after=[t_sq])
                for c in range(C):
                    t_d = pe.do(M.matmul, ps[:, 1, t * n:(t + 1) * n], ones[:], csq[:, c, :], start=False,
                                stop=(c == C - 1))
            w = we[:].rearrange("p t e -> p (t e)")
            t_c = act.do(A.copy, w, ps[:, 1, 0:T * n], after=[t_d])
            dve.do(V.scalar_tensor_tensor, w, ps[:, 0, 0:T * n], -2.0, w, ALU.mult, ALU.add, after=[t_c, t_r])
            t_d = dve.do(V.tensor_scalar, w, w, 1e-12, None, ALU.max)
            t_w = act.do(A.activation, w, w, ACT.Sqrt, after=[t_d])
        else:
            t_w = act.do(A.copy, we[:].rearrange("p t e -> p (t e)"), ps[:, 0, 0:T * n], after=[t_r])
        dve.wait(t_w)
        t_we = self.expert_weights(st, we)
        free = [None] * 2
        for t in range(T):
            bank = 2 + t % 2
            t_tr = pe.do(M.transpose, ps[0:n, bank, 0:P], we[:, t, :], cst['ident'][:], after=[t_we, free[t % 2]])
            t_c = act.do(A.copy, wet[:, t * P:(t + 1) * P], ps[0:n, bank, 0:P], after=[t_tr])
            t_b = pe.do(M.matmul, ps[:, bank, 256:512], wet[:, t * P:(t + 1) * P], bout[:], start=True, stop=True,
                        after=[t_c])
            free[t % 2] = dve.do(V.tensor_tensor, X[:, t, :], ps[:, bank, 256:512], X[:, t, :], ALU.add, after=[t_b])
        self.phase()

        def expert(e, p, load=True, last=False):
            if not last:
                load_biases(e + 1, 1 - p)
            free, af, k, t_h, hf_free, t_cut = {}, [None] * 2, 0, {}, [None] * 3, []

            def hidden(bank, w, m, toks):
                for c in range(C):
                    for i, (a, b) in enumerate(PASSES):
                        t = pe.do(M.matmul, ps[0:FT, bank, :], w[:, a, c, m * FT:(m + 1) * FT],
                                  x_parts[:, b, c, toks], start=(c == 0 and i == 0),
                                  stop=(c == C - 1 and i == 2), after=[free.get(bank)],
                                  signal=(c == C - 1 and i == 2))
                return t

            for h in range(2):
                for m in range(NF):
                    if k < len(keys) and not last:
                        t_cut += [cut_part(keys[k], 1 - p)]
                        if load and k == len(keys) - 1:
                            load_expert(e + 2, t_cut)
                    toks = slice(h * 512, (h + 1) * 512)
                    bank, i, hf = 2 * (k % 2), k % 2, hid_f[k % 3]
                    t1 = hidden(bank, parts['w1'][p], m, toks)
                    if gated:
                        t2 = hidden(bank + 1, parts['w2'][p], m, toks)
                        free[bank] = act.do(A.activation, act_o[i][:], ps[0:FT, bank, :], ACT.Silu,
                                            bias=b1[p][:, m:m + 1], after=[t1, af[i]], alone=True)
                        t = af[i] = free[bank + 1] = dve.do(
                            V.scalar_tensor_tensor, hf[:], ps[0:FT, bank + 1, :], b2[p][:, m:m + 1],
                            act_o[i][:], ALU.add, ALU.mult, after=[t2, free[bank], hf_free[k % 3]], alone=True)
                    else:
                        t = free[bank] = act.do(A.activation, hf[:], ps[0:FT, bank, :], ACT.Gelu,
                                                bias=b1[p][:, m:m + 1], after=[t1, hf_free[k % 3]], alone=True)
                    t_hi = act.do(A.copy, hid[:, 0, m, toks], hf[:], after=[t], alone=True)
                    t_h[h] = hf_free[k % 3] = dve.do(V.tensor_tensor, hid[:, 1, m, toks], hf[:],
                                                     hid[:, 0, m, toks].bitcast(F32), ALU.subtract, after=[t_hi],
                                                     alone=True)
                    k += 1
            for t in range(T):
                bank = 4 + t % 4
                for m in range(NF):
                    for i, (a, b) in enumerate(PASSES):
                        t_y = pe.do(M.matmul, ps[:, bank, 0:D], hid[:, a, m, t * P:(t + 1) * P],
                                    parts['wout'][p][:, b, m, :], start=(m == 0 and i == 0),
                                    stop=(m == NF - 1 and i == 2), after=[free.get(bank), t_h[t // 4]],
                                    signal=(m == NF - 1 and i == 2))
                free[bank] = dve.do(V.scalar_tensor_tensor, X[:, t, :], ps[:, bank, 0:D], we_col(t, e, p),
                                    X[:, t, :], ALU.mult, ALU.add, after=[t_y], alone=True)
                if last and gated:
                    self.take_stats(t, after=[free[bank]])
            self.phase()

        now = [self.tile(st, f"now{i}", [P, T]) for i in range(2)]

        def we_col(t, e, p):
            return now[p][:, t:t + 1]

        def pick(e, p):
            dve.do(V.tensor_copy, now[p][:], we[:, :, bass.ds(e, 1)].rearrange("p t o -> p (t o)"))

        with nc.Fori(0, (n - 2) // 2) as i:
            for p in range(2):
                pick(i * 2 + p, p)
                expert(i * 2 + p, p)
        pick(n - 2, 0)
        expert(n - 2, 0, load=False)
        pick(n - 1, 1)
        expert(n - 1, 1, last=True)
        st.close()


def constants():
    p = np.arange(P)
    f = np.arange(D)
    out = {'ident': np.eye(P)}
    out['pairblk'] = (p[:, None] // S == np.arange(32)[None] // HD)
    out['pairmask'] = ((p[:, None] % 32) // HD == np.arange(2)[None])
    out['headmask'] = (p[:, None] // HD == np.arange(H // 2)[None])
    out['vmask'] = (p[:, None] // S == (f[None] // HD) % 2)
    out['headblk'] = (p[:, None] // HD == p[None] // HD)
    d = p % HD
    freq = np.exp(-(np.float32(2 * (d // 2)) / np.float32(HD)) * np.log(np.float32(10000.0)), dtype=np.float32)
    angle = (np.arange(S, dtype=np.float32)[None] * freq[:, None]).astype(np.float32)
    out['cosine'] = np.cos(angle)
    out['sine'] = np.sin(angle) * np.where(d % 2 == 0, -1.0, 1.0)[:, None]
    e = np.arange(E_MOE)
    out['before'] = np.tile((e[None] < e[:, None]).reshape(1, -1), (P, 1))
    return {n: np.ascontiguousarray(a, np.float32) for n, a in out.items()}


def spread_matrix():
    m = np.zeros((P, ROWS, 2, P), np.float32)
    for r in range(ROWS):
        for k in range(P):
            m[32 * r + k % 32, r, (k // 32) % 2, k] = 1.0
    return m.reshape(P, -1)


def score_biases():
    q = (np.arange(P) % S)[:, None, None]
    h = np.arange(H)[None, :, None]
    k = np.arange(S)[None, None, :]
    slopes = (2.0 ** (-8.0 / H * (h + 1.0))).astype(np.float32)
    alibi = np.where(k > q, NEG, slopes * (k - q).astype(np.float32))
    causal = np.where(k > q, NEG, 0.0) + 0 * h
    return [np.ascontiguousarray(a.reshape(P, H * S), np.float32) for a in (alibi, causal)]


def lay_out(inp):
    a = {k: np.asarray(v) for k, v in inp.items()}
    cols = dict(a)
    swap = np.arange(D).reshape(-1, 2)[:, ::-1].reshape(-1)
    group = (np.arange(D) // HD // 4) * HD + np.arange(D) % HD
    cols['L1_attn_bqs'] = a['L1_attn_bq'][swap]
    for n in ('bk', 'bv'):
        cols[f'L1_attn_{n}'] = a[f'L1_attn_{n}'][group]
    cols['L1_attn_bks'] = a['L1_attn_bk'][group][swap]
    for n in ('q_scale', 'k_scale'):
        cols[f'L2_attn_{n}'] = np.repeat(a[f'L2_attn_{n}'], HD)
    out = {'x': a['x'].reshape(NT, D)}
    out['ctx_t'] = a['ctx_1024'].transpose(0, 2, 1)
    out['spread'] = spread_matrix()
    out['mask_f'] = a['mask_Bx1xSxS2_ff0'][:, 0]
    out['mask_i'] = a['mask_Bx1x1xS2_if1'][:, 0, 0]
    out['bias_cols'] = np.concatenate([cols[n].reshape(C, P).T for n in BIAS_COLS], axis=1)
    out['bias_rows'] = np.stack([a[n] for n in BIAS_ROWS])
    for L in (0, 1, 2, 3):
        for n in ('Wq', 'Wk', 'Wv', 'Wo' if L < 3 else 'Wp'):
            w = a[f'L{L}_xattn_{n}']
            out[f'L{L}_xattn_{n}'] = w.T if L == 1 else w
    w_in = a['L0_attn_w_in'].T
    for i, n in enumerate(('Wq', 'Wk', 'Wv')):
        out[f'L0_attn_{n}'] = w_in[:, i * D:(i + 1) * D]
        out[f'L2_attn_{n}'] = a[f'L2_attn_{n}'].T
    out['L0_attn_Wo'] = a['L0_attn_w_out'].T
    out['L2_attn_Wo'] = a['L2_attn_Wo'].T
    out['L1_attn_Wq'], out['L1_attn_Wqs'] = a['L1_attn_Wq'], a['L1_attn_Wq'][:, swap]
    out['L1_attn_Wk'], out['L1_attn_Wks'] = a['L1_attn_Wk'][:, group], a['L1_attn_Wk'][:, group][:, swap]
    out['L1_attn_Wv'], out['L1_attn_Wo'] = a['L1_attn_Wv'][:, group], a['L1_attn_Wo']
    for n in ('w_gate', 'w_up', 'w_down'):
        out[f'L0_ffn_{n}'] = a[f'L0_ffn_{n}']
    for n in ('wf', 'wi', 'wc', 'wo', 'uf', 'ui', 'uc', 'uo'):
        out[f'L1_ffn_{n}'] = a[f'L1_ffn_{n}'].T
    for n in ('W_dq', 'W_uk', 'W_uv'):
        out[f'L3_attn_{n}'] = a[f'L3_attn_{n}']
    for n in ('W_dq', 'W_uq', 'W_dkv', 'W_o'):
        out[f'L3_attn_{n}T'] = a[f'L3_attn_{n}'].T
    out['L2_ffn_centroidT'] = a['L2_ffn_centroid'].T
    out['L2_ffn_w1'], out['L2_ffn_w2'], out['L2_ffn_wout'] = a['L2_ffn_Wg'], a['L2_ffn_W1'], a['L2_ffn_W2']
    for n, m in (('b1', 'bg'), ('b2', 'b1')):
        out[f'L2_ffn_{n}'] = a[f'L2_ffn_{m}'].reshape(E_MOE, 6, 114).transpose(0, 2, 1)
    out['L2_ffn_bout'] = a['L2_ffn_b2']
    out['L3_ffn_routerT'] = a['L3_ffn_router_w'].T
    out['L3_ffn_w1'] = a['L3_ffn_w1'].transpose(0, 2, 1)
    out['L3_ffn_b1'] = a['L3_ffn_b1'].reshape(E_MOE, 4, P).transpose(0, 2, 1)
    out['L3_ffn_wout'] = a['L3_ffn_w2'].transpose(0, 2, 1)
    out['L3_ffn_bout'] = a['L3_ffn_b2']
    for n, v in constants().items():
        out[f'c_{n}'] = v
    out['c_alibi'], out['c_causal'] = score_biases()
    return {k: np.ascontiguousarray(v) for k, v in out.items()}


def build(nc, dram, stages=range(12)):
    pr = Program(nc, dram, stages)
    pr.load_state()
    steps = [lambda: pr.cross_attention(0, 1.0 / D ** 0.5, 'add'),
             lambda: pr.self_attention(0, HD ** -0.5, 'c_alibi'),
             lambda: pr.quantized_ffn(),
             lambda: pr.cross_attention(1, HD ** -0.5),
             lambda: pr.self_attention(1, HD ** -0.5, 'c_causal'),
             lambda: pr.recurrent_ffn(),
             lambda: pr.cross_attention(2, 1.0, 'fill'),
             lambda: pr.self_attention(2, 1.0, 'c_causal'),
             lambda: pr.expert_ffn(2),
             lambda: pr.cross_attention(3, HD ** -0.5, wo='Wp', bo='bp'),
             lambda: pr.self_attention(3, HD ** -0.5, 'c_causal'),
             lambda: pr.expert_ffn(3)]
    for s in stages:
        steps[s]()
    pr.store_state()


def kernel(**inputs):
    import concourse.bacc as bacc
    from concourse.bass_utils import run_bass_kernel_spmd

    nc = bacc.Bacc("TRN2", target_bir_lowering=False, num_devices=1)
    arrays = lay_out(inputs)
    dram = {n: nc.dram_tensor(f"in_{n}", a.shape, mybir.dt.from_np(a.dtype), kind="ExternalInput").ap()
            for n, a in arrays.items()}
    dram['out'] = nc.dram_tensor("out", (NT, D), F32, kind="ExternalOutput").ap()
    build(nc, dram)
    r = run_bass_kernel_spmd(nc, [{f"in_{n}": a for n, a in arrays.items()}], core_ids=[0])
    return r.results[0]["out"].reshape(B, S, D)
```
